# Optimizing a Trainium2 kernel written in Bass

```python
import numpy as np
import jax
import jax.numpy as jnp

def _softmax(x, axis=-1):
    return jax.nn.softmax(x, axis=axis)

def _gelu(x):
    return jax.nn.gelu(x, approximate=True)

def _silu(x):
    return jax.nn.silu(x)

def _sigmoid(x):
    return jax.nn.sigmoid(x)

def _layernorm(x, axis=-1, eps=1e-05):
    m = jnp.mean(x, axis=axis, keepdims=True)
    v = jnp.var(x, axis=axis, keepdims=True)
    return (x - m) / jnp.sqrt(v + eps)

def _scatter_add(tgt, idx, src, axis=0):
    return tgt.at[idx].add(src)

def _segment_sum(src, seg, n):
    return jax.ops.segment_sum(src, seg, n)
kernel_name = 'mk_gnn_preln_d2_gnn_r32_0f3869'

def setup_inputs(seed: int=0):
    np.random.seed(seed)
    _w = jnp.asarray

    def _rec_inputs():
        import jax
        import jax.numpy as jnp
        _gk = jax.random.key(seed)
        x = -0.000202 + 1 * jax.random.normal(jax.random.fold_in(_gk, 1), (3125, 64), jnp.float32)
        _s = jax.random.randint(jax.random.fold_in(_gk, 2), (25000,), 0, 3125, jnp.int32)
        _d = jax.random.randint(jax.random.fold_in(_gk, 3), (25000,), 0, 3125, jnp.int32)
        _loop = jnp.arange(3125, dtype=jnp.int32)
        src = jnp.concatenate([_s, _d, _loop])
        dst = jnp.concatenate([_d, _s, _loop])
        _o = jnp.argsort(dst, stable=True)
        src = src[_o]
        dst = dst[_o]
        edge_attr_16 = 0.000254156 + 0.999948 * jax.random.normal(jax.random.fold_in(_gk, 11), (53125, 16), jnp.float32)
        return (x, src, dst, edge_attr_16)
    x, src, dst, edge_attr_16 = _rec_inputs()

    def _L0_gnn_setup():
        import jax, jax.numpy as jnp
        import numpy as np
        N = 3125
        E = 50000
        D = 64

        def gcn_conv(x, W, b, src, dst, n_nodes):
            h = x @ W
            ones = jnp.ones((src.shape[0],), dtype=x.dtype)
            deg = jax.ops.segment_sum(ones, dst, num_segments=n_nodes) + 1.0
            dinv = jax.lax.rsqrt(deg)
            msg = h[src] * (dinv[src] * dinv[dst])[:, None]
            agg = jax.ops.segment_sum(msg, dst, num_segments=n_nodes)
            agg = agg + h * (dinv * dinv)[:, None]
            return agg + b
        key = jax.random.key(seed)
        ks = jax.random.split(key, 8)
        x = jax.random.normal(ks[0], (N, D), dtype=jnp.float32)
        edge_index = jax.random.randint(ks[1], (2, E), 0, N, dtype=jnp.int64)
        s = 1.0 / np.sqrt(D)
        W0 = jax.random.normal(ks[2], (D, D), dtype=jnp.float32) * s
        b0 = jax.random.normal(ks[3], (D,), dtype=jnp.float32) * 0.01
        W1 = jax.random.normal(ks[4], (D, D), dtype=jnp.float32) * s
        b1 = jax.random.normal(ks[5], (D,), dtype=jnp.float32) * 0.01
        W2 = jax.random.normal(ks[6], (D, D), dtype=jnp.float32) * s
        b2 = jax.random.normal(ks[7], (D,), dtype=jnp.float32) * 0.01
        return {'x': x, 'edge_index': edge_index, 'W0': W0, 'b0': b0, 'W1': W1, 'b1': b1, 'W2': W2, 'b2': b2}
    _L0_gnn_all = _L0_gnn_setup()
    _L0_gnn_in = {k: v for k, v in _L0_gnn_all.items() if k in ('W0', 'b0', 'W1', 'b1', 'W2', 'b2')}
    del _L0_gnn_all

    def _L1_gnn_setup():
        import jax, jax.numpy as jnp
        import numpy as np
        N, E, D, ED = (50000, 25000, 64, 16)
        H1 = 2 * D + ED

        def _forward(x, edge_weights, W_att1, b_att1, W_att2, b_att2, W_lin, b_lin, W_ih, b_ih, W_hh, b_hh, edge_idx):
            num_nodes = x.shape[0]
            src = edge_idx[0]
            dst = edge_idx[1]
            lin_x = x @ W_lin.T + b_lin
            feat = jnp.concatenate([x[src], edge_weights, x[dst]], axis=1)
            h = jax.nn.relu(feat @ W_att1.T + b_att1)
            scores = (h @ W_att2.T + b_att2)[:, 0]
            m = jax.ops.segment_max(scores, src, num_segments=num_nodes)
            e = jnp.exp(scores - m[src])
            denom = jax.ops.segment_sum(e, src, num_segments=num_nodes)
            alpha = e / denom[src]
            msg = jax.ops.segment_sum(alpha[:, None] * lin_x[dst], src, num_segments=num_nodes)
            gi = x @ W_ih.T + b_ih
            gh = msg @ W_hh.T + b_hh
            i_r, i_z, i_n = jnp.split(gi, 3, axis=1)
            h_r, h_z, h_n = jnp.split(gh, 3, axis=1)
            r = jax.nn.sigmoid(i_r + h_r)
            z = jax.nn.sigmoid(i_z + h_z)
            n = jnp.tanh(i_n + r * h_n)
            new_h = (1.0 - z) * n + z * msg
            deg = jax.ops.segment_sum(jnp.ones_like(scores), src, num_segments=num_nodes)
            return jnp.where(deg[:, None] > 0, new_h, x)
        key = jax.random.key(seed)
        ks = jax.random.split(key, 16)
        s = 0.05
        inp = {'x': jax.random.normal(ks[0], (N, D), jnp.float32), 'edge_idx': jax.random.randint(ks[1], (2, E), 0, N, jnp.int64), 'edge_weights': jax.random.normal(ks[2], (E, ED), jnp.float32), 'W_att1': jax.random.normal(ks[3], (H1, H1), jnp.float32) * s, 'b_att1': jnp.zeros((H1,), jnp.float32), 'W_att2': jax.random.normal(ks[4], (1, H1), jnp.float32) * s, 'b_att2': jnp.zeros((1,), jnp.float32), 'W_lin': jax.random.normal(ks[5], (D, D), jnp.float32) * s, 'b_lin': jnp.zeros((D,), jnp.float32), 'W_ih': jax.random.normal(ks[6], (3 * D, D), jnp.float32) * s, 'b_ih': jnp.zeros((3 * D,), jnp.float32), 'W_hh': jax.random.normal(ks[7], (3 * D, D), jnp.float32) * s, 'b_hh': jnp.zeros((3 * D,), jnp.float32)}
        return inp
    _L1_gnn_all = _L1_gnn_setup()
    _L1_gnn_in = {k: v for k, v in _L1_gnn_all.items() if k in ('W_att1', 'b_att1', 'W_att2', 'b_att2', 'W_lin', 'b_lin', 'W_ih', 'b_ih', 'W_hh', 'b_hh')}
    del _L1_gnn_all
    return {'x': x, 'src': src, 'dst': dst, 'edge_attr_16': edge_attr_16, 'L0_gnn_W0': _L0_gnn_in['W0'], 'L0_gnn_b0': _L0_gnn_in['b0'], 'L0_gnn_W1': _L0_gnn_in['W1'], 'L0_gnn_b1': _L0_gnn_in['b1'], 'L0_gnn_W2': _L0_gnn_in['W2'], 'L0_gnn_b2': _L0_gnn_in['b2'], 'L1_gnn_W_att1': _L1_gnn_in['W_att1'], 'L1_gnn_b_att1': _L1_gnn_in['b_att1'], 'L1_gnn_W_att2': _L1_gnn_in['W_att2'], 'L1_gnn_b_att2': _L1_gnn_in['b_att2'], 'L1_gnn_W_lin': _L1_gnn_in['W_lin'], 'L1_gnn_b_lin': _L1_gnn_in['b_lin'], 'L1_gnn_W_ih': _L1_gnn_in['W_ih'], 'L1_gnn_b_ih': _L1_gnn_in['b_ih'], 'L1_gnn_W_hh': _L1_gnn_in['W_hh'], 'L1_gnn_b_hh': _L1_gnn_in['b_hh']}

def reference(x, src, dst, edge_attr_16, L0_gnn_W0, L0_gnn_b0, L0_gnn_W1, L0_gnn_b1, L0_gnn_W2, L0_gnn_b2, L1_gnn_W_att1, L1_gnn_b_att1, L1_gnn_W_att2, L1_gnn_b_att2, L1_gnn_W_lin, L1_gnn_b_lin, L1_gnn_W_ih, L1_gnn_b_ih, L1_gnn_W_hh, L1_gnn_b_hh):
    import jax
    import jax.numpy as jnp

    def _L0_gnn_ref(x, edge_index, W0, b0, W1, b1, W2, b2):
        import jax, jax.numpy as jnp
        import numpy as np
        N = 3125
        E = 50000
        D = 64

        def gcn_conv(x, W, b, src, dst, n_nodes):
            h = x @ W
            ones = jnp.ones((src.shape[0],), dtype=x.dtype)
            deg = jax.ops.segment_sum(ones, dst, num_segments=n_nodes) + 1.0
            dinv = jax.lax.rsqrt(deg)
            msg = h[src] * (dinv[src] * dinv[dst])[:, None]
            agg = jax.ops.segment_sum(msg, dst, num_segments=n_nodes)
            agg = agg + h * (dinv * dinv)[:, None]
            return agg + b
        src, dst = (edge_index[0], edge_index[1])
        n = x.shape[0]
        h = jax.nn.relu(gcn_conv(x, W0, b0, src, dst, n))
        h = jax.nn.relu(gcn_conv(h, W1, b1, src, dst, n))
        out = gcn_conv(h, W2, b2, src, dst, n)
        return out

    def _L1_gnn_ref(x, edge_idx, edge_weights, W_att1, b_att1, W_att2, b_att2, W_lin, b_lin, W_ih, b_ih, W_hh, b_hh):
        import jax, jax.numpy as jnp
        import numpy as np
        N, E, D, ED = (50000, 25000, 64, 16)
        H1 = 2 * D + ED

        def _forward(x, edge_weights, W_att1, b_att1, W_att2, b_att2, W_lin, b_lin, W_ih, b_ih, W_hh, b_hh, edge_idx):
            num_nodes = x.shape[0]
            src = edge_idx[0]
            dst = edge_idx[1]
            lin_x = x @ W_lin.T + b_lin
            feat = jnp.concatenate([x[src], edge_weights, x[dst]], axis=1)
            h = jax.nn.relu(feat @ W_att1.T + b_att1)
            scores = (h @ W_att2.T + b_att2)[:, 0]
            m = jax.ops.segment_max(scores, src, num_segments=num_nodes)
            e = jnp.exp(scores - m[src])
            denom = jax.ops.segment_sum(e, src, num_segments=num_nodes)
            alpha = e / denom[src]
            msg = jax.ops.segment_sum(alpha[:, None] * lin_x[dst], src, num_segments=num_nodes)
            gi = x @ W_ih.T + b_ih
            gh = msg @ W_hh.T + b_hh
            i_r, i_z, i_n = jnp.split(gi, 3, axis=1)
            h_r, h_z, h_n = jnp.split(gh, 3, axis=1)
            r = jax.nn.sigmoid(i_r + h_r)
            z = jax.nn.sigmoid(i_z + h_z)
            n = jnp.tanh(i_n + r * h_n)
            new_h = (1.0 - z) * n + z * msg
            deg = jax.ops.segment_sum(jnp.ones_like(scores), src, num_segments=num_nodes)
            return jnp.where(deg[:, None] > 0, new_h, x)
        return _forward(x, edge_weights, W_att1, b_att1, W_att2, b_att2, W_lin, b_lin, W_ih, b_ih, W_hh, b_hh, edge_idx)
    edge_index = jnp.stack([src, dst])
    h = jnp.maximum(_layernorm(x, axis=-1), 0.0)
    x = x + _L0_gnn_ref(h, edge_index, L0_gnn_W0, L0_gnn_b0, L0_gnn_W1, L0_gnn_b1, L0_gnn_W2, L0_gnn_b2)
    h = jnp.maximum(_layernorm(x, axis=-1), 0.0)
    x = x + _L1_gnn_ref(h, edge_index, edge_attr_16, L1_gnn_W_att1, L1_gnn_b_att1, L1_gnn_W_att2, L1_gnn_b_att2, L1_gnn_W_lin, L1_gnn_b_lin, L1_gnn_W_ih, L1_gnn_b_ih, L1_gnn_W_hh, L1_gnn_b_hh)
    return x

_drawn_inputs = setup_inputs


def setup_inputs(seed=0):
    import zlib

    import numpy as np

    out = dict(_drawn_inputs(seed))
    spreads = {'L1_gnn_b_att1': (0.0, 2.0),
     'L1_gnn_b_lin': (0.0, 0.1),
     'L1_gnn_b_ih': (0.0, 0.1),
     'L1_gnn_b_hh': (0.0, 0.318)}
    factors = {'edge_attr_16': 8.0,
     'L0_gnn_b0': 8.0,
     'L0_gnn_b1': 8.0,
     'L0_gnn_b2': 5.615,
     'L1_gnn_W_att1': 8.0,
     'L1_gnn_W_att2': 8.0,
     'L1_gnn_W_hh': 2.813}
    for name, (base, spread) in spreads.items():
        noise = np.random.default_rng([zlib.crc32(name.encode()), seed]).standard_normal(out[name].shape)
        drawn = base * np.exp(spread * noise) if base else spread * noise
        out[name] = jnp.asarray(drawn.astype(out[name].dtype))
    for name, factor in factors.items():
        out[name] = (out[name] * factor).astype(out[name].dtype)
    return out
```

```python
import concourse.bass as bass
from concourse import mybir
from contextlib import ExitStack

F32 = mybir.dt.float32
BF16 = mybir.dt.bfloat16
F16 = mybir.dt.float16
I32 = mybir.dt.int32
ALU = mybir.AluOpType
ACT = mybir.ActivationFunctionType
AX = mybir.AxisListType

P = 128
N, D, ED, E = 3125, 64, 16, 53125
H1 = 2 * D + ED
NB = -(-N // P)
BN = -(-N // NB)
assert N == NB * BN
DIV, SHIFT = 4195, 19
assert all((n * DIV) >> SHIFT == n // BN for n in range(N + 1)) and N * DIV < 1 << 24
T = -(-E // P)
LAST_P = E // T
LAST_E = E - LAST_P * T
PAIR = 2 * P
NG = (E + NB * (PAIR - 1)) // PAIR
NG += NG % 4 and 4 - NG % 4
TT = 2 * NG
REC = 2 + ED
TRASH = P * TT
WIN = 512
AC = NB * P
ACOLS = NB * AC + WIN
QL = H1 + D
BIG = 2.0 ** 100
EPS = 1e-5
SPLIT3 = (0, 1, 2)


class Chain:

    def __init__(self, eng, sem, base=0):
        self.eng, self.sem, self.base, self.n = eng, sem, base, 0

    def link(self, ins):
        self.n += 1
        ins.then_inc(self.sem, 1)
        self.eng.wait_ge(self.sem, self.base + self.n)

    def step(self, idx, per):
        self.base, self.n, self.per = idx * per, 0, per

    def end(self):
        assert self.n == self.per, (self.n, self.per)


def run_steps(eng, count, lag, unroll, step):
    head = -(-(2 * unroll + lag) // unroll) * unroll
    head = min(head, count - count % unroll)
    loops = (count - head) // unroll
    for i in range(head):
        step(i, i % unroll, lambda l, i=i: 0 <= i - l < count)
    if loops:
        with eng.Fori(0, loops) as r:
            for u in range(unroll):
                step(r * unroll + (head + u), u, lambda l: True)
    for i in range(head + loops * unroll, count + lag):
        step(i, i % unroll, lambda l, i=i: 0 <= i - l < count)


def node_parts():
    return (0, BN - BN % 16), (BN - BN % 16, BN)


def known(i):
    return isinstance(i, int)


def gnn_kernel(nc, x, src, dst, attr, w_gcn, b_gcn, w_att1t, b_att1, w_att2, b_att2, w_lint, b_lin,
               w_iht, b_ih, w_hht, b_hh, eye, upper, out, dbg=None):
    dbg = dbg or {}
    table = nc.dram_tensor("edge_records", [TRASH + P, REC], F32, kind="Internal").ap()
    qtable = nc.dram_tensor("target_rows", [NB * P, QL], F32, kind="Internal").ap()
    with ExitStack() as ctx:
        def sb(name, shape, dt=F32):
            return ctx.enter_context(nc.sbuf_tensor(name, shape, dt))

        keep = dict(
            ident=sb("ident", [P, P]), identb=sb("identb", [P, P], BF16),
            upper=sb("upper_tri", [P, P]), ones=sb("ones", [P, P]), onesb=sb("onesb", [P, 1], BF16),
            iota=sb("iota_cols", [P, WIN], F16),
            x=sb("x_nodes", [P, NB, D]), h=sb("h_nodes", [P, NB, D]),
            bin_row=sb("bin_row", [1, NG + 8]),
            dinv=sb("dinv", [P, NB + 1]),
            wg=sb("w_gcn_sb", [D, 3, D]), bg=sb("b_gcn_sb", [P, 3, D]),
        )
        srt = ExitStack()
        with srt:
            rank_and_scatter(nc, srt, keep, x, src, dst, attr, w_gcn, b_gcn, eye, upper, table, dbg)
        with ExitStack() as adj:
            adjacency_and_gcn(nc, adj, keep, table, dbg)
        with ExitStack() as att:
            attention(nc, att, keep, table, qtable, w_att1t, b_att1, w_att2, b_att2, w_lint, b_lin,
                      w_iht, b_ih, w_hht, b_hh, out, dbg)


def layernorm_relu(nc, v, ch, xin, hout, tmp, sq, st, eps_std_wait, sqrt_ready):
    ch.link(nc.vector.tensor_reduce(st[:, 0, :], xin, AX.X, ALU.add))
    ch.link(nc.vector.tensor_scalar(st[:, 0, :], st[:, 0, :], 1.0 / D, None, ALU.mult))
    ch.link(nc.vector.tensor_tensor(tmp, xin, st[:, 0, :].unsqueeze(2).to_broadcast([P, NB, D]), ALU.subtract))
    ch.link(nc.vector.tensor_tensor(sq, tmp, tmp, ALU.mult))
    ch.link(nc.vector.tensor_reduce(st[:, 1, :], sq, AX.X, ALU.add))
    nc.vector.tensor_scalar(st[:, 1, :], st[:, 1, :], 1.0 / D, EPS, ALU.mult, ALU.add).then_inc(sqrt_ready, 1)
    v.wait_ge(eps_std_wait, 1)
    ch.link(nc.vector.reciprocal(st[:, 3, :], st[:, 2, :]))
    ch.link(nc.vector.tensor_tensor(sq, tmp, st[:, 3, :].unsqueeze(2).to_broadcast([P, NB, D]), ALU.mult))
    ch.link(nc.vector.tensor_scalar(hout, sq, 0.0, None, ALU.max))


def rank_and_scatter(nc, ctx, keep, x, src, dst, attr, w_gcn, b_gcn, eye, upper, table, dbg):
    def sb(name, shape, dt=F32):
        return ctx.enter_context(nc.sbuf_tensor(name, shape, dt))

    def sem(name):
        return ctx.enter_context(nc.semaphore(name))

    UN = 16
    HALF = UN // 2
    attr_in = sb("attr_in", [P, T, ED])
    dst_f = sb("dst_f", [P, T])
    lo_f = sb("lo_f", [P, T])
    row_i = sb("row_i", [P, T], I32)
    ring = sb("record_ring", [P, 2, HALF, REC])
    ring_i = sb("row_ring", [P, 2, HALF], I32)
    gate = sb("gate", [1, 2])
    with ExitStack() as c1:
        def sb1(name, shape, dt=F32):
            return c1.enter_context(nc.sbuf_tensor(name, shape, dt))

        def sem1(name):
            return c1.enter_context(nc.semaphore(name))

        src_i = sb1("src_i", [P, T], I32)
        dst_i = sb1("dst_i", [P, T], I32)
        int_a = sb1("int_a", [P, T], I32)
        int_b = sb1("int_b", [P, T], I32)
        f_a = sb1("f_a", [P, T])
        f_b = sb1("f_b", [P, T])
        eidx = sb1("edge_index", [P, T])
        hot = sb1("bin_hot", [P, NB, T])
        cum = sb1("bin_cum", [P, NB, T])
        iota_b = sb1("iota_bins", [P, NB])
        iota_g = sb1("iota_pairs", [1, NG])
        ends = sb1("bin_ends", [P, NB + 1])
        cnt = sb1("bin_count", [P, NB])
        tot_i = sb1("bin_total_i", [P, NB], I32)
        pairs = sb1("bin_pairs", [P, NB])
        endp = sb1("bin_end_pair", [P, NB])
        off = sb1("bin_offset", [P, NB])
        pad = sb1("pad_records", [P, TT // 2, REC])
        tmp = sb1("ln_tmp", [P, NB, D])
        sq = sb1("ln_sq", [P, NB, D])
        st = sb1("ln_stats", [P, 4, NB])
        ps_before = c1.enter_context(nc.psum_tensor("ps_before", [P, NB], F32))
        ps_total = c1.enter_context(nc.psum_tensor("ps_total", [P, NB], F32))

        padded = sem1("padded")
        loaded_ids = sem1("loaded_ids")
        loaded_attr = sem1("loaded_attr")
        loaded_x = sem1("loaded_x")
        loaded_const = sem1("loaded_const")
        pool_made = sem1("pool_made")
        prefilled = sem1("prefilled")
        counted = sem1("counted")
        prefixed = sem1("prefixed")
        var_ready = sem1("var_ready")
        std_ready = sem1("std_ready")
        vsteps = sem1("vsteps")
        psteps = sem1("psteps")
        copied = sem1("const_copied")

        def edge_parts(dst_tile, dram, per):
            main = LAST_P - LAST_P % 16
            full = dram[0:LAST_P * T] if len(dram.shape) == 1 else dram[0:LAST_P * T, :]
            pat = "(p t) -> p t" if len(dram.shape) == 1 else "(p t) c -> p t c"
            full = full.rearrange(pat, t=T)
            rest = dram[LAST_P * T:E] if len(dram.shape) == 1 else dram[LAST_P * T:E, :]
            rest = rest.unsqueeze(0)
            return [(dst_tile[0:main], full[0:main]), (dst_tile[main:LAST_P], full[main:LAST_P]),
                    (dst_tile[LAST_P:P, 0:LAST_E], rest)]

        with nc.Block() as block:
            @block.sync
            def _(sp):
                sp.wait_ge(padded, 2)
                for t, d in ((src_i, src), (dst_i, dst)):
                    for o, i in edge_parts(t, d, 1):
                        sp.dma_start(o, i).then_inc(loaded_ids, 16)
                sp.wait_ge(padded, 4)
                for o, i in edge_parts(attr_in, attr, ED):
                    sp.dma_start(o, i).then_inc(loaded_attr, 16)
                xv = x.rearrange("(t p) d -> p t d", p=BN)
                for a, b in node_parts():
                    sp.dma_start(keep["x"][a:b, :, :], xv[a:b, :, :]).then_inc(loaded_x, 16)
                sp.wait_ge(loaded_attr, 48)
                sp.wait_ge(loaded_x, 32)

            @block.scalar
            def _(act):
                act.dma_start(keep["ident"][:], eye).then_inc(loaded_const, 16)
                act.dma_start(keep["upper"][:], upper).then_inc(loaded_const, 16)
                act.dma_start(keep["wg"][:], w_gcn.rearrange("l i o -> i l o")).then_inc(loaded_const, 16)
                act.dma_start(keep["bg"][:], b_gcn.partition_broadcast(P)).then_inc(loaded_const, 16)
                act.wait_ge(pool_made, 2)
                main = table[0:TRASH, :].rearrange("(p t) c -> p t c", t=TT)
                for k in range(2):
                    act.dma_start(main[:, k * (TT // 2):(k + 1) * (TT // 2), :], pad[:]).then_inc(prefilled, 16)
                act.wait_ge(loaded_const, 64)
                nc.scalar.activation(keep["identb"][:], keep["ident"][:], ACT.Copy).then_inc(copied, 1)
                act.wait_ge(var_ready, 1)
                nc.scalar.activation(st[:, 2, :], st[:, 1, :], ACT.Sqrt).then_inc(std_ready, 1)
                act.wait_ge(prefilled, 32)

            @block.gpsimd
            def _(pool):
                ch = Chain(pool, psteps)
                nc.gpsimd.memset(keep["ones"][:], 1.0)
                nc.gpsimd.memset(gate[:], 1.0)
                nc.gpsimd.memset(keep["onesb"][:], 1.0)
                nc.gpsimd.iota(iota_b[:], [[1, NB]], base=0, channel_multiplier=0, allow_small_or_imprecise_dtypes=True)
                nc.gpsimd.iota(eidx[:], [[1, T]], base=0, channel_multiplier=T, allow_small_or_imprecise_dtypes=True)
                nc.gpsimd.iota(iota_g[:], [[1, NG]], base=0, channel_multiplier=0, allow_small_or_imprecise_dtypes=True)
                nc.gpsimd.iota(keep["iota"][:], [[1, WIN]], base=0, channel_multiplier=0,
                               allow_small_or_imprecise_dtypes=True).then_inc(pool_made, 1)
                ch.link(nc.gpsimd.memset(pad[:], 0.0))
                nc.gpsimd.memset(pad[:, :, 1:2], -1.0).then_inc(pool_made, 1)

            @block.tensor
            def _(pe):
                pe.wait_ge(loaded_const, 64)
                pe.wait_ge(pool_made, 1)
                pe.wait_ge(counted, 1)
                nc.tensor.matmul(ps_before[:], keep["upper"][:], cnt[:], start=True, stop=True)
                nc.tensor.matmul(ps_total[:], keep["ones"][:], cnt[:], start=True, stop=True).then_inc(prefixed, 1)

            @block.vector
            def _(v):
                ch = Chain(v, vsteps)
                nc.vector.memset(src_i[:, LAST_E:T], N).then_inc(padded, 1)
                nc.vector.memset(dst_i[:, LAST_E:T], 0).then_inc(padded, 1)
                nc.vector.memset(attr_in[:, LAST_E:T, :], 0.0).then_inc(padded, 1)
                nc.vector.memset(keep["x"][96:P, :, :], 0.0).then_inc(padded, 1)
                nc.vector.memset(ends[:, 0:1], 0.0)
                v.wait_ge(loaded_ids, 96)
                nc.vector.tensor_scalar(int_a[:], src_i[:], float(DIV), None, ALU.mult)
                ch.link(nc.vector.tensor_scalar(int_b[:], dst_i[:], float(DIV), None, ALU.mult))
                nc.vector.tensor_scalar(int_a[:], int_a[:], SHIFT, None, ALU.logical_shift_right)
                ch.link(nc.vector.tensor_scalar(int_b[:], int_b[:], SHIFT, None, ALU.logical_shift_right))
                ch.link(nc.vector.tensor_copy(f_a[:], int_a[:]))
                nc.vector.scalar_tensor_tensor(lo_f[:], f_a[:], float(-BN), src_i[:], ALU.mult, ALU.add)
                nc.vector.scalar_tensor_tensor(dst_f[:], int_b[:], float(P - BN), dst_i[:], ALU.mult, ALU.add)
                v.wait_ge(pool_made, 1)
                ch.link(nc.vector.tensor_tensor(hot[:], f_a[:].unsqueeze(1).to_broadcast([P, NB, T]),
                                                iota_b[:].unsqueeze(2).to_broadcast([P, NB, T]), ALU.is_equal))
                hot2, cum2 = (a[:].rearrange("p b t -> p (b t)") for a in (hot, cum))
                ch.link(nc.vector.tensor_tensor_scan(cum2, hot2, hot2, 0.0, ALU.add, ALU.max))
                ch.link(nc.vector.tensor_copy(ends[:, 1:NB + 1], cum[:, :, T - 1]))
                nc.vector.tensor_tensor(cnt[:], ends[:, 1:NB + 1], ends[:, 0:NB], ALU.subtract).then_inc(counted, 1)
                v.wait_ge(prefixed, 1)
                ch.link(nc.vector.tensor_scalar(tot_i[:], ps_total[:], float(PAIR - 1), None, ALU.add))
                ch.link(nc.vector.tensor_scalar(tot_i[:], tot_i[:], 8, None, ALU.logical_shift_right))
                ch.link(nc.vector.tensor_copy(pairs[:], tot_i[:]))
                ch.link(nc.vector.tensor_tensor_scan(endp[:], pairs[:], pairs[:], 0.0, ALU.add, ALU.max))
                ch.link(nc.vector.tensor_tensor(off[:], endp[:], pairs[:], ALU.subtract))
                ch.link(nc.vector.tensor_scalar(off[:], off[:], float(PAIR), -1.0, ALU.mult, ALU.add))
                ch.link(nc.vector.tensor_tensor(off[:], off[:], ends[:, 0:NB], ALU.subtract))
                ch.link(nc.vector.tensor_tensor(off[:], off[:], ps_before[:], ALU.add))
                ch.link(nc.vector.tensor_tensor(cum[:], cum[:], off[:].unsqueeze(2).to_broadcast([P, NB, T]), ALU.add))
                ch.link(nc.vector.tensor_tensor(cum[:], cum[:], hot[:], ALU.mult))
                ch.link(nc.vector.tensor_reduce(f_a[:], cum[:].rearrange("p b t -> p t b"), AX.X, ALU.add))
                ch.link(nc.vector.tensor_copy(int_a[:], f_a[:]))
                nc.vector.tensor_scalar(int_b[:], int_a[:], 7, None, ALU.logical_shift_right)
                ch.link(nc.vector.tensor_scalar(dst_i[:], int_a[:], P - 1, None, ALU.bitwise_and))
                nc.vector.tensor_copy(f_a[:], dst_i[:])
                ch.link(nc.vector.tensor_copy(f_b[:], int_b[:]))
                ch.link(nc.vector.scalar_tensor_tensor(f_a[:], f_a[:], float(TT), f_b[:], ALU.mult, ALU.add))
                ch.link(nc.vector.tensor_scalar(f_b[:], eidx[:], float(E), None, ALU.is_ge))
                ch.link(nc.vector.scalar_tensor_tensor(f_b[:], eidx[:], float(TRASH - E), f_b[:], ALU.add, ALU.mult))
                ch.link(nc.vector.tensor_tensor(f_a[:], f_a[:], f_b[:], ALU.add))
                ch.link(nc.vector.tensor_copy(row_i[:], f_a[:]))
                c0 = cum[0:1, :, :].rearrange("p b t -> p (b t)")[:, 0:NG * NB].rearrange("p (g b) -> p g b", b=NB)
                ch.link(nc.vector.tensor_tensor(c0, iota_g[:].unsqueeze(2).to_broadcast([1, NG, NB]),
                                                endp[0:1, :].unsqueeze(1).to_broadcast([1, NG, NB]), ALU.is_ge))
                ch.link(nc.vector.tensor_reduce(f_b[0:1, 0:NG], c0, AX.X, ALU.add))
                ch.link(nc.vector.tensor_scalar(keep["bin_row"][0:1, 0:NG], f_b[0:1, 0:NG], float(NB - 1), None, ALU.min))
                v.wait_ge(loaded_x, 32)
                layernorm_relu(nc, v, ch, keep["x"][:], keep["h"][:], tmp[:], sq[:], st, std_ready, var_ready)

    copied_ring = sem("ring_copied")
    gated = sem("gated")
    scattered = [sem(f"scattered{k}") for k in range(2)]
    LOOPS = T // UN
    with nc.Block() as block:
        @block.vector
        def _(v):
            def half(i, k):
                t0 = i * UN + k * HALF
                if not known(i) or i >= 1:
                    v.wait_ge(scattered[k], i * (16 * HALF))
                nc.vector.tensor_copy(ring_i[:, k, :], row_i[:, bass.ds(t0, HALF)])
                nc.vector.tensor_copy(ring[:, k, :, 0], dst_f[:, bass.ds(t0, HALF)])
                nc.vector.tensor_copy(ring[:, k, :, 1], lo_f[:, bass.ds(t0, HALF)])
                nc.vector.tensor_copy(ring[:, k, :, 2:REC], attr_in[:, bass.ds(t0, HALF), :]).then_inc(copied_ring, 1)
            for k in range(2):
                half(0, k)
            with v.Fori(1, LOOPS) as i:
                for k in range(2):
                    half(i, k)

        @block.gpsimd
        def _(pool):
            def half(i, k):
                if not known(i) or 2 * i + k > 0:
                    pool.wait_ge(gated, i * 2 + k)
                pool.wait_ge(copied_ring, i * 2 + k + 1)
                nc.gpsimd.tensor_tensor(gate[:, 1:2], gate[:, 0:1], gate[:, 0:1], ALU.mult).then_inc(gated, 1)
                for j in range(HALF):
                    pool.indirect_dma_start(table[:, :], bass.IndirectOffsetOnAxis(ap=ring_i[:, k, j:j + 1], axis=0),
                                            ring[:, k, j, :], None).then_inc(scattered[k], 16)
            for k in range(2):
                half(0, k)
            with pool.Fori(1, LOOPS) as i:
                for k in range(2):
                    half(i, k)

        @block.sync
        def _(sp):
            for k in range(2):
                sp.wait_ge(scattered[k], 16 * HALF * LOOPS)
            if "table" in dbg:
                sp.dma_start(dbg["table"], table[0:TRASH, :]).then_inc(copied_ring, 16)
                sp.wait_ge(copied_ring, 16 + 2 * LOOPS)
            if "bin_row" in dbg:
                sp.dma_start(dbg["bin_row"], keep["bin_row"][0:1, 0:NG]).then_inc(copied_ring, 16)
                sp.dma_start(dbg["h"], keep["h"][:]).then_inc(copied_ring, 16)
                sp.wait_ge(copied_ring, 48+ 2 * LOOPS)


class Loads:

    def __init__(self, eng, name, top):
        self.eng, self.top = eng, top
        self.regs = [eng.alloc_register(f"{name}{k}") for k in range(4)]

    def __call__(self, row, at):
        self.eng.load(self.regs, row[0:1, bass.ds(at, 4)])
        return [self.eng.snap(r, min_val=0, max_val=self.top) for r in self.regs]


LEAD = 4


def adjacency_and_gcn(nc, ctx, keep, table, dbg):
    def sb(name, shape, dt=F32):
        return ctx.enter_context(nc.sbuf_tensor(name, shape, dt))

    adj = sb("adjacency", [P, ACOLS], BF16)
    edges = ExitStack()
    dst_s = edges.enter_context(nc.sbuf_tensor("dst_sorted", [P, NG, 2], F32))
    rel_s = edges.enter_context(nc.sbuf_tensor("dst_in_window", [P, NG, 2], F32))
    lo_s = edges.enter_context(nc.sbuf_tensor("lo_sorted", [P, NG, 2], F32))
    win_i = edges.enter_context(nc.sbuf_tensor("window_at", [1, NG + 8], I32))
    bin_i = edges.enter_context(nc.sbuf_tensor("bin_at", [1, NG + 8], I32))
    flag_i = edges.enter_context(nc.sbuf_tensor("wide_flag", [1, 1], I32))

    HG = NG // 2
    with ExitStack() as c1:
        def sb1(name, shape, dt=F32):
            return c1.enter_context(nc.sbuf_tensor(name, shape, dt))

        def sem1(name):
            return c1.enter_context(nc.semaphore(name))

        rec = adj[:, 0:2 * TT * REC].bitcast(F32).rearrange("p (t c) -> p t c", c=REC)
        low = sb1("low", [P, NG, 2])
        ext = sb1("extremes", [P, 2, NG])
        mm = sb1("pair_extremes", [P, 4])
        row = sb1("extreme_rows", [1, 4, HG])
        w0 = sb1("window_start", [1, NG])
        w_i = sb1("window_start_i", [1, NG], I32)
        tmp = sb1("row_tmp", [1, NG])
        flag = sb1("flag_f", [1, 1])
        ps_t = c1.enter_context(nc.psum_tensor("ps_extremes", [P, 4, P], F32))
        ps_row = c1.enter_context(nc.psum_tensor("ps_rows", [1, 4, HG], F32))
        ps_w = c1.enter_context(nc.psum_tensor("ps_window", [P, NG], F32))
        loaded = sem1("records_loaded")
        vsteps = sem1("stat_vsteps")
        to_pe = sem1("stat_to_pe")
        from_pe = sem1("stat_from_pe")
        with nc.Block() as block:
            @block.sync
            def _(sp):
                sp.dma_start(rec, table[0:TRASH, :].rearrange("(p t) c -> p t c", t=TT)).then_inc(loaded, 16)
                sp.wait_ge(loaded, 16)

            @block.tensor
            def _(pe):
                pe.wait_ge(to_pe, 1)
                for q in range(4):
                    last = nc.tensor.transpose(ps_t[0:HG, q, :], ext[:, q // 2, (q % 2) * HG:(q % 2 + 1) * HG], keep["ident"][:])
                last.then_inc(from_pe, 1)
                pe.wait_ge(to_pe, 2)
                for q in range(4):
                    last = nc.tensor.matmul(ps_row[0:1, q, :], mm[0:HG, q:q + 1], keep["ident"][0:HG, 0:HG], start=True, stop=True)
                last.then_inc(from_pe, 1)
                pe.wait_ge(to_pe, 3)
                nc.tensor.matmul(ps_w[:], keep["ones"][0:1, :], w0[:], start=True, stop=True).then_inc(from_pe, 1)

            @block.vector
            def _(v):
                ch = Chain(v, vsteps)
                nc.vector.memset(win_i[:], 0)
                nc.vector.memset(bin_i[:], 0)
                v.wait_ge(loaded, 16)
                rec2 = rec.rearrange("p (g j) c -> p g j c", j=2)
                nc.vector.tensor_copy(dst_s[:], rec2[:, :, :, 0])
                ch.link(nc.vector.tensor_copy(lo_s[:], rec2[:, :, :, 1]))
                ch.link(nc.vector.tensor_scalar(low[:], lo_s[:], 0.0, 4096.0, ALU.is_lt, ALU.mult))
                ch.link(nc.vector.tensor_tensor(low[:], low[:], dst_s[:], ALU.add))
                nc.vector.tensor_reduce(ext[:, 0, :], low[:], AX.X, ALU.min)
                nc.vector.tensor_reduce(ext[:, 1, :], dst_s[:], AX.X, ALU.max).then_inc(to_pe, 1)
                v.wait_ge(from_pe, 1)
                nc.vector.tensor_reduce(mm[0:HG, 0:2], ps_t[0:HG, 0:2, :], AX.X, ALU.min)
                nc.vector.tensor_reduce(mm[0:HG, 2:4], ps_t[0:HG, 2:4, :], AX.X, ALU.max).then_inc(to_pe, 1)
                v.wait_ge(from_pe, 2)
                ch.link(nc.vector.tensor_copy(row[:], ps_row[:]))
                least, most = (row[0:1, 2 * k:2 * k + 2, :].rearrange("p a g -> p (a g)") for k in range(2))
                ch.link(nc.vector.tensor_scalar(w_i[:], least, float(NB * P - 1), None, ALU.min))
                ch.link(nc.vector.tensor_scalar(w_i[:], w_i[:], -2, None, ALU.bitwise_and))
                nc.vector.tensor_copy(w0[:], w_i[:]).then_inc(to_pe, 1)
                v.wait_ge(to_pe, 3)
                nc.vector.tensor_scalar(bin_i[0:1, LEAD:LEAD + NG], keep["bin_row"][0:1, 0:NG], float(AC), None, ALU.mult)
                ch.link(nc.vector.scalar_tensor_tensor(win_i[0:1, LEAD:LEAD + NG], keep["bin_row"][0:1, 0:NG], float(AC), w0[:], ALU.mult, ALU.add))
                ch.link(nc.vector.tensor_tensor(tmp[:], most, w0[:], ALU.subtract))
                ch.link(nc.vector.tensor_reduce(flag[:], tmp[:], AX.X, ALU.max))
                ch.link(nc.vector.tensor_scalar(flag_i[:], flag[:], float(WIN), None, ALU.is_ge))
                v.wait_ge(from_pe, 3)
                ch.link(nc.vector.tensor_tensor(rel_s[:], dst_s[:], ps_w[:].unsqueeze(2).to_broadcast([P, NG, 2]), ALU.subtract))

    with ExitStack() as c2:
        def sb2(name, shape, dt=F32):
            return c2.enter_context(nc.sbuf_tensor(name, shape, dt))

        def sem2(name):
            return c2.enter_context(nc.semaphore(name))

        R = 2
        src_hot = sb2("src_hot", [P, R, 2, P], BF16)
        dst_hot = sb2("dst_hot", [P, R, 2, WIN], BF16)
        far = sb2("far_dst", [P, NG, 2])
        far2 = sb2("far_mask", [P, NG, 2])
        ps = [c2.enter_context(nc.psum_tensor(f"ps_counts{k}", [P, WIN], F32)) for k in range(R)]
        cleared = sem2("adj_cleared")
        hots = sem2("hots_ready")
        counted = sem2("pair_counted")
        added = sem2("pair_added")
        far_hots, far_counted, far_added = sem2("far_hots"), sem2("far_counted"), sem2("far_added")
        vsteps = sem2("adj_vsteps")

        with nc.Block() as block:
            CUT = 26 * 1024
            words = adj[:].bitcast(F32)

            @block.gpsimd
            def _(pool):
                nc.gpsimd.memset(words[:, CUT:], 0.0).then_inc(cleared, 1)

            def hot(v, g, u, target):
                for j in range(2):
                    nc.vector.tensor_scalar(src_hot[:, u, j, :], keep["iota"][:, 0:P], lo_s[:, bass.ds(g, 1), j], None, ALU.is_equal)
                    last = nc.vector.tensor_scalar(dst_hot[:, u, j, :], keep["iota"][:], target[:, bass.ds(g, 1), j], None, ALU.is_equal)
                return last

            def count(u):
                for j in range(2):
                    last = nc.tensor.matmul(ps[u][:], src_hot[:, u, j, :], dst_hot[:, u, j, :], start=(j == 0), stop=(j == 1))
                return last

            @block.vector
            def _(v):
                ch = Chain(v, vsteps)
                ch.link(nc.vector.memset(words[:, 0:CUT], 0.0))
                v.wait_ge(cleared, 1)
                step = AC + P
                diag = adj[:, 0:(NB - 1) * step].rearrange("p (b c) -> p b c", c=step)[:, :, 0:P]
                ch.link(nc.vector.tensor_copy(diag, keep["identb"][:].unsqueeze(1).to_broadcast([P, NB - 1, P])))
                ch.link(nc.vector.tensor_copy(adj[:, (NB - 1) * step:(NB - 1) * step + P], keep["identb"][:]))
                load = Loads(v, "window", ACOLS - WIN)
                at = [None]

                def one(i, u, live):
                    if u == 0:
                        at[0] = load(win_i, i + LEAD - 1)
                    if live(0):
                        if not known(i) or i >= R:
                            v.wait_ge(counted, i - R + 1)
                        hot(v, i, u % R, rel_s).then_inc(hots, 1)
                    if live(1):
                        v.wait_ge(counted, i)
                        if not known(i) or i >= 2:
                            v.wait_ge(added, i - 1)
                        win = adj[:, bass.ds(at[0][u], WIN)]
                        nc.vector.tensor_tensor(win, win, ps[(u + 1) % R][:], ALU.add).then_inc(added, 1)
                run_steps(v, NG, 1, 4, one)
                v.wait_ge(added, NG)

            @block.tensor
            def _(pe):
                def one(i, u, live):
                    if live(0):
                        pe.wait_ge(hots, i + 1)
                        if not known(i) or i >= R:
                            pe.wait_ge(added, i - R + 1)
                        count(u % R).then_inc(counted, 1)
                run_steps(pe, NG, 0, 4, one)

        with nc.Block() as block:
            @block.vector
            def _(v):
                ch = Chain(v, vsteps, 3)
                wide = v.value_load(flag_i[0:1, 0:1], min_val=0, max_val=1)
                with v.If(wide != 0):
                    load = v.alloc_register("bin_column")
                    ch.link(nc.vector.tensor_scalar(far2[:], rel_s[:], float(WIN), None, ALU.is_ge))
                    ch.link(nc.vector.scalar_tensor_tensor(far[:], dst_s[:], 1.0, far2[:], ALU.add, ALU.mult))
                    ch.link(nc.vector.tensor_scalar(far[:], far[:], -1.0, None, ALU.add))
                    with v.Fori(0, 7) as k:
                        with v.Fori(0, NG) as g:
                            v.load(load, bin_i[0:1, bass.ds(g + LEAD, 1)])
                            col = v.snap(load, min_val=0, max_val=(NB - 1) * AC)
                            hot(v, g, 0, far).then_inc(far_hots, 1)
                            v.wait_ge(far_counted, k * NG + g + 1)
                            win = adj[:, bass.ds(col + k * WIN, WIN)]
                            nc.vector.tensor_tensor(win, win, ps[0][:], ALU.add).then_inc(far_added, 1)
                            v.wait_ge(far_added, k * NG + g + 1)
                        nc.vector.tensor_scalar(far[:], far[:], float(-WIN), None, ALU.add).then_inc(far_hots, 1)
                        v.wait_ge(far_hots, (k + 1) * (NG + 1))

            @block.tensor
            def _(pe):
                wide = pe.value_load(flag_i[0:1, 0:1], min_val=0, max_val=1)
                with pe.If(wide != 0):
                    with pe.Fori(0, 7) as k:
                        with pe.Fori(0, NG) as g:
                            pe.wait_ge(far_hots, k * (NG + 1) + g + 1)
                            count(0).then_inc(far_counted, 1)

            if "A" in dbg:
                @block.sync
                def _(sp):
                    wide = sp.value_load(flag_i[0:1, 0:1], min_val=0, max_val=1)
                    with sp.If(wide != 0):
                        sp.wait_ge(far_added, 7 * NG)
                    sp.dma_start(dbg["A"], adj[:]).then_inc(cleared, 16)
                    sp.dma_start(dbg["flag"], flag_i[:]).then_inc(cleared, 16)
                    sp.wait_ge(cleared, 33)
    edges.close()

    h3 = [sb(f"h_parts{k}", [P, NB, 3, D], BF16) for k in range(2)]
    with ExitStack() as c3:
        ps_deg = c3.enter_context(nc.psum_tensor("ps_deg", [P, NB], F32))
        ideg = c3.enter_context(nc.sbuf_tensor("inv_deg", [P, NB], F32))
        degs, inv, root, vsteps = (c3.enter_context(nc.semaphore(x)) for x in ("deg_ready", "inv_ready", "root_ready", "deg_vsteps"))
        with nc.Block() as block:
            @block.tensor
            def _(pe):
                with pe.Fori(0, NB) as m:
                    for k in range(NB):
                        nc.tensor.matmul(ps_deg[:, bass.ds(m, 1)], adj[:, bass.ds(m * P + k * AC, P)], keep["onesb"][:],
                                         start=(k == 0), stop=(k == NB - 1))
                pe.drain().then_inc(degs, 1)

            @block.scalar
            def _(act):
                act.wait_ge(inv, 1)
                nc.scalar.activation(keep["dinv"][:, 0:NB], ideg[:], ACT.Sqrt).then_inc(root, 1)

            @block.vector
            def _(v):
                ch = Chain(v, vsteps)
                v.wait_ge(degs, 1)
                nc.vector.reciprocal(ideg[:], ps_deg[:]).then_inc(inv, 1)
                v.wait_ge(root, 1)
                h = keep["h"]
                ch.link(nc.vector.tensor_tensor(h[:], h[:], keep["dinv"][:, 0:NB].unsqueeze(2).to_broadcast([P, NB, D]), ALU.mult))
                ch.link(nc.vector.tensor_copy(h3[0][:, :, 0, :], h[:]))
                ch.link(nc.vector.tensor_tensor(h[:], h[:], h3[0][:, :, 0, :], ALU.subtract))
                ch.link(nc.vector.tensor_copy(h3[0][:, :, 1, :], h[:]))
                ch.link(nc.vector.tensor_tensor(h3[0][:, :, 2, :], h[:], h3[0][:, :, 1, :], ALU.subtract))

    for layer in range(3):
        with ExitStack() as c4:
            gcn_layer(nc, c4, keep, adj, h3[layer % 2], h3[(layer + 1) % 2], layer)
    if "x1" in dbg:
        with nc.semaphore("dbg_x1") as s, nc.Block() as block:
            @block.sync
            def _(sp):
                sp.dma_start(dbg["x1"], keep["x"][:]).then_inc(s, 16)
                sp.wait_ge(s, 16)


def gcn_layer(nc, ctx, keep, adj, h3, h3_next, layer):
    def sb(name, shape, dt=F32):
        return ctx.enter_context(nc.sbuf_tensor(f"{name}_{layer}", shape, dt))

    def sem(name):
        return ctx.enter_context(nc.semaphore(f"{name}_{layer}"))

    def psum(name, shape):
        return [ctx.enter_context(nc.psum_tensor(f"{name}{k}_{layer}", shape, F32)) for k in range(2)]

    agg = sb("agg", [P, 2, P])
    agg_t = sb("agg_t", [D, 2, P])
    res = sb("res", [P, 2, D])
    ps_agg, ps_t, ps_o = psum("ps_agg", [P, 3, D]), psum("ps_aggt", [P, P]), psum("ps_out", [P, D])
    gathered, summed, turned, turned_c, multiplied, finished = (
        sem(x) for x in ("gathered", "summed", "turned", "turned_copied", "multiplied", "finished"))
    vsteps, zeroed = sem("layer_vsteps"), sem("agg_zeroed")
    last_layer = layer == 2

    with nc.Block() as block:
        @block.tensor
        def _(pe):
            def one(i, u, live):
                if live(0):
                    if not known(i) or i >= 2:
                        pe.wait_ge(summed, i - 1)
                    for k in range(NB):
                        last = nc.tensor.matmul(ps_agg[u][:], adj[:, bass.ds(i * P + k * AC, P)], h3[:, k, :, :],
                                                start=(k == 0), stop=(k == NB - 1))
                    last.then_inc(gathered, 1)
                if live(1):
                    pe.wait_ge(summed, i)
                    if not known(i) or i >= 3:
                        pe.wait_ge(turned_c, i - 2)
                    nc.tensor.transpose(ps_t[1 - u][:], agg[:, 1 - u, :], keep["ident"][:]).then_inc(turned, 1)
                if live(2):
                    pe.wait_ge(turned_c, i - 1)
                    if not known(i) or i >= 4:
                        pe.wait_ge(finished, i - 3)
                    nc.tensor.matmul(ps_o[u][:], agg_t[:, u, :], keep["wg"][:, layer, :], start=True, stop=True).then_inc(multiplied, 1)
            run_steps(pe, NB, 2, 2, one)

        @block.scalar
        def _(act):
            def one(i, u, live):
                if live(0):
                    act.wait_ge(turned, i + 1)
                    if not known(i) or i >= 2:
                        act.wait_ge(multiplied, i - 1)
                    nc.scalar.activation(agg_t[:, u, :], ps_t[u][0:D, :], ACT.Copy).then_inc(turned_c, 1)
            run_steps(act, NB, 0, 2, one)

        @block.vector
        def _(v):
            ch = Chain(v, vsteps)
            nc.vector.memset(agg[:], 0.0).then_inc(zeroed, 1)
            v.wait_ge(zeroed, 1)

            def one(i, u, live):
                if live(0):
                    v.wait_ge(gathered, i + 1)
                    if not known(i) or i >= 2:
                        v.wait_ge(turned, i - 1)
                    nc.vector.tensor_reduce(agg[:, u, 0:D], ps_agg[u][:].rearrange("p s d -> p d s"), AX.X, ALU.add).then_inc(summed, 1)
                if live(2):
                    m = i - 2
                    dinv = keep["dinv"][:, bass.ds(m, 1)]
                    v.wait_ge(multiplied, i - 1)
                    ch.step(m, 2 if last_layer else 6)
                    r = res[:, u, :]
                    ch.link(nc.vector.scalar_tensor_tensor(r, ps_o[u][:], dinv, keep["bg"][:, layer, :], ALU.mult, ALU.add))
                    if last_layer:
                        xm = keep["x"][:, bass.ds(m, 1), :]
                        ch.link(nc.vector.tensor_tensor(xm, xm, res[:, u:u + 1, :], ALU.add))
                        nc.vector.memset(res[0:1, u, 0:1], 0.0).then_inc(finished, 1)
                    else:
                        part = [h3_next[:, bass.ds(m, 1), k, :] for k in range(3)]
                        r3 = res[:, u:u + 1, :]
                        ch.link(nc.vector.tensor_scalar(r, r, 0.0, dinv, ALU.max, ALU.mult))
                        ch.link(nc.vector.tensor_copy(part[0], r3))
                        ch.link(nc.vector.tensor_tensor(r3, r3, part[0], ALU.subtract))
                        ch.link(nc.vector.tensor_copy(part[1], r3))
                        ch.link(nc.vector.tensor_tensor(part[2], r3, part[1], ALU.subtract))
                        nc.vector.memset(res[0:1, u, 0:1], 0.0).then_inc(finished, 1)
                    ch.end()
            run_steps(v, NB, 2, 2, one)


class Bins:

    def __init__(self, eng, count):
        self.eng = eng
        self.regs = [eng.alloc_register(f"bin{k}") for k in range(count)]

    def __call__(self, row, at):
        self.eng.load(self.regs, row[0:1, bass.ds(at, len(self.regs))])
        return [self.eng.snap(r, min_val=0, max_val=NB - 1) for r in self.regs]


def attention(nc, ctx, keep, table, qtable, w_att1t, b_att1, w_att2, b_att2, w_lint, b_lin,
              w_iht, b_ih, w_hht, b_hh, out, dbg):
    def sb(name, shape, dt=F32):
        return ctx.enter_context(nc.sbuf_tensor(name, shape, dt))

    p3 = sb("source_parts", [P, NB, 3, H1], BF16)
    gi = sb("gates_in", [P, NB, 3 * D])
    w_edge = sb("w_edge", [2 * REC, 2, H1])
    w2 = sb("w_att2_sb", [P, H1])
    b2 = sb("b_att2_sb", [P, 1])
    w_hh = sb("w_hh_sb", [D + 1, 3 * D])
    acc = sb("acc", [P, NB, D + 1])
    with ExitStack() as c1:
        node_tables(nc, c1, keep, p3, gi, w_edge, w2, b2, w_hh, qtable, w_att1t, b_att1, w_att2, b_att2,
                    w_lint, b_lin, w_iht, b_ih, w_hht, b_hh)
    with ExitStack() as c2:
        edge_attention(nc, c2, keep, p3, w_edge, w2, b2, acc, table, qtable)
    with ExitStack() as c3:
        gru(nc, c3, keep, gi, w_hh, acc, out)


def node_tables(nc, ctx, keep, p3, gi, w_edge, w2, b2, w_hh, qtable, w_att1t, b_att1, w_att2, b_att2,
                w_lint, b_lin, w_iht, b_ih, w_hht, b_hh):
    def sb(name, shape, dt=F32):
        return ctx.enter_context(nc.sbuf_tensor(name, shape, dt))

    def sem(name):
        return ctx.enter_context(nc.semaphore(name))

    A1, G1, Q1, L1 = 0, H1, H1 + 3 * D, 2 * H1 + 3 * D
    w_node = sb("w_node", [D + 1, L1 + D])
    ql = sb("target_values", [P, NB, QL])
    tmp, sq, st = sb("ln_tmp2", [P, NB, D]), sb("ln_sq2", [P, NB, D]), sb("ln_stats2", [P, 4, NB])
    tile = sb("h_tile", [P, 2, P])
    h_t = sb("h_turned", [D + 1, 2, P])
    rest = sb("p_rest", [P, 2, H1])
    ps_t = [ctx.enter_context(nc.psum_tensor(f"ps_ht{k}", [P, P], F32)) for k in range(2)]
    ps_a = [ctx.enter_context(nc.psum_tensor(f"ps_source{k}", [P, H1], F32)) for k in range(2)]
    ps_q = [ctx.enter_context(nc.psum_tensor(f"ps_target{k}", [P, 3 * D + QL], F32)) for k in range(2)]
    weights, zeroed, normed, var_r, std_r, vsteps = (
        sem(x) for x in ("node_weights", "node_zeroed", "node_normed", "var_ready2", "std_ready2", "node_vsteps"))
    tiled, turned, turned_c, made, kept_a, kept_p, stored = (
        sem(x) for x in ("tiled", "h_turned_ready", "h_turned_copied", "made", "kept_act", "kept_parts", "stored"))
    NW = 14

    with nc.Block() as block:
        @block.gpsimd
        def _(pool):
            nc.gpsimd.memset(tile[:], 0.0).then_inc(zeroed, 1)

        @block.sync
        def _(sp):
            sp.wait_ge(zeroed, 2)
            for o, i in ((w_node[0:D, A1:A1 + H1], w_att1t[0:D, :]), (w_node[0:D, G1:G1 + 3 * D], w_iht),
                         (w_node[0:D, Q1:Q1 + H1], w_att1t[D + ED:H1, :]), (w_node[0:D, L1:L1 + D], w_lint),
                         (w_node[D:D + 1, A1:A1 + H1], b_att1.unsqueeze(0)),
                         (w_node[D:D + 1, G1:G1 + 3 * D], b_ih.unsqueeze(0)),
                         (w_node[D:D + 1, L1:L1 + D], b_lin.unsqueeze(0)),
                         (w_edge[2:REC, 0, :], w_att1t[D:D + ED, :]), (w_edge[REC + 2:2 * REC, 1, :], w_att1t[D:D + ED, :]),
                         (w2[:], w_att2[0, :].partition_broadcast(P)), (b2[:], b_att2.partition_broadcast(P)),
                         (w_hh[0:D, :], w_hht), (w_hh[D:D + 1, :], b_hh.unsqueeze(0))):
                sp.dma_start(o, i).then_inc(weights, 16)
            sp.wait_ge(kept_a, NB)
            sp.dma_start(qtable.rearrange("(t p) c -> p t c", p=P), ql[:]).then_inc(stored, 16)
            sp.wait_ge(stored, 16)
            sp.wait_ge(weights, 16 * (NW - 1))

        @block.scalar
        def _(act):
            act.wait_ge(var_r, 1)
            nc.scalar.activation(st[:, 2, :], st[:, 1, :], ACT.Sqrt).then_inc(std_r, 1)
            act.wait_ge(normed, 1)
            act.wait_ge(zeroed, 2)

            def one(i, u, live):
                if live(0):
                    if not known(i) or i >= 2:
                        act.wait_ge(turned, i - 1)
                    nc.scalar.activation(tile[:, u:u + 1, 0:D], keep["h"][:, bass.ds(i, 1), :], ACT.Copy).then_inc(tiled, 1)
                if live(1):
                    act.wait_ge(turned, i)
                    if not known(i) or i >= 3:
                        act.wait_ge(made, i - 2)
                    nc.scalar.activation(h_t[0:D, 1 - u, :], ps_t[1 - u][0:D, :], ACT.Copy).then_inc(turned_c, 1)
                if live(2):
                    m = i - 2
                    act.wait_ge(made, i - 1)
                    nc.scalar.activation(gi[:, bass.ds(m, 1), :], ps_q[u][:, 0:3 * D].unsqueeze(1), ACT.Copy)
                    nc.scalar.activation(ql[:, bass.ds(m, 1), :], ps_q[u][:, 3 * D:].unsqueeze(1), ACT.Copy).then_inc(kept_a, 1)
            run_steps(act, NB, 2, 2, one)

        @block.tensor
        def _(pe):
            pe.wait_ge(weights, 16 * (NW - 1))
            pe.wait_ge(zeroed, 2)

            def one(i, u, live):
                if live(0):
                    pe.wait_ge(tiled, i + 1)
                    if not known(i) or i >= 2:
                        pe.wait_ge(turned_c, i - 1)
                    nc.tensor.transpose(ps_t[u][:], tile[:, u, :], keep["ident"][:]).then_inc(turned, 1)
                if live(1):
                    pe.wait_ge(turned_c, i)
                    if not known(i) or i >= 3:
                        pe.wait_ge(kept_a, i - 2)
                        pe.wait_ge(kept_p, i - 2)
                    v = 1 - u
                    nc.tensor.matmul(ps_a[v][:], h_t[:, v, :], w_node[:, 0:H1], start=True, stop=True)
                    nc.tensor.matmul(ps_q[v][:], h_t[:, v, :], w_node[:, H1:L1 + D], start=True, stop=True).then_inc(made, 1)
            run_steps(pe, NB, 1, 2, one)

        @block.vector
        def _(v):
            ch = Chain(v, vsteps)
            nc.vector.memset(w_node[D:D + 1, :], 0.0)
            nc.vector.memset(w_edge[:], 0.0)
            nc.vector.memset(h_t[D:D + 1, :, :], 1.0).then_inc(zeroed, 1)
            layernorm_relu(nc, v, ch, keep["x"][:], keep["h"][:], tmp[:], sq[:], st, std_r, var_r)
            nc.vector.memset(st[0:1, 0, 0:1], 0.0).then_inc(normed, 1)
            before = ch.n
            ch.step(0, 3)

            def one(i, u, live):
                if live(0):
                    v.wait_ge(made, i + 1)
                    ch.base, ch.n = before + i * 3, 0
                    part = [p3[:, bass.ds(i, 1), k, :] for k in range(3)]
                    r = rest[:, u:u + 1, :]
                    ps = ps_a[u][:, 0:H1].unsqueeze(1)
                    ch.link(nc.vector.tensor_scalar(part[0], ps, 1.0, None, ALU.mult))
                    ch.link(nc.vector.tensor_tensor(r, ps, part[0], ALU.subtract))
                    ch.link(nc.vector.tensor_copy(part[1], r))
                    nc.vector.tensor_tensor(part[2], r, part[1], ALU.subtract).then_inc(kept_p, 1)
                    ch.end()
            run_steps(v, NB, 0, 2, one)


def edge_attention(nc, ctx, keep, p3, w_edge, w2, b2, acc, table, qtable):
    def sb(name, shape, dt=F32):
        return ctx.enter_context(nc.sbuf_tensor(name, shape, dt))

    def sem(name):
        return ctx.enter_context(nc.semaphore(name))

    def psum(name, shape, dt=F32, n=2):
        return [ctx.enter_context(nc.psum_tensor(f"{name}{k}", shape, dt)) for k in range(n)]

    U = 8
    GR = 4
    bin_i = sb("bin_at2", [1, NG + 24], I32)
    rec = sb("rec_ring", [P, 2 * U, REC])
    idx = sb("idx_ring", [P, 2 * U], I32)
    rows = sb("row_ring2", [P, 2 * U, QL + 1])
    gate = sb("gate2", [1, 2])
    hot = sb("hot", [P, 2, 2, P], BF16)
    hot32 = sb("hot32", [P, 8, 2, P])
    neg = sb("neg", [P, 2, 2, P])
    hot_t = sb("hot_turned", [P, 4, 2, P], BF16)
    rec_t = sb("rec_turned", [2 * REC, 2, P])
    hid = sb("hidden", [P, 2, H1])
    score = sb("score", [P, 4, 2])
    by_src = sb("by_source", [P, 2, 2, P])
    mx = sb("mx", [P, 4])
    new = sb("new_top", [P, 4])
    parts = sb("top_parts", [P, 4, 2], BF16)
    drop = sb("top_drop", [P, 4])
    scale = sb("scale", [P, 4])
    arg = sb("arg", [P, 4, 2])
    arg2 = sb("arg2", [P, 4, 2])
    ew = sb("edge_weight", [P, 4, 2])
    val = sb("weighted", [P, 2, 2, D + 1])
    top = sb("top", [P, NB])

    ps_turn = psum("ps_turn", [P, 2 * P])
    ps_hid = psum("ps_hid", [P, 2, H1])
    ps_src = psum("ps_src", [P, 2, P])
    ps_top = psum("ps_top", [P, 2, 2, 2], n=1)[0]
    ps_sum = psum("ps_sum", [P, 2, D + 1], n=1)[0]

    ready, rec_in0, rec_in1, idx_ready, gated = (sem(x) for x in ("att_ready", "rec_in0", "rec_in1", "idx_ready", "gated2"))
    rec_in = [rec_in0, rec_in1]
    gathered = [sem(f"gathered{k}") for k in range(U)]
    (hots, turned, turned_c, lifted, hidden, scored, laid, src_turned, topped, top_back, args, weighed, rescaled,
     valued, aggregated, summed) = (
        sem(x) for x in ("hots2", "turned2", "turned_c2", "lifted", "hidden_ready", "scored", "laid", "src_turned",
                         "topped", "top_back", "args", "weighed", "rescaled", "valued", "aggregated", "summed2"))
    c_score, c_top, c_arg = sem("c_score"), sem("c_top"), sem("c_arg")
    setup = sem("att_setup")

    def later(i, n):
        return not known(i) or i >= n

    tview = table[0:TRASH, :].rearrange("(p t) c -> p t c", t=TT)

    with nc.Block() as block:
        @block.sync
        def _(sp):
            def one(i, u, live):
                if u % GR == 0:
                    h = u // GR
                    if later(i, U):
                        sp.wait_ge(turned, i - U + GR)
                        sp.wait_ge(hots, i - U + GR)
                        sp.wait_ge(idx_ready, i - U + GR)
                    sp.dma_start(rec[:, 2 * GR * h:2 * GR * (h + 1), :], tview[:, bass.ds(i * 2, 2 * GR), :]).then_inc(rec_in[h], 16)
            run_steps(sp, NG, 0, U, one)
            sp.wait_ge(rec_in[0], 16 * (-(-NG // U)))
            sp.wait_ge(rec_in[1], 16 * (NG // U))

        @block.gpsimd
        def _(pool):
            pool.wait_ge(ready, 1)

            def one(i, u, live):
                if u % 2 == 0:
                    if later(i, 2):
                        pool.wait_ge(gated, i)
                    if later(i, U):
                        pool.wait_ge(valued, i - U + 2)
                        pool.wait_ge(scored, i - U + 2)
                    pool.wait_ge(idx_ready, i - u % GR + GR)
                    nc.gpsimd.tensor_tensor(gate[:, 1:2], gate[:, 0:1], gate[:, 0:1], ALU.mult).then_inc(gated, 2)
                for j in range(2):
                    t = 2 * u + j
                    pool.indirect_dma_start(rows[:, t, 0:QL], None, qtable[:, :],
                                            bass.IndirectOffsetOnAxis(ap=idx[:, t:t + 1], axis=0)).then_inc(gathered[u], 16)
            run_steps(pool, NG, 0, U, one)

        @block.tensor
        def _(pe):
            pe.wait_ge(ready, 1)
            bins = Bins(pe, U)
            at = [None]

            def one(i, u, live):
                if u == 0:
                    at[0] = bins(bin_i, i + U - 1)
                if live(0):
                    pe.wait_ge(hots, i + 1)
                    if later(i, 2):
                        pe.wait_ge(turned_c, i - 1)
                    o16 = ps_turn[u % 2][:, 0:P].bitcast(BF16)
                    for j in range(2):
                        nc.tensor.transpose(o16[:, j * P:(j + 1) * P], hot[:, u % 2, j, :], keep["identb"][:])
                    nc.tensor.transpose(ps_turn[u % 2][0:2 * REC, P:2 * P], rec[:, 2 * u:2 * u + 2, :].rearrange("p t c -> p (t c)"),
                                        keep["ident"][:]).then_inc(turned, 1)
                if live(1):
                    pe.wait_ge(turned_c, i)
                    if later(i, 3):
                        pe.wait_ge(scored, i - 2)
                    w = (u - 1) % U
                    for j in range(2):
                        for k in SPLIT3:
                            nc.tensor.matmul(ps_hid[w % 2][:, j, :], hot_t[:, w % 4, j, :], p3[:, bass.ds(at[0][u], 1), k, :],
                                             start=(k == 0), stop=False)
                        last = nc.tensor.matmul(ps_hid[w % 2][:, j, :], rec_t[:, w % 2, :], w_edge[:, j, :], start=False, stop=True)
                    last.then_inc(hidden, 1)
                if live(2):
                    w = (u - 2) % U
                    pe.wait_ge(laid, i - 1)
                    if later(i, 4):
                        pe.wait_ge(topped, i - 3)
                    for j in range(2):
                        last = nc.tensor.transpose(ps_src[w % 2][:, j, :], by_src[:, w % 2, j, :], keep["ident"][:])
                    last.then_inc(src_turned, 1)
                if live(3):
                    w = (u - 3) % U
                    pe.wait_ge(topped, i - 2)
                    if later(i, 4):
                        pe.wait_ge(args, i - 3)
                    for j in range(2):
                        last = nc.tensor.matmul(ps_top[:, w % 2, j, :], hot_t[:, w % 4, j, :], parts[:, w % 4, :], start=True, stop=True)
                    last.then_inc(top_back, 1)
                if live(5):
                    w = (u - 5) % U
                    pe.wait_ge(valued, i - 4)
                    if later(i, 6):
                        pe.wait_ge(summed, i - 5)
                    for j in range(2):
                        last = nc.tensor.matmul(ps_sum[:, w % 2, :], hot32[:, w % 8, j, :], val[:, w % 2, j, :],
                                                start=(j == 0), stop=(j == 1))
                    last.then_inc(aggregated, 1)
            run_steps(pe, NG, 5, U, one)

        @block.scalar
        def _(act):
            act.wait_ge(ready, 1)

            def one(i, u, live):
                if live(0):
                    act.wait_ge(hots, i + 1)
                    if later(i, 8):
                        act.wait_ge(aggregated, i - 7)
                    if later(i, 2):
                        act.wait_ge(laid, i - 1)
                    nc.scalar.activation(hot32[:, u % 8, :, :], hot[:, u % 2, :, :], ACT.Copy)
                    nc.scalar.activation(neg[:, u % 2, :, :], hot[:, u % 2, :, :], ACT.Copy, bias=-BIG, scale=BIG).then_inc(lifted, 1)
                    act.wait_ge(turned, i + 1)
                    if later(i, 4):
                        act.wait_ge(top_back, i - 3)
                    if later(i, 2):
                        act.wait_ge(hidden, i - 1)
                    nc.scalar.activation(hot_t[:, u % 4, :, :].rearrange("p j s -> p (j s)"), ps_turn[u % 2][:, 0:P].bitcast(BF16), ACT.Copy)
                    nc.scalar.activation(rec_t[:, u % 2, :], ps_turn[u % 2][0:2 * REC, P:2 * P], ACT.Copy).then_inc(turned_c, 1)
                if live(1):
                    w = (u - 1) % U
                    act.wait_ge(scored, i)
                    act.wait_ge(lifted, i)
                    if later(i, 3):
                        act.wait_ge(src_turned, i - 2)
                    for j in range(2):
                        last = nc.scalar.activation(by_src[:, w % 2, j, :], neg[:, w % 2, j, :], ACT.Identity,
                                                    bias=score[:, w % 4, j:j + 1])
                    last.then_inc(laid, 1)
                if live(3):
                    w = (u - 3) % U
                    act.wait_ge(args, i - 2)
                    if later(i, 7):
                        act.wait_ge(valued, i - 6)
                        act.wait_ge(summed, i - 6)
                    nc.scalar.activation(scale[:, w % 4:w % 4 + 1], drop[:, w % 4:w % 4 + 1], ACT.Exp)
                    nc.scalar.activation(ew[:, w % 4, :], arg2[:, w % 4, :], ACT.Exp).then_inc(weighed, 1)
            run_steps(act, NG, 3, U, one)

        @block.vector
        def _(v):
            nc.vector.memset(rows[:, :, QL:QL + 1], 1.0)
            nc.vector.memset(gate[:], 1.0)
            nc.vector.memset(top[:], -BIG)
            nc.vector.memset(acc[:], 0.0)
            nc.vector.memset(bin_i[:], 0).then_inc(setup, 1)
            v.wait_ge(setup, 1)
            nc.vector.tensor_copy(bin_i[0:1, U:U + NG], keep["bin_row"][0:1, 0:NG]).then_inc(setup, 1)
            v.wait_ge(setup, 2)
            v.sem_inc(ready, 1)
            bins = Bins(v, U + 3)
            ch_s, ch_t, ch_a = Chain(v, c_score), Chain(v, c_top), Chain(v, c_arg)
            at = [None]

            def one(i, u, live):
                if u == 0:
                    at[0] = bins(bin_i, i + U - 5)
                if live(0):
                    if u % GR == 0:
                        h = u // GR
                        v.wait_ge(rec_in[h], (i - u) * (16 // U) + 16)
                        if later(i, U):
                            for k in range(GR):
                                v.wait_ge(gathered[h * GR + k], (i - u) * (32 // U))
                        nc.vector.tensor_copy(idx[:, 2 * GR * h:2 * GR * (h + 1)], rec[:, 2 * GR * h:2 * GR * (h + 1), 0]).then_inc(idx_ready, GR)
                    if later(i, 2):
                        v.wait_ge(turned, i - 1)
                        v.wait_ge(lifted, i - 1)
                    for j in range(2):
                        last = nc.vector.tensor_scalar(hot[:, u % 2, j, :], keep["iota"][:, 0:P], rec[:, 2 * u + j, 1:2], None, ALU.is_equal)
                    last.then_inc(hots, 1)
                if live(1):
                    g, w = i - 1, (u - 1) % U
                    v.wait_ge(hidden, i)
                    v.wait_ge(gathered[w], (g - w) * (32 // U) + 32)
                    if later(i, 5):
                        v.wait_ge(laid, i - 4)
                    ch_s.step(g, 3)
                    ch_s.link(nc.vector.tensor_tensor(hid[:], ps_hid[w % 2][:], rows[:, 2 * w:2 * w + 2, 0:H1], ALU.add))
                    nc.vector.scalar_tensor_tensor(hid[:, 0, :], hid[:, 0, :], 0.0, w2[:], ALU.max, ALU.mult, accum_out=score[:, w % 4, 0:1])
                    ch_s.link(nc.vector.scalar_tensor_tensor(hid[:, 1, :], hid[:, 1, :], 0.0, w2[:], ALU.max, ALU.mult, accum_out=score[:, w % 4, 1:2]))
                    ch_s.link(nc.vector.tensor_scalar(score[:, w % 4, :], score[:, w % 4, :], b2[:, 0:1], None, ALU.add))
                    v.sem_inc(scored, 1)
                    ch_s.end()
                if live(2):
                    g, w = i - 2, (u - 2) % U
                    s4 = w % 4
                    b = at[0][u + 3]
                    tp = top[:, bass.ds(b, 1)]
                    v.wait_ge(src_turned, i - 1)
                    ch_t.step(g, 6)
                    ch_t.link(nc.vector.tensor_reduce(mx[:, s4:s4 + 1], ps_src[w % 2][:].rearrange("p j e -> p (j e)"), AX.X, ALU.max))
                    ch_t.link(nc.vector.tensor_tensor(mx[:, s4:s4 + 1], mx[:, s4:s4 + 1], tp, ALU.max))
                    ch_t.link(nc.vector.tensor_copy(parts[:, s4, 0:1], mx[:, s4:s4 + 1]))
                    ch_t.link(nc.vector.tensor_tensor(parts[:, s4, 1:2], mx[:, s4:s4 + 1], parts[:, s4, 0:1], ALU.subtract))
                    ch_t.link(nc.vector.tensor_tensor(new[:, s4:s4 + 1], parts[:, s4, 0:1], parts[:, s4, 1:2], ALU.add))
                    ch_t.link(nc.vector.tensor_tensor(drop[:, s4:s4 + 1], tp, new[:, s4:s4 + 1], ALU.subtract))
                    nc.vector.tensor_scalar(tp, new[:, s4:s4 + 1], 1.0, None, ALU.mult).then_inc(topped, 1)
                    v.wait_ge(topped, i - 1)
                    ch_t.end()
                if live(3):
                    g, w = i - 3, (u - 3) % U
                    s4 = w % 4
                    v.wait_ge(top_back, i - 2)
                    ch_a.step(g, 2)
                    ch_a.link(nc.vector.tensor_reduce(arg[:, s4, :], ps_top[:, w % 2, :, :], AX.X, ALU.add))
                    ch_a.link(nc.vector.tensor_tensor(arg[:, s4, :], score[:, s4, :], arg[:, s4, :], ALU.subtract))
                    nc.vector.tensor_scalar(arg2[:, s4, :], arg[:, s4, :], 0.0, None, ALU.min).then_inc(args, 1)
                    ch_a.end()
                if live(4):
                    w = (u - 4) % U
                    v.wait_ge(weighed, i - 3)
                    if later(i, 6):
                        v.wait_ge(aggregated, i - 5)
                    nc.vector.tensor_tensor(val[:, w % 2, :, :], rows[:, 2 * w:2 * w + 2, H1:QL + 1],
                                            ew[:, w % 4, :].unsqueeze(2).to_broadcast([P, 2, D + 1]), ALU.mult).then_inc(valued, 1)
                if live(5):
                    w = (u - 5) % U
                    v.wait_ge(aggregated, i - 4)
                    if later(i, 6):
                        v.wait_ge(summed, i - 5)
                    a = acc[:, bass.ds(at[0][u], 1), :]
                    nc.vector.scalar_tensor_tensor(a, a, scale[:, w % 4:w % 4 + 1], ps_sum[:, w % 2:w % 2 + 1, :], ALU.mult, ALU.add).then_inc(summed, 1)
            run_steps(v, NG, 5, U, one)


def gru(nc, ctx, keep, gi, w_hh, acc, out):
    def sb(name, shape, dt=F32):
        return ctx.enter_context(nc.sbuf_tensor(name, shape, dt))

    def sem(name):
        return ctx.enter_context(nc.semaphore(name))

    msg, gh = sb("message", [P, NB, D]), sb("gates_msg", [P, NB, 3 * D])
    den, has = sb("den", [P, NB]), sb("has_edge", [P, NB])
    tile, m_t = sb("msg_tile", [P, 2, P]), sb("msg_turned", [D + 1, 2, P])
    rz, nn, t1 = sb("rz", [P, NB, 2 * D]), sb("nn", [P, NB, D]), sb("gru_t1", [P, NB, D])
    ps_t = [ctx.enter_context(nc.psum_tensor(f"ps_mt{k}", [P, P], F32)) for k in range(2)]
    ps_g = [ctx.enter_context(nc.psum_tensor(f"ps_gates{k}", [P, 3 * D], F32)) for k in range(2)]
    zeroed, begun, vsteps, tiled, turned, turned_c, made, kept, summed, gated, pre_n, n_done, stored = (
        sem(x) for x in ("gru_zeroed", "msg_ready", "gru_vsteps", "gru_tiled", "gru_turned", "gru_turned_c", "gru_made",
                         "gru_kept", "gru_summed", "gru_gated", "gru_pre_n", "gru_n", "out_stored"))
    x, h = keep["x"], keep["h"]

    with nc.Block() as block:
        @block.gpsimd
        def _(pool):
            nc.gpsimd.memset(tile[:], 0.0).then_inc(zeroed, 1)

        @block.scalar
        def _(act):
            act.wait_ge(begun, 1)
            act.wait_ge(zeroed, 2)

            def one(i, u, live):
                if live(0):
                    if not known(i) or i >= 2:
                        act.wait_ge(turned, i - 1)
                    nc.scalar.activation(tile[:, u:u + 1, 0:D], msg[:, bass.ds(i, 1), :], ACT.Copy).then_inc(tiled, 1)
                if live(1):
                    act.wait_ge(turned, i)
                    if not known(i) or i >= 3:
                        act.wait_ge(made, i - 2)
                    nc.scalar.activation(m_t[0:D, 1 - u, :], ps_t[1 - u][0:D, :], ACT.Copy).then_inc(turned_c, 1)
            run_steps(act, NB, 1, 2, one)
            act.wait_ge(summed, 1)
            nc.scalar.activation(rz[:], rz[:], ACT.Sigmoid).then_inc(gated, 1)
            act.wait_ge(pre_n, 1)
            nc.scalar.activation(nn[:], nn[:], ACT.Tanh).then_inc(n_done, 1)

        @block.tensor
        def _(pe):
            def one(i, u, live):
                if live(0):
                    pe.wait_ge(tiled, i + 1)
                    if not known(i) or i >= 2:
                        pe.wait_ge(turned_c, i - 1)
                    nc.tensor.transpose(ps_t[u][:], tile[:, u, :], keep["ident"][:]).then_inc(turned, 1)
                if live(1):
                    pe.wait_ge(turned_c, i)
                    if not known(i) or i >= 3:
                        pe.wait_ge(kept, i - 2)
                    nc.tensor.matmul(ps_g[1 - u][:], m_t[:, 1 - u, :], w_hh[:], start=True, stop=True).then_inc(made, 1)
            run_steps(pe, NB, 1, 2, one)

        @block.vector
        def _(v):
            ch = Chain(v, vsteps)
            nc.vector.memset(m_t[D:D + 1, :, :], 1.0).then_inc(zeroed, 1)
            nc.vector.tensor_scalar(has[:], acc[:, :, D], 0.5, None, ALU.is_ge)
            ch.link(nc.vector.tensor_scalar(den[:], acc[:, :, D], 0.5, None, ALU.max))
            ch.link(nc.vector.reciprocal(den[:], den[:]))
            nc.vector.tensor_tensor(msg[:], acc[:, :, 0:D], den[:].unsqueeze(2).to_broadcast([P, NB, D]), ALU.mult).then_inc(begun, 1)

            def one(i, u, live):
                if live(0):
                    v.wait_ge(made, i + 1)
                    nc.vector.tensor_scalar(gh[:, bass.ds(i, 1), :], ps_g[u][:].unsqueeze(1), 1.0, None, ALU.mult).then_inc(kept, 1)
            run_steps(v, NB, 0, 2, one)
            v.wait_ge(kept, NB)
            nc.vector.tensor_tensor(rz[:], gi[:, :, 0:2 * D], gh[:, :, 0:2 * D], ALU.add).then_inc(summed, 1)
            v.wait_ge(gated, 1)
            ch.link(nc.vector.tensor_tensor(t1[:], rz[:, :, 0:D], gh[:, :, 2 * D:3 * D], ALU.mult))
            nc.vector.tensor_tensor(nn[:], t1[:], gi[:, :, 2 * D:3 * D], ALU.add).then_inc(pre_n, 1)
            v.wait_ge(n_done, 1)
            z = rz[:, :, D:2 * D]
            ch.link(nc.vector.tensor_tensor(t1[:], msg[:], nn[:], ALU.subtract))
            ch.link(nc.vector.tensor_tensor(t1[:], t1[:], z, ALU.mult))
            ch.link(nc.vector.tensor_tensor(t1[:], t1[:], nn[:], ALU.add))
            ch.link(nc.vector.tensor_tensor(t1[:], t1[:], h[:], ALU.subtract))
            ch.link(nc.vector.tensor_tensor(t1[:], t1[:], has[:].unsqueeze(2).to_broadcast([P, NB, D]), ALU.mult))
            ch.link(nc.vector.tensor_tensor(t1[:], t1[:], h[:], ALU.add))
            ch.link(nc.vector.tensor_tensor(x[:], x[:], t1[:], ALU.add))
            v.sem_inc(begun, 1)

        @block.sync
        def _(sp):
            sp.wait_ge(begun, 2)
            ov = out.rearrange("(t p) d -> p t d", p=BN)
            for a, b in node_parts():
                sp.dma_start(ov[a:b, :, :], x[a:b, :, :]).then_inc(stored, 16)
            sp.wait_ge(stored, 32)


_OUT = ((N, D), "float32")


def kernel(x, src, dst, edge_attr_16, L0_gnn_W0, L0_gnn_b0, L0_gnn_W1, L0_gnn_b1, L0_gnn_W2, L0_gnn_b2,
           L1_gnn_W_att1, L1_gnn_b_att1, L1_gnn_W_att2, L1_gnn_b_att2, L1_gnn_W_lin, L1_gnn_b_lin,
           L1_gnn_W_ih, L1_gnn_b_ih, L1_gnn_W_hh, L1_gnn_b_hh):
    import numpy as np
    import concourse.bacc as bacc
    from concourse.bass_utils import run_bass_kernel_spmd

    def turned(w):
        return np.ascontiguousarray(np.asarray(w).T)

    arrays = dict(
        x=x, src=src, dst=dst, attr=edge_attr_16,
        w_gcn=np.stack([np.asarray(w) for w in (L0_gnn_W0, L0_gnn_W1, L0_gnn_W2)]),
        b_gcn=np.stack([np.asarray(b) for b in (L0_gnn_b0, L0_gnn_b1, L0_gnn_b2)]),
        w_att1t=turned(L1_gnn_W_att1), b_att1=L1_gnn_b_att1, w_att2=L1_gnn_W_att2, b_att2=L1_gnn_b_att2,
        w_lint=turned(L1_gnn_W_lin), b_lin=L1_gnn_b_lin, w_iht=turned(L1_gnn_W_ih), b_ih=L1_gnn_b_ih,
        w_hht=turned(L1_gnn_W_hh), b_hh=L1_gnn_b_hh,
        eye=np.eye(P, dtype=np.float32), upper=np.triu(np.ones((P, P), np.float32), 1),
    )
    nc = bacc.Bacc("TRN2", target_bir_lowering=False, num_devices=1)
    ins, args = {}, {}
    for name, a in arrays.items():
        a = np.ascontiguousarray(a)
        ins[f"in_{name}"] = a
        args[name] = nc.dram_tensor(f"in_{name}", a.shape, mybir.dt.from_np(a.dtype), kind="ExternalInput").ap()
    args["out"] = nc.dram_tensor("out_0", _OUT[0], F32, kind="ExternalOutput").ap()
    gnn_kernel(nc, **args)
    r = run_bass_kernel_spmd(nc, [ins], core_ids=[0])
    return r.results[0]["out_0"]
```

```python
import concourse.bass as bass
from concourse import mybir
from contextlib import ExitStack

F32 = mybir.dt.float32
BF16 = mybir.dt.bfloat16
F16 = mybir.dt.float16
I32 = mybir.dt.int32
ALU = mybir.AluOpType
ACT = mybir.ActivationFunctionType
AX = mybir.AxisListType

P = 128
N, D, ED, E = 3125, 64, 16, 53125
H1 = 2 * D + ED
NB = -(-N // P)
BN = -(-N // NB)
assert N == NB * BN
DIV, SHIFT = 4195, 19
assert all((n * DIV) >> SHIFT == n // BN for n in range(N + 1)) and N * DIV < 1 << 24
T = -(-E // P)
LAST_P = E // T
LAST_E = E - LAST_P * T
PAIR = 2 * P
NG = (E + NB * (PAIR - 1)) // PAIR
NG += NG % 4 and 4 - NG % 4
TT = 2 * NG
A_PART = (0, 0, 0, 1, 1, 1, 2, 2)
W_PART = (0, 1, 2, 0, 1, 2, 0, 1)
REC = 2 + len(A_PART) * ED // 2
TRASH = P * TT
WIN = 512
AC = NB * P
ACOLS = NB * AC + WIN
HW = H1 + 1
QL = HW + D
BIG = 2.0 ** 100
EPS = 1e-5
SPLIT3 = (0, 1, 2)


class Chain:

    def __init__(self, eng, sem, base=0):
        self.eng, self.sem, self.base, self.n = eng, sem, base, 0

    def link(self, ins):
        self.n += 1
        ins.then_inc(self.sem, 1)
        self.eng.wait_ge(self.sem, self.base + self.n)

    def step(self, idx, per):
        self.base, self.n, self.per = idx * per, 0, per

    def end(self):
        assert self.n == self.per, (self.n, self.per)


def run_steps(eng, count, lag, unroll, step):
    head = -(-(2 * unroll + lag) // unroll) * unroll
    head = min(head, count - count % unroll)
    loops = (count - head) // unroll
    for i in range(head):
        step(i, i % unroll, lambda l, i=i: 0 <= i - l < count)
    if loops:
        with eng.Fori(0, loops) as r:
            for u in range(unroll):
                step(r * unroll + (head + u), u, lambda l: True)
    for i in range(head + loops * unroll, count + lag):
        step(i, i % unroll, lambda l, i=i: 0 <= i - l < count)


def node_parts():
    return (0, BN - BN % 16), (BN - BN % 16, BN)


def known(i):
    return isinstance(i, int)


def gnn_kernel(nc, x, src, dst, attr, w_gcn, b_gcn, w_att1t, b_att1, w_att2, b_att2, w_lint, b_lin,
               w_iht, b_ih, w_hht, b_hh, eye, upper, part_mask, out, dbg=None):
    dbg = dbg or {}
    table = nc.dram_tensor("edge_records", [TRASH + P, REC], F32, kind="Internal").ap()
    qtable = nc.dram_tensor("target_rows", [NB * P, QL], F32, kind="Internal").ap()
    with ExitStack() as ctx:
        def sb(name, shape, dt=F32):
            return ctx.enter_context(nc.sbuf_tensor(name, shape, dt))

        keep = dict(
            ident=sb("ident", [P, P]), identb=sb("identb", [P, P], BF16),
            upper=sb("upper_tri", [P, P]), ones=sb("ones", [P, P]), onesb=sb("onesb", [P, 1], BF16),
            iota=sb("iota_cols", [P, WIN], F16),
            x=sb("x_nodes", [P, NB, D]), h=sb("h_nodes", [P, NB, D]),
            bin_row=sb("bin_row", [1, NG + 8]),
            dinv=sb("dinv", [P, NB + 1]),
            wg=sb("w_gcn_sb", [D, 3, D]), bg=sb("b_gcn_sb", [P, 3, D]),
        )
        srt = ExitStack()
        with srt:
            rank_and_scatter(nc, srt, keep, x, src, dst, attr, w_gcn, b_gcn, eye, upper, table, dbg)
        with ExitStack() as adj:
            adjacency_and_gcn(nc, adj, keep, table, dbg)
        with ExitStack() as att:
            attention(nc, att, keep, table, qtable, w_att1t, b_att1, w_att2, b_att2, w_lint, b_lin,
                      w_iht, b_ih, w_hht, b_hh, part_mask, out, dbg)


def layernorm_relu(nc, v, ch, xin, hout, tmp, sq, st, eps_std_wait, sqrt_ready):
    ch.link(nc.vector.tensor_reduce(st[:, 0, :], xin, AX.X, ALU.add))
    ch.link(nc.vector.tensor_scalar(st[:, 0, :], st[:, 0, :], 1.0 / D, None, ALU.mult))
    ch.link(nc.vector.tensor_tensor(tmp, xin, st[:, 0, :].unsqueeze(2).to_broadcast([P, NB, D]), ALU.subtract))
    ch.link(nc.vector.tensor_tensor(sq, tmp, tmp, ALU.mult))
    ch.link(nc.vector.tensor_reduce(st[:, 1, :], sq, AX.X, ALU.add))
    nc.vector.tensor_scalar(st[:, 1, :], st[:, 1, :], 1.0 / D, EPS, ALU.mult, ALU.add).then_inc(sqrt_ready, 1)
    v.wait_ge(eps_std_wait, 1)
    ch.link(nc.vector.reciprocal(st[:, 3, :], st[:, 2, :]))
    ch.link(nc.vector.tensor_tensor(sq, tmp, st[:, 3, :].unsqueeze(2).to_broadcast([P, NB, D]), ALU.mult))
    ch.link(nc.vector.tensor_scalar(hout, sq, 0.0, None, ALU.max))


def rank_and_scatter(nc, ctx, keep, x, src, dst, attr, w_gcn, b_gcn, eye, upper, table, dbg):
    def sb(name, shape, dt=F32):
        return ctx.enter_context(nc.sbuf_tensor(name, shape, dt))

    def sem(name):
        return ctx.enter_context(nc.semaphore(name))

    UN = 16
    HALF = UN // 2
    attr_in = sb("attr_in", [P, T, ED])
    dst_f = sb("dst_f", [P, T])
    lo_f = sb("lo_f", [P, T])
    dst_bin = sb("dst_bin", [P, T])
    dst_lo = sb("dst_lo", [P, T])
    row_i = sb("row_i", [P, T], I32)
    ring = sb("record_ring", [P, 2, HALF, REC])
    ring_i = sb("row_ring", [P, 2, HALF], I32)
    gate = sb("gate", [1, 2])
    with ExitStack() as c1:
        def sb1(name, shape, dt=F32):
            return c1.enter_context(nc.sbuf_tensor(name, shape, dt))

        def sem1(name):
            return c1.enter_context(nc.semaphore(name))

        src_i = sb1("src_i", [P, T], I32)
        dst_i = sb1("dst_i", [P, T], I32)
        int_a = sb1("int_a", [P, T], I32)
        int_b = sb1("int_b", [P, T], I32)
        f_a = sb1("f_a", [P, T])
        f_b = sb1("f_b", [P, T])
        eidx = sb1("edge_index", [P, T])
        hot = sb1("bin_hot", [P, NB, T])
        cum = sb1("bin_cum", [P, NB, T])
        iota_b = sb1("iota_bins", [P, NB])
        iota_g = sb1("iota_pairs", [1, NG])
        ends = sb1("bin_ends", [P, NB + 1])
        cnt = sb1("bin_count", [P, NB])
        tot_i = sb1("bin_total_i", [P, NB], I32)
        pairs = sb1("bin_pairs", [P, NB])
        endp = sb1("bin_end_pair", [P, NB])
        off = sb1("bin_offset", [P, NB])
        pad = sb1("pad_records", [P, TT // 8, REC])
        tmp = sb1("ln_tmp", [P, NB, D])
        sq = sb1("ln_sq", [P, NB, D])
        st = sb1("ln_stats", [P, 4, NB])
        ps_before = c1.enter_context(nc.psum_tensor("ps_before", [P, NB], F32))
        ps_total = c1.enter_context(nc.psum_tensor("ps_total", [P, NB], F32))

        padded = sem1("padded")
        loaded_ids = sem1("loaded_ids")
        loaded_attr = sem1("loaded_attr")
        loaded_x = sem1("loaded_x")
        loaded_const = sem1("loaded_const")
        pool_made = sem1("pool_made")
        prefilled = sem1("prefilled")
        counted = sem1("counted")
        prefixed = sem1("prefixed")
        var_ready = sem1("var_ready")
        std_ready = sem1("std_ready")
        vsteps = sem1("vsteps")
        psteps = sem1("psteps")
        copied = sem1("const_copied")

        def edge_parts(dst_tile, dram, per):
            main = LAST_P - LAST_P % 16
            full = dram[0:LAST_P * T] if len(dram.shape) == 1 else dram[0:LAST_P * T, :]
            pat = "(p t) -> p t" if len(dram.shape) == 1 else "(p t) c -> p t c"
            full = full.rearrange(pat, t=T)
            rest = dram[LAST_P * T:E] if len(dram.shape) == 1 else dram[LAST_P * T:E, :]
            rest = rest.unsqueeze(0)
            return [(dst_tile[0:main], full[0:main]), (dst_tile[main:LAST_P], full[main:LAST_P]),
                    (dst_tile[LAST_P:P, 0:LAST_E], rest)]

        with nc.Block() as block:
            @block.sync
            def _(sp):
                sp.wait_ge(padded, 2)
                for t, d in ((src_i, src), (dst_i, dst)):
                    for o, i in edge_parts(t, d, 1):
                        sp.dma_start(o, i).then_inc(loaded_ids, 16)
                sp.wait_ge(padded, 4)
                for o, i in edge_parts(attr_in, attr, ED):
                    sp.dma_start(o, i).then_inc(loaded_attr, 16)
                xv = x.rearrange("(t p) d -> p t d", p=BN)
                for a, b in node_parts():
                    sp.dma_start(keep["x"][a:b, :, :], xv[a:b, :, :]).then_inc(loaded_x, 16)
                sp.wait_ge(loaded_attr, 48)
                sp.wait_ge(loaded_x, 32)

            @block.scalar
            def _(act):
                act.dma_start(keep["ident"][:], eye).then_inc(loaded_const, 16)
                act.dma_start(keep["upper"][:], upper).then_inc(loaded_const, 16)
                act.dma_start(keep["wg"][:], w_gcn.rearrange("l i o -> i l o")).then_inc(loaded_const, 16)
                act.dma_start(keep["bg"][:], b_gcn.partition_broadcast(P)).then_inc(loaded_const, 16)
                act.wait_ge(pool_made, 2)
                main = table[0:TRASH, :].rearrange("(p t) c -> p t c", t=TT)
                for k in range(8):
                    act.dma_start(main[:, k * (TT // 8):(k + 1) * (TT // 8), :], pad[:]).then_inc(prefilled, 16)
                act.wait_ge(loaded_const, 64)
                nc.scalar.activation(keep["identb"][:], keep["ident"][:], ACT.Copy).then_inc(copied, 1)
                act.wait_ge(var_ready, 1)
                nc.scalar.activation(st[:, 2, :], st[:, 1, :], ACT.Sqrt).then_inc(std_ready, 1)
                act.wait_ge(prefilled, 8 * 16)

            @block.gpsimd
            def _(pool):
                ch = Chain(pool, psteps)
                nc.gpsimd.memset(keep["ones"][:], 1.0)
                nc.gpsimd.memset(gate[:], 1.0)
                nc.gpsimd.memset(keep["onesb"][:], 1.0)
                nc.gpsimd.iota(iota_b[:], [[1, NB]], base=0, channel_multiplier=0, allow_small_or_imprecise_dtypes=True)
                nc.gpsimd.iota(eidx[:], [[1, T]], base=0, channel_multiplier=T, allow_small_or_imprecise_dtypes=True)
                nc.gpsimd.iota(iota_g[:], [[1, NG]], base=0, channel_multiplier=0, allow_small_or_imprecise_dtypes=True)
                nc.gpsimd.iota(keep["iota"][:], [[1, WIN]], base=0, channel_multiplier=0,
                               allow_small_or_imprecise_dtypes=True).then_inc(pool_made, 1)
                ch.link(nc.gpsimd.memset(pad[:], 0.0))
                nc.gpsimd.memset(pad[:, :, 1:2], -1.0).then_inc(pool_made, 1)

            @block.tensor
            def _(pe):
                pe.wait_ge(loaded_const, 64)
                pe.wait_ge(pool_made, 1)
                pe.wait_ge(counted, 1)
                nc.tensor.matmul(ps_before[:], keep["upper"][:], cnt[:], start=True, stop=True)
                nc.tensor.matmul(ps_total[:], keep["ones"][:], cnt[:], start=True, stop=True).then_inc(prefixed, 1)

            @block.vector
            def _(v):
                ch = Chain(v, vsteps)
                nc.vector.memset(src_i[:, LAST_E:T], N).then_inc(padded, 1)
                nc.vector.memset(dst_i[:, LAST_E:T], N).then_inc(padded, 1)
                nc.vector.memset(attr_in[:, LAST_E:T, :], 0.0).then_inc(padded, 1)
                nc.vector.memset(keep["x"][96:P, :, :], 0.0).then_inc(padded, 1)
                nc.vector.memset(ends[:, 0:1], 0.0)
                v.wait_ge(loaded_ids, 96)
                nc.vector.tensor_scalar(int_a[:], src_i[:], float(DIV), None, ALU.mult)
                ch.link(nc.vector.tensor_scalar(int_b[:], dst_i[:], float(DIV), None, ALU.mult))
                nc.vector.tensor_scalar(int_a[:], int_a[:], SHIFT, None, ALU.logical_shift_right)
                ch.link(nc.vector.tensor_scalar(int_b[:], int_b[:], SHIFT, None, ALU.logical_shift_right))
                ch.link(nc.vector.tensor_copy(f_a[:], int_a[:]))
                nc.vector.scalar_tensor_tensor(lo_f[:], f_a[:], float(-BN), src_i[:], ALU.mult, ALU.add)
                nc.vector.tensor_copy(dst_bin[:], int_b[:])
                nc.vector.scalar_tensor_tensor(dst_lo[:], int_b[:], float(-BN), dst_i[:], ALU.mult, ALU.add)
                nc.vector.scalar_tensor_tensor(dst_f[:], int_b[:], float(P - BN), dst_i[:], ALU.mult, ALU.add)
                v.wait_ge(pool_made, 1)
                ch.link(nc.vector.tensor_tensor(hot[:], f_a[:].unsqueeze(1).to_broadcast([P, NB, T]),
                                                iota_b[:].unsqueeze(2).to_broadcast([P, NB, T]), ALU.is_equal))
                hot2, cum2 = (a[:].rearrange("p b t -> p (b t)") for a in (hot, cum))
                ch.link(nc.vector.tensor_tensor_scan(cum2, hot2, hot2, 0.0, ALU.add, ALU.max))
                ch.link(nc.vector.tensor_copy(ends[:, 1:NB + 1], cum[:, :, T - 1]))
                nc.vector.tensor_tensor(cnt[:], ends[:, 1:NB + 1], ends[:, 0:NB], ALU.subtract).then_inc(counted, 1)
                v.wait_ge(prefixed, 1)
                ch.link(nc.vector.tensor_scalar(tot_i[:], ps_total[:], float(PAIR - 1), None, ALU.add))
                ch.link(nc.vector.tensor_scalar(tot_i[:], tot_i[:], 8, None, ALU.logical_shift_right))
                ch.link(nc.vector.tensor_copy(pairs[:], tot_i[:]))
                ch.link(nc.vector.tensor_tensor_scan(endp[:], pairs[:], pairs[:], 0.0, ALU.add, ALU.max))
                ch.link(nc.vector.tensor_tensor(off[:], endp[:], pairs[:], ALU.subtract))
                ch.link(nc.vector.tensor_scalar(off[:], off[:], float(PAIR), -1.0, ALU.mult, ALU.add))
                ch.link(nc.vector.tensor_tensor(off[:], off[:], ends[:, 0:NB], ALU.subtract))
                ch.link(nc.vector.tensor_tensor(off[:], off[:], ps_before[:], ALU.add))
                ch.link(nc.vector.tensor_tensor(cum[:], cum[:], off[:].unsqueeze(2).to_broadcast([P, NB, T]), ALU.add))
                ch.link(nc.vector.tensor_tensor(cum[:], cum[:], hot[:], ALU.mult))
                ch.link(nc.vector.tensor_reduce(f_a[:], cum[:].rearrange("p b t -> p t b"), AX.X, ALU.add))
                ch.link(nc.vector.tensor_copy(int_a[:], f_a[:]))
                nc.vector.tensor_scalar(int_b[:], int_a[:], 7, None, ALU.logical_shift_right)
                ch.link(nc.vector.tensor_scalar(dst_i[:], int_a[:], P - 1, None, ALU.bitwise_and))
                nc.vector.tensor_copy(f_a[:], dst_i[:])
                ch.link(nc.vector.tensor_copy(f_b[:], int_b[:]))
                ch.link(nc.vector.scalar_tensor_tensor(f_a[:], f_a[:], float(TT), f_b[:], ALU.mult, ALU.add))
                ch.link(nc.vector.tensor_scalar(f_b[:], eidx[:], float(E), None, ALU.is_ge))
                ch.link(nc.vector.scalar_tensor_tensor(f_b[:], eidx[:], float(TRASH - E), f_b[:], ALU.add, ALU.mult))
                ch.link(nc.vector.tensor_tensor(f_a[:], f_a[:], f_b[:], ALU.add))
                ch.link(nc.vector.tensor_copy(row_i[:], f_a[:]))
                c0 = cum[0:1, :, :].rearrange("p b t -> p (b t)")[:, 0:NG * NB].rearrange("p (g b) -> p g b", b=NB)
                ch.link(nc.vector.tensor_tensor(c0, iota_g[:].unsqueeze(2).to_broadcast([1, NG, NB]),
                                                endp[0:1, :].unsqueeze(1).to_broadcast([1, NG, NB]), ALU.is_ge))
                ch.link(nc.vector.tensor_reduce(f_b[0:1, 0:NG], c0, AX.X, ALU.add))
                ch.link(nc.vector.tensor_scalar(keep["bin_row"][0:1, 0:NG], f_b[0:1, 0:NG], float(NB - 1), None, ALU.min))
                v.wait_ge(loaded_x, 32)
                layernorm_relu(nc, v, ch, keep["x"][:], keep["h"][:], tmp[:], sq[:], st, std_ready, var_ready)

    copied_ring = sem("ring_copied")
    gated = sem("gated")
    scattered = [sem(f"scattered{k}") for k in range(2)]
    split, lo_hots, lo_counted, deg_ready, root_ready, dsteps = (
        sem(x) for x in ("attr_split", "lo_hots", "lo_counted", "inv_deg_ready", "root_ready", "deg_vsteps"))
    rest = sb("attr_rest", [P, HALF, ED])
    bin_hot = sb("dst_bin_hot", [P, T, NB], BF16)
    lo_hot = sb("dst_lo_hot", [P, 2, HALF, P], BF16)
    ideg = sb("inv_deg", [P, NB])
    ps_deg = ctx.enter_context(nc.psum_tensor("ps_deg", [P, NB], F32))
    LOOPS = T // UN
    with nc.Block() as block:
        @block.vector
        def _(v):
            def half(i, k):
                t0 = i * UN + k * HALF
                if not known(i) or i >= 1:
                    v.wait_ge(scattered[k], i * (16 * HALF))
                ch = Chain(v, split, (i * 2 + k) * 3)
                bf = ring[:, k, :, 2:REC].bitcast(BF16).rearrange("p t (b c) -> p t b c", c=ED)
                a = attr_in[:, bass.ds(t0, HALF), :]

                def part(n):
                    bs = [b for b, x in enumerate(A_PART) if x == n]
                    return bf[:, :, bs[0]:bs[-1] + 1, :], [P, HALF, len(bs), ED]
                (p0, s0), (p1, s1), (p2, s2) = (part(n) for n in range(3))
                nc.vector.tensor_copy(ring_i[:, k, :], row_i[:, bass.ds(t0, HALF)])
                nc.vector.tensor_copy(ring[:, k, :, 0], dst_f[:, bass.ds(t0, HALF)])
                nc.vector.tensor_copy(ring[:, k, :, 1], lo_f[:, bass.ds(t0, HALF)])
                ch.link(nc.vector.tensor_copy(p0, a.unsqueeze(2).to_broadcast(s0)))
                ch.link(nc.vector.tensor_tensor(rest[:], a, p0[:, :, 0, :], ALU.subtract))
                ch.link(nc.vector.tensor_copy(p1, rest[:].unsqueeze(2).to_broadcast(s1)))
                nc.vector.tensor_tensor(p2, rest[:].unsqueeze(2).to_broadcast(s2), p1[:, :, 0:s2[2], :], ALU.subtract).then_inc(copied_ring, 1)
                if not known(i) or i >= 1:
                    v.wait_ge(lo_counted, i * 2 + k - 1)
                for t in range(HALF):
                    last = nc.vector.tensor_scalar(lo_hot[:, k, t, :], keep["iota"][:, 0:P], dst_lo[:, bass.ds(t0 + t, 1)], None, ALU.is_equal)
                last.then_inc(lo_hots, 1)
            ch = Chain(v, dsteps)
            ch.link(nc.vector.tensor_tensor(bin_hot[:], dst_bin[:].unsqueeze(2).to_broadcast([P, T, NB]),
                                            keep["iota"][:, 0:NB].unsqueeze(1).to_broadcast([P, T, NB]), ALU.is_equal))
            for k in range(2):
                half(0, k)
            with v.Fori(1, LOOPS) as i:
                for k in range(2):
                    half(i, k)
            v.wait_ge(lo_counted, 2 * LOOPS)
            ch.link(nc.vector.tensor_scalar(ideg[:], ps_deg[:], 1.0, None, ALU.add))
            nc.vector.reciprocal(ideg[:], ideg[:]).then_inc(deg_ready, 1)
            v.wait_ge(root_ready, 1)
            h = keep["h"]
            ch.link(nc.vector.tensor_tensor(h[:], h[:], keep["dinv"][:, 0:NB].unsqueeze(2).to_broadcast([P, NB, D]), ALU.mult))

        @block.scalar
        def _(act):
            act.wait_ge(deg_ready, 1)
            nc.scalar.activation(keep["dinv"][:, 0:NB], ideg[:], ACT.Sqrt).then_inc(root_ready, 1)

        @block.tensor
        def _(pe):
            def half(i, k):
                pe.wait_ge(lo_hots, i * 2 + k + 1)
                for t in range(HALF):
                    first = known(i) and i + k + t == 0
                    last = nc.tensor.matmul(ps_deg[:], lo_hot[:, k, t, :], bin_hot[:, bass.ds(i * UN + k * HALF + t, 1), :],
                                            start=first, stop=False, skip_group_check=True)
                last.then_inc(lo_counted, 1)
            for k in range(2):
                half(0, k)
            with pe.Fori(1, LOOPS) as i:
                for k in range(2):
                    half(i, k)

        @block.gpsimd
        def _(pool):
            def half(i, k):
                if not known(i) or 2 * i + k > 0:
                    pool.wait_ge(gated, i * 2 + k)
                pool.wait_ge(copied_ring, i * 2 + k + 1)
                nc.gpsimd.tensor_tensor(gate[:, 1:2], gate[:, 0:1], gate[:, 0:1], ALU.mult).then_inc(gated, 1)
                for j in range(HALF):
                    pool.indirect_dma_start(table[:, :], bass.IndirectOffsetOnAxis(ap=ring_i[:, k, j:j + 1], axis=0),
                                            ring[:, k, j, :], None).then_inc(scattered[k], 16)
            for k in range(2):
                half(0, k)
            with pool.Fori(1, LOOPS) as i:
                for k in range(2):
                    half(i, k)

        @block.sync
        def _(sp):
            for k in range(2):
                sp.wait_ge(scattered[k], 16 * HALF * LOOPS)
            if "table" in dbg:
                sp.dma_start(dbg["table"], table[0:TRASH, :]).then_inc(copied_ring, 16)
                sp.wait_ge(copied_ring, 16 + 2 * LOOPS)
            if "bin_row" in dbg:
                sp.dma_start(dbg["bin_row"], keep["bin_row"][0:1, 0:NG]).then_inc(copied_ring, 16)
                sp.dma_start(dbg["h"], keep["h"][:]).then_inc(copied_ring, 16)
                sp.wait_ge(copied_ring, 48+ 2 * LOOPS)


class Loads:

    def __init__(self, eng, name, top):
        self.eng, self.top = eng, top
        self.regs = [eng.alloc_register(f"{name}{k}") for k in range(4)]

    def __call__(self, row, at):
        self.eng.load(self.regs, row[0:1, bass.ds(at, 4)])
        return [self.eng.snap(r, min_val=0, max_val=self.top) for r in self.regs]


LEAD = 4


def adjacency_and_gcn(nc, ctx, keep, table, dbg):
    def sb(name, shape, dt=F32):
        return ctx.enter_context(nc.sbuf_tensor(name, shape, dt))

    adj = sb("adjacency", [P, ACOLS], BF16)
    edges = ExitStack()
    dst_s = edges.enter_context(nc.sbuf_tensor("dst_sorted", [P, NG, 2], F32))
    rel_s = edges.enter_context(nc.sbuf_tensor("dst_in_window", [P, NG, 2], F32))
    lo_s = edges.enter_context(nc.sbuf_tensor("lo_sorted", [P, NG, 2], F32))
    win_i = edges.enter_context(nc.sbuf_tensor("window_at", [1, NG + 8], I32))
    bin_i = edges.enter_context(nc.sbuf_tensor("bin_at", [1, NG + 8], I32))
    flag_i = edges.enter_context(nc.sbuf_tensor("wide_flag", [1, 1], I32))

    HG = NG // 2
    with ExitStack() as c1:
        def sb1(name, shape, dt=F32):
            return c1.enter_context(nc.sbuf_tensor(name, shape, dt))

        def sem1(name):
            return c1.enter_context(nc.semaphore(name))

        rec = adj[:, 0:2 * TT * REC].bitcast(F32).rearrange("p (t c) -> p t c", c=REC)
        low = sb1("low", [P, NG, 2])
        ext = sb1("extremes", [P, 2, NG])
        mm = sb1("pair_extremes", [P, 4])
        row = sb1("extreme_rows", [1, 4, HG])
        w0 = sb1("window_start", [1, NG])
        w_i = sb1("window_start_i", [1, NG], I32)
        tmp = sb1("row_tmp", [1, NG])
        flag = sb1("flag_f", [1, 1])
        ps_t = c1.enter_context(nc.psum_tensor("ps_extremes", [P, 4, P], F32))
        ps_row = c1.enter_context(nc.psum_tensor("ps_rows", [1, 4, HG], F32))
        ps_w = c1.enter_context(nc.psum_tensor("ps_window", [P, NG], F32))
        CH = 4
        TC = TT // CH
        loaded = [sem1(f"records_loaded{k}") for k in range(CH)]
        vsteps = sem1("stat_vsteps")
        to_pe = sem1("stat_to_pe")
        from_pe = sem1("stat_from_pe")
        with nc.Block() as block:
            @block.sync
            def _(sp):
                tv = table[0:TRASH, :].rearrange("(p t) c -> p t c", t=TT)
                for k in range(CH):
                    sp.dma_start(rec[:, k * TC:(k + 1) * TC, :], tv[:, k * TC:(k + 1) * TC, :]).then_inc(loaded[k], 16)
                for k in range(CH):
                    sp.wait_ge(loaded[k], 16)

            @block.tensor
            def _(pe):
                pe.wait_ge(to_pe, 1)
                for q in range(4):
                    last = nc.tensor.transpose(ps_t[0:HG, q, :], ext[:, q // 2, (q % 2) * HG:(q % 2 + 1) * HG], keep["ident"][:])
                last.then_inc(from_pe, 1)
                pe.wait_ge(to_pe, 2)
                for q in range(4):
                    last = nc.tensor.matmul(ps_row[0:1, q, :], mm[0:HG, q:q + 1], keep["ident"][0:HG, 0:HG], start=True, stop=True)
                last.then_inc(from_pe, 1)
                pe.wait_ge(to_pe, 3)
                nc.tensor.matmul(ps_w[:], keep["ones"][0:1, :], w0[:], start=True, stop=True).then_inc(from_pe, 1)

            @block.vector
            def _(v):
                ch = Chain(v, vsteps)
                nc.vector.memset(win_i[:], 0)
                nc.vector.memset(bin_i[:], 0)
                rec2 = rec.rearrange("p (g j) c -> p g j c", j=2)
                for k in range(CH):
                    v.wait_ge(loaded[k], 16)
                    gs = slice(k * TC // 2, (k + 1) * TC // 2)
                    ch.link(nc.vector.tensor_copy(dst_s[:, gs, :], rec2[:, gs, :, 0]))
                    ch.link(nc.vector.tensor_copy(lo_s[:, gs, :], rec2[:, gs, :, 1]))
                ch.link(nc.vector.tensor_scalar(low[:], lo_s[:], 0.0, 4096.0, ALU.is_lt, ALU.mult))
                ch.link(nc.vector.tensor_tensor(low[:], low[:], dst_s[:], ALU.add))
                nc.vector.tensor_reduce(ext[:, 0, :], low[:], AX.X, ALU.min)
                nc.vector.tensor_reduce(ext[:, 1, :], dst_s[:], AX.X, ALU.max).then_inc(to_pe, 1)
                v.wait_ge(from_pe, 1)
                nc.vector.tensor_reduce(mm[0:HG, 0:2], ps_t[0:HG, 0:2, :], AX.X, ALU.min)
                nc.vector.tensor_reduce(mm[0:HG, 2:4], ps_t[0:HG, 2:4, :], AX.X, ALU.max).then_inc(to_pe, 1)
                v.wait_ge(from_pe, 2)
                ch.link(nc.vector.tensor_copy(row[:], ps_row[:]))
                least, most = (row[0:1, 2 * k:2 * k + 2, :].rearrange("p a g -> p (a g)") for k in range(2))
                ch.link(nc.vector.tensor_scalar(w_i[:], least, float(NB * P - 1), None, ALU.min))
                ch.link(nc.vector.tensor_scalar(w_i[:], w_i[:], -2, None, ALU.bitwise_and))
                nc.vector.tensor_copy(w0[:], w_i[:]).then_inc(to_pe, 1)
                v.wait_ge(to_pe, 3)
                nc.vector.tensor_scalar(bin_i[0:1, LEAD:LEAD + NG], keep["bin_row"][0:1, 0:NG], float(AC), None, ALU.mult)
                ch.link(nc.vector.scalar_tensor_tensor(win_i[0:1, LEAD:LEAD + NG], keep["bin_row"][0:1, 0:NG], float(AC), w0[:], ALU.mult, ALU.add))
                ch.link(nc.vector.tensor_tensor(tmp[:], most, w0[:], ALU.subtract))
                ch.link(nc.vector.tensor_reduce(flag[:], tmp[:], AX.X, ALU.max))
                ch.link(nc.vector.tensor_scalar(flag_i[:], flag[:], float(WIN), None, ALU.is_ge))
                v.wait_ge(from_pe, 3)
                ch.link(nc.vector.tensor_tensor(rel_s[:], dst_s[:], ps_w[:].unsqueeze(2).to_broadcast([P, NG, 2]), ALU.subtract))

    with ExitStack() as c2:
        def sb2(name, shape, dt=F32):
            return c2.enter_context(nc.sbuf_tensor(name, shape, dt))

        def sem2(name):
            return c2.enter_context(nc.semaphore(name))

        R = 2
        src_hot = sb2("src_hot", [P, R, 2, P], BF16)
        dst_hot = sb2("dst_hot", [P, R, 2, WIN], BF16)
        far = sb2("far_dst", [P, NG, 2])
        far2 = sb2("far_mask", [P, NG, 2])
        ps = [c2.enter_context(nc.psum_tensor(f"ps_counts{k}", [P, WIN], F32)) for k in range(R)]
        cleared = sem2("adj_cleared")
        hots = sem2("hots_ready")
        counted = sem2("pair_counted")
        added = sem2("pair_added")
        far_hots, far_counted, far_added = sem2("far_hots"), sem2("far_counted"), sem2("far_added")
        vsteps = sem2("adj_vsteps")

        with nc.Block() as block:
            CUT = 26 * 1024
            words = adj[:].bitcast(F32)

            @block.gpsimd
            def _(pool):
                nc.gpsimd.memset(words[:, CUT:], 0.0).then_inc(cleared, 1)

            def hot(v, g, u, target):
                for j in range(2):
                    nc.vector.tensor_scalar(src_hot[:, u, j, :], keep["iota"][:, 0:P], lo_s[:, bass.ds(g, 1), j], None, ALU.is_equal)
                    last = nc.vector.tensor_scalar(dst_hot[:, u, j, :], keep["iota"][:], target[:, bass.ds(g, 1), j], None, ALU.is_equal)
                return last

            def count(u):
                for j in range(2):
                    last = nc.tensor.matmul(ps[u][:], src_hot[:, u, j, :], dst_hot[:, u, j, :], start=(j == 0), stop=(j == 1))
                return last

            @block.vector
            def _(v):
                ch = Chain(v, vsteps)
                ch.link(nc.vector.memset(words[:, 0:CUT], 0.0))
                v.wait_ge(cleared, 1)
                step = AC + P
                diag = adj[:, 0:(NB - 1) * step].rearrange("p (b c) -> p b c", c=step)[:, :, 0:P]
                ch.link(nc.vector.tensor_copy(diag, keep["identb"][:].unsqueeze(1).to_broadcast([P, NB - 1, P])))
                ch.link(nc.vector.tensor_copy(adj[:, (NB - 1) * step:(NB - 1) * step + P], keep["identb"][:]))
                load = Loads(v, "window", ACOLS - WIN)
                at = [None]

                def one(i, u, live):
                    if u == 0:
                        at[0] = load(win_i, i + LEAD - 1)
                    if live(0):
                        if not known(i) or i >= R:
                            v.wait_ge(counted, i - R + 1)
                        hot(v, i, u % R, rel_s).then_inc(hots, 1)
                    if live(1):
                        v.wait_ge(counted, i)
                        if not known(i) or i >= 2:
                            v.wait_ge(added, i - 1)
                        win = adj[:, bass.ds(at[0][u], WIN)]
                        nc.vector.tensor_tensor(win, win, ps[(u + 1) % R][:], ALU.add).then_inc(added, 1)
                run_steps(v, NG, 1, 4, one)
                v.wait_ge(added, NG)

            @block.tensor
            def _(pe):
                def one(i, u, live):
                    if live(0):
                        pe.wait_ge(hots, i + 1)
                        if not known(i) or i >= R:
                            pe.wait_ge(added, i - R + 1)
                        count(u % R).then_inc(counted, 1)
                run_steps(pe, NG, 0, 4, one)

        with nc.Block() as block:
            @block.vector
            def _(v):
                ch = Chain(v, vsteps, 3)
                wide = v.value_load(flag_i[0:1, 0:1], min_val=0, max_val=1)
                with v.If(wide != 0):
                    load = v.alloc_register("bin_column")
                    ch.link(nc.vector.tensor_scalar(far2[:], rel_s[:], float(WIN), None, ALU.is_ge))
                    ch.link(nc.vector.scalar_tensor_tensor(far[:], dst_s[:], 1.0, far2[:], ALU.add, ALU.mult))
                    ch.link(nc.vector.tensor_scalar(far[:], far[:], -1.0, None, ALU.add))
                    with v.Fori(0, 7) as k:
                        with v.Fori(0, NG) as g:
                            v.load(load, bin_i[0:1, bass.ds(g + LEAD, 1)])
                            col = v.snap(load, min_val=0, max_val=(NB - 1) * AC)
                            hot(v, g, 0, far).then_inc(far_hots, 1)
                            v.wait_ge(far_counted, k * NG + g + 1)
                            win = adj[:, bass.ds(col + k * WIN, WIN)]
                            nc.vector.tensor_tensor(win, win, ps[0][:], ALU.add).then_inc(far_added, 1)
                            v.wait_ge(far_added, k * NG + g + 1)
                        nc.vector.tensor_scalar(far[:], far[:], float(-WIN), None, ALU.add).then_inc(far_hots, 1)
                        v.wait_ge(far_hots, (k + 1) * (NG + 1))

            @block.tensor
            def _(pe):
                wide = pe.value_load(flag_i[0:1, 0:1], min_val=0, max_val=1)
                with pe.If(wide != 0):
                    with pe.Fori(0, 7) as k:
                        with pe.Fori(0, NG) as g:
                            pe.wait_ge(far_hots, k * (NG + 1) + g + 1)
                            count(0).then_inc(far_counted, 1)

            if "A" in dbg:
                @block.sync
                def _(sp):
                    wide = sp.value_load(flag_i[0:1, 0:1], min_val=0, max_val=1)
                    with sp.If(wide != 0):
                        sp.wait_ge(far_added, 7 * NG)
                    sp.dma_start(dbg["A"], adj[:]).then_inc(cleared, 16)
                    sp.dma_start(dbg["flag"], flag_i[:]).then_inc(cleared, 16)
                    sp.wait_ge(cleared, 33)
    edges.close()

    h3 = [sb(f"h_parts{k}", [P, NB, 3, D], BF16) for k in range(2)]
    with nc.semaphore("split_vsteps") as vsteps, nc.Block() as block:
        @block.vector
        def _(v):
            ch = Chain(v, vsteps)
            h = keep["h"]
            ch.link(nc.vector.tensor_copy(h3[0][:, :, 0, :], h[:]))
            ch.link(nc.vector.tensor_tensor(h[:], h[:], h3[0][:, :, 0, :], ALU.subtract))
            ch.link(nc.vector.tensor_copy(h3[0][:, :, 1, :], h[:]))
            ch.link(nc.vector.tensor_tensor(h3[0][:, :, 2, :], h[:], h3[0][:, :, 1, :], ALU.subtract))

    for layer in range(3):
        with ExitStack() as c4:
            gcn_layer(nc, c4, keep, adj, h3[layer % 2], h3[(layer + 1) % 2], layer)
    if "x1" in dbg:
        with nc.semaphore("dbg_x1") as s, nc.Block() as block:
            @block.sync
            def _(sp):
                sp.dma_start(dbg["x1"], keep["x"][:]).then_inc(s, 16)
                sp.wait_ge(s, 16)


def gcn_layer(nc, ctx, keep, adj, h3, h3_next, layer):
    def sb(name, shape, dt=F32):
        return ctx.enter_context(nc.sbuf_tensor(f"{name}_{layer}", shape, dt))

    def sem(name):
        return ctx.enter_context(nc.semaphore(f"{name}_{layer}"))

    def psum(name, shape):
        return [ctx.enter_context(nc.psum_tensor(f"{name}{k}_{layer}", shape, F32)) for k in range(2)]

    agg = sb("agg", [P, 2, P])
    agg_t = sb("agg_t", [D, 2, P])
    res = sb("res", [P, 2, D])
    ps_agg, ps_t, ps_o = psum("ps_agg", [P, 3, D]), psum("ps_aggt", [P, P]), psum("ps_out", [P, D])
    gathered, summed, turned, turned_c, multiplied, finished = (
        sem(x) for x in ("gathered", "summed", "turned", "turned_copied", "multiplied", "finished"))
    vsteps, zeroed = sem("layer_vsteps"), sem("agg_zeroed")
    last_layer = layer == 2

    with nc.Block() as block:
        @block.tensor
        def _(pe):
            def one(i, u, live):
                if live(0):
                    if not known(i) or i >= 2:
                        pe.wait_ge(summed, i - 1)
                    for k in range(NB):
                        last = nc.tensor.matmul(ps_agg[u][:], adj[:, bass.ds(i * P + k * AC, P)], h3[:, k, :, :],
                                                start=(k == 0), stop=(k == NB - 1))
                    last.then_inc(gathered, 1)
                if live(1):
                    pe.wait_ge(summed, i)
                    if not known(i) or i >= 3:
                        pe.wait_ge(turned_c, i - 2)
                    nc.tensor.transpose(ps_t[1 - u][:], agg[:, 1 - u, :], keep["ident"][:]).then_inc(turned, 1)
                if live(2):
                    pe.wait_ge(turned_c, i - 1)
                    if not known(i) or i >= 4:
                        pe.wait_ge(finished, i - 3)
                    nc.tensor.matmul(ps_o[u][:], agg_t[:, u, :], keep["wg"][:, layer, :], start=True, stop=True).then_inc(multiplied, 1)
            run_steps(pe, NB, 2, 2, one)

        @block.scalar
        def _(act):
            def one(i, u, live):
                if live(0):
                    act.wait_ge(turned, i + 1)
                    if not known(i) or i >= 2:
                        act.wait_ge(multiplied, i - 1)
                    nc.scalar.activation(agg_t[:, u, :], ps_t[u][0:D, :], ACT.Copy).then_inc(turned_c, 1)
            run_steps(act, NB, 0, 2, one)

        @block.vector
        def _(v):
            ch = Chain(v, vsteps)
            nc.vector.memset(agg[:], 0.0).then_inc(zeroed, 1)
            v.wait_ge(zeroed, 1)

            def one(i, u, live):
                if live(0):
                    v.wait_ge(gathered, i + 1)
                    if not known(i) or i >= 2:
                        v.wait_ge(turned, i - 1)
                    nc.vector.tensor_reduce(agg[:, u, 0:D], ps_agg[u][:].rearrange("p s d -> p d s"), AX.X, ALU.add).then_inc(summed, 1)
                if live(2):
                    m = i - 2
                    dinv = keep["dinv"][:, bass.ds(m, 1)]
                    v.wait_ge(multiplied, i - 1)
                    ch.step(m, 2 if last_layer else 6)
                    r = res[:, u, :]
                    ch.link(nc.vector.scalar_tensor_tensor(r, ps_o[u][:], dinv, keep["bg"][:, layer, :], ALU.mult, ALU.add))
                    if last_layer:
                        xm = keep["x"][:, bass.ds(m, 1), :]
                        ch.link(nc.vector.tensor_tensor(xm, xm, res[:, u:u + 1, :], ALU.add))
                        nc.vector.memset(res[0:1, u, 0:1], 0.0).then_inc(finished, 1)
                    else:
                        part = [h3_next[:, bass.ds(m, 1), k, :] for k in range(3)]
                        r3 = res[:, u:u + 1, :]
                        ch.link(nc.vector.tensor_scalar(r, r, 0.0, dinv, ALU.max, ALU.mult))
                        ch.link(nc.vector.tensor_copy(part[0], r3))
                        ch.link(nc.vector.tensor_tensor(r3, r3, part[0], ALU.subtract))
                        ch.link(nc.vector.tensor_copy(part[1], r3))
                        ch.link(nc.vector.tensor_tensor(part[2], r3, part[1], ALU.subtract))
                        nc.vector.memset(res[0:1, u, 0:1], 0.0).then_inc(finished, 1)
                    ch.end()
            run_steps(v, NB, 2, 2, one)


class Bins:

    def __init__(self, eng, count):
        self.eng = eng
        self.regs = [eng.alloc_register(f"bin{k}") for k in range(count)]

    def __call__(self, row, at):
        self.eng.load(self.regs, row[0:1, bass.ds(at, len(self.regs))])
        return [self.eng.snap(r, min_val=0, max_val=NB - 1) for r in self.regs]


def attention(nc, ctx, keep, table, qtable, w_att1t, b_att1, w_att2, b_att2, w_lint, b_lin,
              w_iht, b_ih, w_hht, b_hh, part_mask, out, dbg):
    def sb(name, shape, dt=F32):
        return ctx.enter_context(nc.sbuf_tensor(name, shape, dt))

    p3 = sb("source_parts", [P, NB, 3, HW], BF16)
    gi = sb("gates_in", [P, NB, 3 * D])
    w_edge = sb("w_edge", [P, HW], BF16)
    w2 = sb("w_att2_sb", [P, HW])
    w_hh = sb("w_hh_sb", [D + 1, 3 * D])
    acc = sb("acc", [P, NB, D + 1])
    with ExitStack() as c1:
        node_tables(nc, c1, keep, p3, gi, w_edge, w2, w_hh, qtable, w_att1t, b_att1, w_att2, b_att2,
                    w_lint, b_lin, w_iht, b_ih, w_hht, b_hh, part_mask)
    with ExitStack() as c2:
        edge_attention(nc, c2, keep, p3, w_edge, w2, acc, table, qtable)
    with ExitStack() as c3:
        gru(nc, c3, keep, gi, w_hh, acc, out)


def node_tables(nc, ctx, keep, p3, gi, w_edge, w2, w_hh, qtable, w_att1t, b_att1, w_att2, b_att2,
                w_lint, b_lin, w_iht, b_ih, w_hht, b_hh, part_mask):
    def sb(name, shape, dt=F32):
        return ctx.enter_context(nc.sbuf_tensor(name, shape, dt))

    def sem(name):
        return ctx.enter_context(nc.semaphore(name))

    A1, G1 = 0, HW
    Q1, ONE, L1 = HW + 3 * D, 2 * H1 + 1 + 3 * D, 2 * HW + 3 * D
    w_node = sb("w_node", [D + 1, L1 + D])
    ql = sb("target_values", [P, NB, QL])
    tmp, sq, st = sb("ln_tmp2", [P, NB, D]), sb("ln_sq2", [P, NB, D]), sb("ln_stats2", [P, 4, NB])
    tile = sb("h_tile", [P, 2, P])
    h_t = sb("h_turned", [D + 1, 2, P])
    rest = sb("p_rest", [P, 2, HW])
    we, we_r, we_p, mask = sb("w_edge_f", [P, HW]), sb("w_edge_rest", [P, HW]), sb("w_edge_p", [P, 3, HW], BF16), sb("part_mask_sb", [P, 3])
    ps_t = [ctx.enter_context(nc.psum_tensor(f"ps_ht{k}", [P, P], F32)) for k in range(2)]
    ps_a = [ctx.enter_context(nc.psum_tensor(f"ps_source{k}", [P, HW], F32)) for k in range(2)]
    ps_q = [ctx.enter_context(nc.psum_tensor(f"ps_target{k}", [P, 3 * D + QL], F32)) for k in range(2)]
    weights, zeroed, normed, var_r, std_r, vsteps = (
        sem(x) for x in ("node_weights", "node_zeroed", "node_normed", "var_ready2", "std_ready2", "node_vsteps"))
    tiled, turned, turned_c, made, kept_a, kept_p, stored = (
        sem(x) for x in ("tiled", "h_turned_ready", "h_turned_copied", "made", "kept_act", "kept_parts", "stored"))
    loads = [(w_node[0:D, A1:A1 + H1], w_att1t[0:D, :]), (w_node[0:D, G1:G1 + 3 * D], w_iht),
             (w_node[0:D, Q1:Q1 + H1], w_att1t[D + ED:H1, :]), (w_node[0:D, L1:L1 + D], w_lint),
             (w_node[D:D + 1, A1:A1 + H1], b_att1.unsqueeze(0)),
             (w_node[D:D + 1, G1:G1 + 3 * D], b_ih.unsqueeze(0)),
             (w_node[D:D + 1, L1:L1 + D], b_lin.unsqueeze(0)),
             *((we[k * ED:(k + 1) * ED, 0:H1], w_att1t[D:D + ED, :]) for k in range(len(W_PART))),
             (mask[:], part_mask), (w2[:, 0:H1], w_att2[0, :].partition_broadcast(P)),
             (w2[:, H1:HW], b_att2.partition_broadcast(P)),
             (w_hh[0:D, :], w_hht), (w_hh[D:D + 1, :], b_hh.unsqueeze(0))]
    NW = len(loads)

    with nc.Block() as block:
        @block.gpsimd
        def _(pool):
            nc.gpsimd.memset(tile[:], 0.0).then_inc(zeroed, 1)

        @block.sync
        def _(sp):
            sp.wait_ge(zeroed, 2)
            for o, i in loads:
                sp.dma_start(o, i).then_inc(weights, 16)
            sp.wait_ge(kept_a, NB)
            sp.dma_start(qtable.rearrange("(t p) c -> p t c", p=P), ql[:]).then_inc(stored, 16)
            sp.wait_ge(stored, 16)
            sp.wait_ge(weights, 16 * NW)

        @block.scalar
        def _(act):
            act.wait_ge(var_r, 1)
            nc.scalar.activation(st[:, 2, :], st[:, 1, :], ACT.Sqrt).then_inc(std_r, 1)
            act.wait_ge(normed, 1)
            act.wait_ge(zeroed, 2)

            def one(i, u, live):
                if live(0):
                    if not known(i) or i >= 2:
                        act.wait_ge(turned, i - 1)
                    nc.scalar.activation(tile[:, u:u + 1, 0:D], keep["h"][:, bass.ds(i, 1), :], ACT.Copy).then_inc(tiled, 1)
                if live(1):
                    act.wait_ge(turned, i)
                    if not known(i) or i >= 3:
                        act.wait_ge(made, i - 2)
                    nc.scalar.activation(h_t[0:D, 1 - u, :], ps_t[1 - u][0:D, :], ACT.Copy).then_inc(turned_c, 1)
                if live(2):
                    m = i - 2
                    act.wait_ge(made, i - 1)
                    nc.scalar.activation(gi[:, bass.ds(m, 1), :], ps_q[u][:, 0:3 * D].unsqueeze(1), ACT.Copy)
                    nc.scalar.activation(ql[:, bass.ds(m, 1), :], ps_q[u][:, 3 * D:].unsqueeze(1), ACT.Copy).then_inc(kept_a, 1)
            run_steps(act, NB, 2, 2, one)

        @block.tensor
        def _(pe):
            pe.wait_ge(weights, 16 * NW)
            pe.wait_ge(zeroed, 2)

            def one(i, u, live):
                if live(0):
                    pe.wait_ge(tiled, i + 1)
                    if not known(i) or i >= 2:
                        pe.wait_ge(turned_c, i - 1)
                    nc.tensor.transpose(ps_t[u][:], tile[:, u, :], keep["ident"][:]).then_inc(turned, 1)
                if live(1):
                    pe.wait_ge(turned_c, i)
                    if not known(i) or i >= 3:
                        pe.wait_ge(kept_a, i - 2)
                        pe.wait_ge(kept_p, i - 2)
                    v = 1 - u
                    nc.tensor.matmul(ps_a[v][:], h_t[:, v, :], w_node[:, 0:HW], start=True, stop=True)
                    nc.tensor.matmul(ps_q[v][:], h_t[:, v, :], w_node[:, HW:L1 + D], start=True, stop=True).then_inc(made, 1)
            run_steps(pe, NB, 1, 2, one)

        @block.vector
        def _(v):
            ch = Chain(v, vsteps)
            ch.link(nc.vector.memset(w_node[:], 0.0))
            nc.vector.memset(we[:, H1:HW], 0.0)
            ch.link(nc.vector.memset(h_t[D:D + 1, :, :], 1.0))
            nc.vector.memset(w_node[D:D + 1, ONE:ONE + 1], 1.0).then_inc(zeroed, 1)
            layernorm_relu(nc, v, ch, keep["x"][:], keep["h"][:], tmp[:], sq[:], st, std_r, var_r)
            nc.vector.memset(st[0:1, 0, 0:1], 0.0).then_inc(normed, 1)
            v.wait_ge(weights, 16 * NW)
            ch.link(nc.vector.tensor_copy(we_p[:, 0, :], we[:]))
            ch.link(nc.vector.tensor_tensor(we_r[:], we[:], we_p[:, 0, :], ALU.subtract))
            ch.link(nc.vector.tensor_copy(we_p[:, 1, :], we_r[:]))
            ch.link(nc.vector.tensor_tensor(we_p[:, 2, :], we_r[:], we_p[:, 1, :], ALU.subtract))
            ch.link(nc.vector.tensor_scalar(we[:], we_p[:, 0, :], mask[:, 0:1], None, ALU.mult))
            ch.link(nc.vector.scalar_tensor_tensor(we[:], we_p[:, 1, :], mask[:, 1:2], we[:], ALU.mult, ALU.add))
            ch.link(nc.vector.scalar_tensor_tensor(w_edge[:], we_p[:, 2, :], mask[:, 2:3], we[:], ALU.mult, ALU.add))
            before = ch.n
            ch.step(0, 3)

            def one(i, u, live):
                if live(0):
                    v.wait_ge(made, i + 1)
                    ch.base, ch.n = before + i * 3, 0
                    part = [p3[:, bass.ds(i, 1), k, :] for k in range(3)]
                    r = rest[:, u:u + 1, :]
                    ps = ps_a[u][:].unsqueeze(1)
                    ch.link(nc.vector.tensor_scalar(part[0], ps, 1.0, None, ALU.mult))
                    ch.link(nc.vector.tensor_tensor(r, ps, part[0], ALU.subtract))
                    ch.link(nc.vector.tensor_copy(part[1], r))
                    nc.vector.tensor_tensor(part[2], r, part[1], ALU.subtract).then_inc(kept_p, 1)
                    ch.end()
            run_steps(v, NB, 0, 2, one)


def edge_attention(nc, ctx, keep, p3, w_edge, w2, acc, table, qtable):
    def sb(name, shape, dt=F32):
        return ctx.enter_context(nc.sbuf_tensor(name, shape, dt))

    def sem(name):
        return ctx.enter_context(nc.semaphore(name))

    def psum(name, shape, dt=F32, n=2):
        return [ctx.enter_context(nc.psum_tensor(f"{name}{k}", shape, dt)) for k in range(n)]

    U = 8
    GR = 4
    AHEAD = 16
    bin_i = sb("bin_at2", [1, NG + 3 * AHEAD], I32)
    rec = sb("rec_ring", [P, 2 * U, REC])
    idx = sb("idx_ring", [P, 2 * U], I32)
    rows = sb("row_ring2", [P, 2 * U, QL])
    gate = sb("gate2", [1, 2])
    hot = sb("hot", [P, 8, 2, P], BF16)
    hot32 = sb("hot32", [P, 4, 2, P])
    neg = sb("neg", [P, 4, 2, P], BF16)
    turn = sb("turn", [P, 8, 4, P], BF16)
    hid = sb("hidden_sum", [P, 2, HW])
    junk = sb("hidden_relu", [P, 2, 2, HW])
    score = sb("score", [P, 8, 2])
    by_src = sb("by_src", [P, 2, 2, P])
    mx = sb("mx", [P, 4])
    mx2 = sb("mx2", [P, 4])
    parts = sb("top_parts", [P, 4, 2], BF16)
    new = sb("top_new", [P, 4])
    rise = sb("top_rise", [P, 4])
    scale = sb("scale", [P, 4])
    arg = sb("arg", [P, 4, 2])
    ew = sb("edge_weight", [P, 4, 2])
    val = sb("weighted", [P, 2, 2, D + 1])
    top = sb("top", [P, NB])

    ps_turn = psum("ps_turn", [P, 4, P], BF16)
    ps_hid = psum("ps_hid", [P, 2, HW])
    ps_src = psum("ps_src", [P, 2, P])
    ps_top = psum("ps_top", [P, 2], n=1)[0]
    ps_sum = psum("ps_sum", [P, D + 1], n=1)[0]

    ready, setup, idx_ready, gated = (sem(x) for x in ("att_ready", "att_setup", "idx_ready", "gated2"))
    rec_in = [sem(f"rec_in{k}") for k in range(2)]
    gathered = [sem(f"gathered{k}") for k in range(U)]
    (hots, turned, turned_c, negated, hidden, added, scored, laid, by_source, topped, top_back, floated, args,
     weighed, valued, aggregated, summed) = (
        sem(x) for x in ("hots2", "turned2", "turned_c2", "negated", "hidden", "hid_added", "scored", "laid", "by_source",
                         "topped", "top_back", "floated", "args", "weighed", "valued", "aggregated", "summed2"))
    c_top = sem("c_top")

    def done(eng, sem, i, back):
        if not known(i) or i >= back:
            eng.wait_ge(sem, i - back + 1)

    tview = table[0:TRASH, :].rearrange("(p t) c -> p t c", t=TT)

    with nc.Block() as block:
        @block.sync
        def _(sp):
            def one(i, u, live):
                if u % GR == 0:
                    h = u // GR
                    if not known(i) or i >= U:
                        sp.wait_ge(turned, i - U + GR)
                        sp.wait_ge(hots, i - U + GR)
                        sp.wait_ge(idx_ready, i - U + GR)
                    sp.dma_start(rec[:, 2 * GR * h:2 * GR * (h + 1), :], tview[:, bass.ds(i * 2, 2 * GR), :]).then_inc(rec_in[h], 16)
            run_steps(sp, NG, 0, U, one)
            for h in range(2):
                sp.wait_ge(rec_in[h], 16 * (NG // U))

        @block.gpsimd
        def _(pool):
            pool.wait_ge(ready, 1)

            def one(i, u, live):
                done(pool, gated, i, 1)
                done(pool, valued, i, U)
                pool.wait_ge(idx_ready, i - u % GR + GR)
                nc.gpsimd.tensor_tensor(gate[:, 1:2], gate[:, 0:1], gate[:, 0:1], ALU.mult).then_inc(gated, 1)
                for t in (2 * u, 2 * u + 1):
                    pool.indirect_dma_start(rows[:, t, :], None, qtable[:, :],
                                            bass.IndirectOffsetOnAxis(ap=idx[:, t:t + 1], axis=0)).then_inc(gathered[u], 16)
            run_steps(pool, NG, 0, U, one)

        @block.tensor
        def _(pe):
            pe.wait_ge(ready, 1)
            bins = Bins(pe, U)
            at = [None]

            def one(i, u, live):
                if u == 0:
                    at[0] = bins(bin_i, i + AHEAD - 2)
                if live(1):
                    w = (u - 1) % U
                    done(pe, hots, i, 1)
                    done(pe, turned_c, i, 3)
                    for j in range(2):
                        nc.tensor.transpose(ps_turn[w % 2][:, j, :], hot[:, w, j, :], keep["identb"][:])
                    for j in range(2):
                        last = nc.tensor.transpose(ps_turn[w % 2][:, 2 + j, :], rec[:, 2 * w + j, 2:REC].bitcast(BF16), keep["identb"][:])
                    last.then_inc(turned, 1)
                if live(2):
                    w = (u - 2) % U
                    done(pe, turned_c, i, 2)
                    done(pe, added, i, 4)
                    for j in range(2):
                        for k in SPLIT3:
                            nc.tensor.matmul(ps_hid[w % 2][:, j, :], turn[:, w, j, :], p3[:, bass.ds(at[0][u], 1), k, :],
                                             start=(k == 0), stop=False)
                        last = nc.tensor.matmul(ps_hid[w % 2][:, j, :], turn[:, w, 2 + j, :], w_edge[:], start=False, stop=True)
                    last.then_inc(hidden, 1)
                if live(4):
                    w = (u - 4) % U
                    done(pe, laid, i, 4)
                    done(pe, topped, i, 6)
                    for j in range(2):
                        last = nc.tensor.transpose(ps_src[w % 2][:, j, :], by_src[:, w % 2, j, :], keep["ident"][:])
                    last.then_inc(by_source, 1)
                if live(6):
                    w = (u - 6) % U
                    done(pe, topped, i, 6)
                    done(pe, args, i, 7)
                    for j in range(2):
                        for k in range(2):
                            last = nc.tensor.matmul(ps_top[:, j:j + 1], turn[:, w, j, :], parts[:, w % 4, k:k + 1],
                                                    start=(k == 0), stop=(k == 1))
                    last.then_inc(top_back, 1)
                if live(9):
                    w = (u - 9) % U
                    done(pe, valued, i, 9)
                    done(pe, floated, i, 9)
                    done(pe, summed, i, 10)
                    for j in range(2):
                        last = nc.tensor.matmul(ps_sum[:], hot32[:, w % 4, j, :], val[:, w % 2, j, :],
                                                start=(j == 0), stop=(j == 1))
                    last.then_inc(aggregated, 1)
            run_steps(pe, NG, 9, U, one)

        @block.scalar
        def _(act):
            act.wait_ge(ready, 1)

            def one(i, u, live):
                if live(1):
                    w = (u - 1) % U
                    done(act, hots, i, 1)
                    done(act, laid, i, 5)
                    nc.scalar.activation(neg[:, w % 4, :, :], hot[:, w, :, :], ACT.Copy, bias=-BIG, scale=BIG).then_inc(negated, 1)
                if live(6):
                    w = (u - 6) % U
                    done(act, aggregated, i, 10)
                    nc.scalar.activation(hot32[:, w % 4, :, :], hot[:, w, :, :], ACT.Copy).then_inc(floated, 1)
                if live(1):
                    w = (u - 1) % U
                    done(act, turned, i, 1)
                    done(act, top_back, i, 9)
                    nc.scalar.activation(turn[:, w, :, :], ps_turn[w % 2][:], ACT.Copy).then_inc(turned_c, 1)
                if live(3):
                    w = (u - 3) % U
                    done(act, scored, i, 3)
                    done(act, negated, i, 3)
                    done(act, by_source, i, 5)
                    for j in range(2):
                        last = nc.scalar.activation(by_src[:, w % 2, j, :], neg[:, w % 4, j, :], ACT.Identity,
                                                    bias=score[:, w, j:j + 1])
                    last.then_inc(laid, 1)
                if live(7):
                    w = (u - 7) % U
                    done(act, args, i, 7)
                    done(act, summed, i, 11)
                    done(act, valued, i, 11)
                    nc.scalar.activation(scale[:, w % 4:w % 4 + 1], rise[:, w % 4:w % 4 + 1], ACT.Exp, scale=-1.0)
                    nc.scalar.activation(ew[:, w % 4, :], arg[:, w % 4, :], ACT.Exp).then_inc(weighed, 1)
            run_steps(act, NG, 7, U, one)

        @block.vector
        def _(v):
            nc.vector.memset(gate[:], 1.0)
            nc.vector.memset(top[:], -BIG)
            nc.vector.memset(acc[:], 0.0)
            nc.vector.memset(bin_i[:], 0).then_inc(setup, 1)
            v.wait_ge(setup, 1)
            nc.vector.tensor_copy(bin_i[0:1, AHEAD:AHEAD + NG], keep["bin_row"][0:1, 0:NG]).then_inc(setup, 1)
            v.wait_ge(setup, 2)
            v.sem_inc(ready, 1)
            bins = Bins(v, U + 5)
            at = [None]

            def one(i, u, live):
                if u == 0:
                    at[0] = bins(bin_i, i + AHEAD - 10)
                w5, w7, w8, w10 = ((u - k) % U for k in (5, 7, 8, 10))
                s5 = w5 % 4
                if live(5):
                    b5 = top[:, bass.ds(at[0][u + 5], 1)]

                def top_step(n):
                    v.wait_ge(c_top, (i - 5) * 6 + n)

                if live(0):
                    if u % GR == 0:
                        h = u // GR
                        v.wait_ge(rec_in[h], (i - u) * (16 // U) + 16)
                        if not known(i) or i >= U:
                            for k in range(GR):
                                v.wait_ge(gathered[h * GR + k], (i - u) * (32 // U))
                        nc.vector.tensor_copy(idx[:, 2 * GR * h:2 * GR * (h + 1)], rec[:, 2 * GR * h:2 * GR * (h + 1), 0]).then_inc(idx_ready, GR)
                    done(v, turned, i, 8)
                    done(v, floated, i, 8)
                    done(v, negated, i, 8)
                    for j in range(2):
                        last = nc.vector.tensor_scalar(hot[:, u, j, :], keep["iota"][:, 0:P], rec[:, 2 * u + j, 1:2], None, ALU.is_equal)
                    last.then_inc(hots, 1)
                if live(3):
                    w = (u - 3) % U
                    done(v, hidden, i, 3)
                    v.wait_ge(gathered[w], (i - 3 - w) * (32 // U) + 32)
                    done(v, scored, i, 4)
                    nc.vector.tensor_tensor(hid[:], ps_hid[w % 2][:], rows[:, 2 * w:2 * w + 2, 0:HW], ALU.add).then_inc(added, 1)
                if live(6):
                    done(v, topped, i, 6)
                    nc.vector.tensor_scalar(top[:, bass.ds(at[0][u + 4], 1)], new[:, (s5 - 1) % 4:(s5 - 1) % 4 + 1], 1.0, None, ALU.mult).then_inc(c_top, 1)
                if live(5):
                    done(v, by_source, i, 5)
                    nc.vector.tensor_reduce(mx[:, s5:s5 + 1], ps_src[w5 % 2][:].rearrange("p j e -> p (j e)"), AX.X, ALU.max).then_inc(c_top, 1)
                if live(3):
                    w = (u - 3) % U
                    done(v, added, i, 3)
                    for j in range(2):
                        last = nc.vector.scalar_tensor_tensor(junk[:, w % 2, j, :], hid[:, j, :], 0.0, w2[:], ALU.max, ALU.mult,
                                                              accum_out=score[:, w, j:j + 1])
                    last.then_inc(scored, 1)
                if live(5):
                    top_step(1)
                    nc.vector.tensor_tensor(mx2[:, s5:s5 + 1], mx[:, s5:s5 + 1], b5, ALU.max).then_inc(c_top, 1)
                if live(7):
                    done(v, top_back, i, 7)
                    for j in range(2):
                        last = nc.vector.tensor_scalar(arg[:, w7 % 4, j:j + 1], score[:, w7, j:j + 1], ps_top[:, j:j + 1], 64.0,
                                                       ALU.subtract, ALU.min)
                    last.then_inc(args, 1)
                if live(5):
                    top_step(2)
                    nc.vector.tensor_copy(parts[:, s5, 0:1], mx2[:, s5:s5 + 1]).then_inc(c_top, 1)
                if live(8):
                    done(v, weighed, i, 8)
                    done(v, aggregated, i, 10)
                    nc.vector.tensor_tensor(val[:, w8 % 2, :, :], rows[:, 2 * w8:2 * w8 + 2, H1:QL],
                                            ew[:, w8 % 4, :].unsqueeze(2).to_broadcast([P, 2, D + 1]), ALU.mult).then_inc(valued, 1)
                if live(5):
                    top_step(3)
                    nc.vector.tensor_tensor(parts[:, s5, 1:2], mx2[:, s5:s5 + 1], parts[:, s5, 0:1], ALU.subtract).then_inc(c_top, 1)
                if live(10):
                    done(v, aggregated, i, 10)
                    done(v, summed, i, 11)
                    a = acc[:, bass.ds(at[0][u], 1), :]
                    nc.vector.scalar_tensor_tensor(a, a, scale[:, w10 % 4:w10 % 4 + 1], ps_sum[:].unsqueeze(1), ALU.mult, ALU.add).then_inc(summed, 1)
                if live(5):
                    top_step(4)
                    nc.vector.tensor_tensor(new[:, s5:s5 + 1], parts[:, s5, 0:1], parts[:, s5, 1:2], ALU.add).then_inc(c_top, 1)
                    top_step(5)
                    nc.vector.tensor_tensor(rise[:, s5:s5 + 1], new[:, s5:s5 + 1], b5, ALU.subtract).then_inc(topped, 1)
            run_steps(v, NG, 10, U, one)


def gru(nc, ctx, keep, gi, w_hh, acc, out):
    def sb(name, shape, dt=F32):
        return ctx.enter_context(nc.sbuf_tensor(name, shape, dt))

    def sem(name):
        return ctx.enter_context(nc.semaphore(name))

    msg, gh = sb("message", [P, NB, D]), sb("gates_msg", [P, NB, 3 * D])
    den, has = sb("den", [P, NB]), sb("has_edge", [P, NB])
    tile, m_t = sb("msg_tile", [P, 2, P]), sb("msg_turned", [D + 1, 2, P])
    rz, nn, t1 = sb("rz", [P, NB, 2 * D]), sb("nn", [P, NB, D]), sb("gru_t1", [P, NB, D])
    ps_t = [ctx.enter_context(nc.psum_tensor(f"ps_mt{k}", [P, P], F32)) for k in range(2)]
    ps_g = [ctx.enter_context(nc.psum_tensor(f"ps_gates{k}", [P, 3 * D], F32)) for k in range(2)]
    zeroed, begun, vsteps, tiled, turned, turned_c, made, kept, summed, gated, pre_n, n_done, stored = (
        sem(x) for x in ("gru_zeroed", "msg_ready", "gru_vsteps", "gru_tiled", "gru_turned", "gru_turned_c", "gru_made",
                         "gru_kept", "gru_summed", "gru_gated", "gru_pre_n", "gru_n", "out_stored"))
    x, h = keep["x"], keep["h"]

    with nc.Block() as block:
        @block.gpsimd
        def _(pool):
            nc.gpsimd.memset(tile[:], 0.0).then_inc(zeroed, 1)

        @block.scalar
        def _(act):
            act.wait_ge(begun, 1)
            act.wait_ge(zeroed, 2)

            def one(i, u, live):
                if live(0):
                    if not known(i) or i >= 2:
                        act.wait_ge(turned, i - 1)
                    nc.scalar.activation(tile[:, u:u + 1, 0:D], msg[:, bass.ds(i, 1), :], ACT.Copy).then_inc(tiled, 1)
                if live(1):
                    act.wait_ge(turned, i)
                    if not known(i) or i >= 3:
                        act.wait_ge(made, i - 2)
                    nc.scalar.activation(m_t[0:D, 1 - u, :], ps_t[1 - u][0:D, :], ACT.Copy).then_inc(turned_c, 1)
            run_steps(act, NB, 1, 2, one)
            act.wait_ge(summed, 1)
            nc.scalar.activation(rz[:], rz[:], ACT.Sigmoid).then_inc(gated, 1)
            act.wait_ge(pre_n, 1)
            nc.scalar.activation(nn[:], nn[:], ACT.Tanh).then_inc(n_done, 1)

        @block.tensor
        def _(pe):
            def one(i, u, live):
                if live(0):
                    pe.wait_ge(tiled, i + 1)
                    if not known(i) or i >= 2:
                        pe.wait_ge(turned_c, i - 1)
                    nc.tensor.transpose(ps_t[u][:], tile[:, u, :], keep["ident"][:]).then_inc(turned, 1)
                if live(1):
                    pe.wait_ge(turned_c, i)
                    if not known(i) or i >= 3:
                        pe.wait_ge(kept, i - 2)
                    nc.tensor.matmul(ps_g[1 - u][:], m_t[:, 1 - u, :], w_hh[:], start=True, stop=True).then_inc(made, 1)
            run_steps(pe, NB, 1, 2, one)

        @block.vector
        def _(v):
            ch = Chain(v, vsteps)
            nc.vector.memset(m_t[D:D + 1, :, :], 1.0).then_inc(zeroed, 1)
            nc.vector.tensor_scalar(has[:], acc[:, :, 0], 0.5, None, ALU.is_ge)
            ch.link(nc.vector.tensor_scalar(den[:], acc[:, :, 0], 0.5, None, ALU.max))
            ch.link(nc.vector.reciprocal(den[:], den[:]))
            nc.vector.tensor_tensor(msg[:], acc[:, :, 1:D + 1], den[:].unsqueeze(2).to_broadcast([P, NB, D]), ALU.mult).then_inc(begun, 1)

            def one(i, u, live):
                if live(0):
                    v.wait_ge(made, i + 1)
                    nc.vector.tensor_scalar(gh[:, bass.ds(i, 1), :], ps_g[u][:].unsqueeze(1), 1.0, None, ALU.mult).then_inc(kept, 1)
            run_steps(v, NB, 0, 2, one)
            v.wait_ge(kept, NB)
            nc.vector.tensor_tensor(rz[:], gi[:, :, 0:2 * D], gh[:, :, 0:2 * D], ALU.add).then_inc(summed, 1)
            v.wait_ge(gated, 1)
            ch.link(nc.vector.tensor_tensor(t1[:], rz[:, :, 0:D], gh[:, :, 2 * D:3 * D], ALU.mult))
            nc.vector.tensor_tensor(nn[:], t1[:], gi[:, :, 2 * D:3 * D], ALU.add).then_inc(pre_n, 1)
            v.wait_ge(n_done, 1)
            z = rz[:, :, D:2 * D]
            ch.link(nc.vector.tensor_tensor(t1[:], msg[:], nn[:], ALU.subtract))
            ch.link(nc.vector.tensor_tensor(t1[:], t1[:], z, ALU.mult))
            ch.link(nc.vector.tensor_tensor(t1[:], t1[:], nn[:], ALU.add))
            ch.link(nc.vector.tensor_tensor(t1[:], t1[:], h[:], ALU.subtract))
            ch.link(nc.vector.tensor_tensor(t1[:], t1[:], has[:].unsqueeze(2).to_broadcast([P, NB, D]), ALU.mult))
            ch.link(nc.vector.tensor_tensor(t1[:], t1[:], h[:], ALU.add))
            ch.link(nc.vector.tensor_tensor(x[:], x[:], t1[:], ALU.add))
            v.sem_inc(begun, 1)

        @block.sync
        def _(sp):
            sp.wait_ge(begun, 2)
            ov = out.rearrange("(t p) d -> p t d", p=BN)
            for a, b in node_parts():
                sp.dma_start(ov[a:b, :, :], x[a:b, :, :]).then_inc(stored, 16)
            sp.wait_ge(stored, 32)


_OUT = ((N, D), "float32")


def kernel(x, src, dst, edge_attr_16, L0_gnn_W0, L0_gnn_b0, L0_gnn_W1, L0_gnn_b1, L0_gnn_W2, L0_gnn_b2,
           L1_gnn_W_att1, L1_gnn_b_att1, L1_gnn_W_att2, L1_gnn_b_att2, L1_gnn_W_lin, L1_gnn_b_lin,
           L1_gnn_W_ih, L1_gnn_b_ih, L1_gnn_W_hh, L1_gnn_b_hh):
    import numpy as np
    import concourse.bacc as bacc
    from concourse.bass_utils import run_bass_kernel_spmd

    def turned(w):
        return np.ascontiguousarray(np.asarray(w).T)

    arrays = dict(
        x=x, src=src, dst=dst, attr=edge_attr_16,
        w_gcn=np.stack([np.asarray(w) for w in (L0_gnn_W0, L0_gnn_W1, L0_gnn_W2)]),
        b_gcn=np.stack([np.asarray(b) for b in (L0_gnn_b0, L0_gnn_b1, L0_gnn_b2)]),
        w_att1t=turned(L1_gnn_W_att1), b_att1=L1_gnn_b_att1, w_att2=L1_gnn_W_att2, b_att2=L1_gnn_b_att2,
        w_lint=turned(L1_gnn_W_lin), b_lin=L1_gnn_b_lin, w_iht=turned(L1_gnn_W_ih), b_ih=L1_gnn_b_ih,
        w_hht=turned(L1_gnn_W_hh), b_hh=L1_gnn_b_hh,
        part_mask=np.repeat(np.eye(3, dtype=np.float32)[list(W_PART)], ED, axis=0),
        eye=np.eye(P, dtype=np.float32), upper=np.triu(np.ones((P, P), np.float32), 1),
    )
    nc = bacc.Bacc("TRN2", target_bir_lowering=False, num_devices=1)
    ins, args = {}, {}
    for name, a in arrays.items():
        a = np.ascontiguousarray(a)
        ins[f"in_{name}"] = a
        args[name] = nc.dram_tensor(f"in_{name}", a.shape, mybir.dt.from_np(a.dtype), kind="ExternalInput").ap()
    args["out"] = nc.dram_tensor("out_0", _OUT[0], F32, kind="ExternalOutput").ap()
    gnn_kernel(nc, **args)
    r = run_bass_kernel_spmd(nc, [ins], core_ids=[0])
    return r.results[0]["out_0"]
```

```python
import concourse.bass as bass
from concourse import mybir
from contextlib import ExitStack

F32 = mybir.dt.float32
BF16 = mybir.dt.bfloat16
F16 = mybir.dt.float16
I32 = mybir.dt.int32
ALU = mybir.AluOpType
ACT = mybir.ActivationFunctionType
AX = mybir.AxisListType

P = 128
N, D, ED, E = 3125, 64, 16, 53125
H1 = 2 * D + ED
NB = -(-N // P)
BN = -(-N // NB)
assert N == NB * BN
DIV, SHIFT = 4195, 19
assert all((n * DIV) >> SHIFT == n // BN for n in range(N + 1)) and N * DIV < 1 << 24
T = -(-E // P)
LAST_P = E // T
LAST_E = E - LAST_P * T
PAIR = 2 * P
NG = (E + NB * (PAIR - 1)) // PAIR
NG += NG % 4 and 4 - NG % 4
TT = 2 * NG
A_PART = (0, 1, 2, 0)
W_PART = (0, 0, 0, 2, 1, 1, 1, None)
HG = NG // 2
REC = 2 + len(A_PART) * ED // 2
TRASH = P * TT
WIN = 512
AC = NB * P
ACOLS = NB * AC + WIN
HW = H1 + 1
QL = HW + D
BIG = 2.0 ** 100
EPS = 1e-5
SPLIT3 = (0, 1, 2)


class Chain:

    def __init__(self, eng, sem, base=0):
        self.eng, self.sem, self.base, self.n = eng, sem, base, 0

    def link(self, ins):
        self.n += 1
        ins.then_inc(self.sem, 1)
        self.eng.wait_ge(self.sem, self.base + self.n)

    def step(self, idx, per):
        self.base, self.n, self.per = idx * per, 0, per

    def end(self):
        assert self.n == self.per, (self.n, self.per)


def run_steps(eng, count, lag, unroll, step, head=None):
    if head is None:
        head = -(-(2 * unroll + lag) // unroll) * unroll
    head = min(head, count - count % unroll)
    loops = (count - head) // unroll
    for i in range(head):
        step(i, i % unroll, lambda l, i=i: 0 <= i - l < count)
    if loops:
        with eng.Fori(0, loops) as r:
            for u in range(unroll):
                step(r * unroll + (head + u), u, lambda l: True)
    for i in range(head + loops * unroll, count + lag):
        step(i, i % unroll, lambda l, i=i: 0 <= i - l < count)


def node_parts():
    return (0, BN - BN % 16), (BN - BN % 16, BN)


def known(i):
    return isinstance(i, int)


def gnn_kernel(nc, x, src, dst, attr, w_gcn, b_gcn, w_att1t, b_att1, w_att2, b_att2, w_lint, b_lin,
               w_iht, b_ih, w_hht, b_hh, eye, upper, part_mask, out, dbg=None):
    dbg = dbg or {}
    table = nc.dram_tensor("edge_records", [TRASH + P, REC], F32, kind="Internal").ap()
    qtable = nc.dram_tensor("target_rows", [NB * P, QL], F32, kind="Internal").ap()
    with ExitStack() as ctx:
        def sb(name, shape, dt=F32):
            return ctx.enter_context(nc.sbuf_tensor(name, shape, dt))

        keep = dict(
            ident=sb("ident", [P, P]), identb=sb("identb", [P, P], BF16),
            upper=sb("upper_tri", [P, P]), ones=sb("ones", [P, P]), onesb=sb("onesb", [P, 1], BF16),
            iota=sb("iota_cols", [P, WIN], F16),
            x=sb("x_nodes", [P, NB, D]), h=sb("h_nodes", [P, NB, D]),
            bin_row=sb("bin_row", [1, NG + 8]),
            dinv=sb("dinv", [P, NB + 1]),
            wg=sb("w_gcn_sb", [D, 3, D]), bg=sb("b_gcn_sb", [P, 3, D]),
        )
        srt = ExitStack()
        with srt:
            rank_and_scatter(nc, srt, keep, x, src, dst, attr, w_gcn, b_gcn, eye, upper, table, dbg)
        with ExitStack() as adj:
            adjacency_and_gcn(nc, adj, keep, table, dbg)
        with ExitStack() as att:
            attention(nc, att, keep, table, qtable, w_att1t, b_att1, w_att2, b_att2, w_lint, b_lin,
                      w_iht, b_ih, w_hht, b_hh, part_mask, out, dbg)


def ln_centre(nc, ch, xin, tmp, st):
    ch.link(nc.vector.tensor_reduce(st[:, 0, :], xin, AX.X, ALU.add))
    ch.link(nc.vector.tensor_scalar(st[:, 0, :], st[:, 0, :], 1.0 / D, None, ALU.mult))
    ch.link(nc.vector.tensor_tensor(tmp, xin, st[:, 0, :].unsqueeze(2).to_broadcast([P, NB, D]), ALU.subtract))


def ln_variance(nc, ch, tmp, sq, st, var_ready):
    ch.link(nc.vector.tensor_tensor(sq, tmp, tmp, ALU.mult))
    ch.link(nc.vector.tensor_reduce(st[:, 1, :], sq, AX.X, ALU.add))
    nc.vector.tensor_scalar(st[:, 1, :], st[:, 1, :], 1.0 / D, EPS, ALU.mult, ALU.add).then_inc(var_ready, 1)


def ln_scale(nc, v, ch, tmp, sq, st, std_ready, hout):
    v.wait_ge(std_ready, 1)
    ch.link(nc.vector.reciprocal(st[:, 3, :], st[:, 2, :]))
    ch.link(nc.vector.tensor_tensor(sq, tmp, st[:, 3, :].unsqueeze(2).to_broadcast([P, NB, D]), ALU.mult))
    ch.link(nc.vector.tensor_scalar(hout, sq, 0.0, None, ALU.max))


def rank_and_scatter(nc, ctx, keep, x, src, dst, attr, w_gcn, b_gcn, eye, upper, table, dbg):
    def sb(name, shape, dt=F32):
        return ctx.enter_context(nc.sbuf_tensor(name, shape, dt))

    def sem(name):
        return ctx.enter_context(nc.semaphore(name))

    UN = 16
    HALF = UN // 2
    attr_in = sb("attr_in", [P, T, ED])
    dst_f = sb("dst_f", [P, T])
    lo_f = sb("lo_f", [P, T])
    dst_bin = sb("dst_bin", [P, T])
    dst_lo = sb("dst_lo", [P, T])
    row_i = sb("row_i", [P, T], I32)
    ring = sb("record_ring", [P, 2, HALF, REC])
    ring_i = sb("row_ring", [P, 2, HALF], I32)
    gate = sb("gate", [1, 2])
    endp = sb("bin_end_pair", [P, NB])
    pair_no = sb("pair_number", [P, 2])
    with ExitStack() as c1:
        def sb1(name, shape, dt=F32):
            return c1.enter_context(nc.sbuf_tensor(name, shape, dt))

        def sem1(name):
            return c1.enter_context(nc.semaphore(name))

        src_i = sb1("src_i", [P, T], I32)
        dst_i = sb1("dst_i", [P, T], I32)
        int_a = sb1("int_a", [P, T], I32)
        int_b = sb1("int_b", [P, T], I32)
        place_i, row_hi, row_lo = (sb1(x, [P, T], I32) for x in ("place", "place_row", "place_tile"))
        eidx = sb1("edge_index", [P, T])
        pad_row = sb1("padding_row", [P, T])
        src_bin = sb1("src_bin", [P, T], F16)
        hot = sb1("bin_hot", [P, NB, T], F16)
        cum = sb1("bin_cum", [P, NB, T], F16)
        ident16 = sb1("ident16", [P, P], F16)
        offs = sb1("edge_offset", [P, 2, T])
        ends = sb1("bin_ends", [P, NB + 1])
        cnt = sb1("bin_count", [P, NB])
        tot_i = sb1("bin_total_i", [P, NB], I32)
        pairs = sb1("bin_pairs", [P, NB])
        off = sb1("bin_offset", [P, NB])
        pad = sb1("pad_records", [P, TT // 8, REC])
        ps_before = c1.enter_context(nc.psum_tensor("ps_before", [P, NB], F32))
        ps_total = c1.enter_context(nc.psum_tensor("ps_total", [P, NB], F32))
        ps_rank = c1.enter_context(nc.psum_tensor("ps_rank", [P, T], F32))

        padded = sem1("padded")
        loaded_ids = sem1("loaded_ids")
        loaded_attr = sem1("loaded_attr")
        loaded_x = sem1("loaded_x")
        loaded_const = sem1("loaded_const")
        pool_made = sem1("pool_made")
        prefilled = sem1("prefilled")
        counted = sem1("counted")
        prefixed = sem1("prefixed")
        picked = sem1("picked")
        summing = sem1("summing")
        ranked = sem1("ranked")
        vsteps = sem1("vsteps")
        psteps = sem1("psteps")
        copied = sem1("const_copied")

        def edge_parts(dst_tile, dram, per):
            main = LAST_P - LAST_P % 16
            full = dram[0:LAST_P * T] if len(dram.shape) == 1 else dram[0:LAST_P * T, :]
            pat = "(p t) -> p t" if len(dram.shape) == 1 else "(p t) c -> p t c"
            full = full.rearrange(pat, t=T)
            rest = dram[LAST_P * T:E] if len(dram.shape) == 1 else dram[LAST_P * T:E, :]
            rest = rest.unsqueeze(0)
            return [(dst_tile[0:main], full[0:main]), (dst_tile[main:LAST_P], full[main:LAST_P]),
                    (dst_tile[LAST_P:P, 0:LAST_E], rest)]

        with nc.Block() as block:
            @block.sync
            def _(sp):
                sp.wait_ge(padded, 2)
                for t, d in ((src_i, src), (dst_i, dst)):
                    for o, i in edge_parts(t, d, 1):
                        sp.dma_start(o, i).then_inc(loaded_ids, 16)
                sp.wait_ge(padded, 4)
                for o, i in edge_parts(attr_in, attr, ED):
                    sp.dma_start(o, i).then_inc(loaded_attr, 16)
                xv = x.rearrange("(t p) d -> p t d", p=BN)
                for a, b in node_parts():
                    sp.dma_start(keep["x"][a:b, :, :], xv[a:b, :, :]).then_inc(loaded_x, 16)
                sp.wait_ge(loaded_attr, 48)
                sp.wait_ge(loaded_x, 32)

            @block.scalar
            def _(act):
                act.dma_start(keep["ident"][:], eye).then_inc(loaded_const, 16)
                act.dma_start(keep["upper"][:], upper).then_inc(loaded_const, 16)
                act.dma_start(keep["wg"][:], w_gcn.rearrange("l i o -> i l o")).then_inc(loaded_const, 16)
                act.dma_start(keep["bg"][:], b_gcn.partition_broadcast(P)).then_inc(loaded_const, 16)
                act.wait_ge(pool_made, 2)
                act.wait_ge(loaded_ids, 96)
                main = table[0:TRASH, :].rearrange("(p t) c -> p t c", t=TT)
                for k in range(8):
                    act.dma_start(main[:, k * (TT // 8):(k + 1) * (TT // 8), :], pad[:]).then_inc(prefilled, 16)
                act.wait_ge(loaded_const, 64)
                nc.scalar.activation(keep["identb"][:], keep["ident"][:], ACT.Copy).then_inc(copied, 1)
                nc.scalar.activation(ident16[:], keep["ident"][:], ACT.Copy).then_inc(copied, 1)
                act.wait_ge(prefilled, 8 * 16)

            @block.gpsimd
            def _(pool):
                ch = Chain(pool, psteps)
                nc.gpsimd.memset(keep["ones"][:], 1.0)
                nc.gpsimd.memset(gate[:], 1.0)
                nc.gpsimd.memset(keep["onesb"][:], 1.0)
                nc.gpsimd.iota(eidx[:], [[1, T]], base=0, channel_multiplier=T, allow_small_or_imprecise_dtypes=True)
                nc.gpsimd.iota(pair_no[:], [[HG, 2]], base=0, channel_multiplier=1, allow_small_or_imprecise_dtypes=True)
                nc.gpsimd.iota(keep["iota"][:], [[1, WIN]], base=0, channel_multiplier=0,
                               allow_small_or_imprecise_dtypes=True).then_inc(pool_made, 1)
                ch.link(nc.gpsimd.memset(pad[:], 0.0))
                nc.gpsimd.memset(pad[:, :, 1:2], -1.0).then_inc(pool_made, 1)

            @block.tensor
            def _(pe):
                pe.wait_ge(loaded_const, 64)
                pe.wait_ge(pool_made, 1)
                pe.wait_ge(counted, 1)
                nc.tensor.matmul(ps_before[:], keep["upper"][:], cnt[:], start=True, stop=True)
                nc.tensor.matmul(ps_total[:], keep["ones"][:], cnt[:], start=True, stop=True).then_inc(prefixed, 1)
                pe.wait_ge(copied, 2)
                pe.wait_ge(picked, 1)
                for b in range(NB):
                    last = nc.tensor.matmul(ps_rank[:], ident16[:], cum[:, b, :], start=(b == 0), stop=(b == NB - 1))
                last.then_inc(ranked, 1)

            @block.vector
            def _(v):
                ch = Chain(v, vsteps)
                nc.vector.memset(src_i[:, LAST_E:T], N).then_inc(padded, 1)
                nc.vector.memset(dst_i[:, LAST_E:T], N).then_inc(padded, 1)
                nc.vector.memset(attr_in[:, LAST_E:T, :], 0.0).then_inc(padded, 1)
                nc.vector.memset(keep["x"][96:P, :, :], 0.0).then_inc(padded, 1)
                nc.vector.memset(ends[:, 0:1], 0.0)
                v.wait_ge(pool_made, 1)
                ch.link(nc.vector.tensor_scalar(pad_row[:], eidx[:], float(E), None, ALU.is_ge))
                ch.link(nc.vector.scalar_tensor_tensor(pad_row[:], eidx[:], float(TRASH - E), pad_row[:], ALU.add, ALU.mult))
                v.wait_ge(loaded_ids, 96)
                nc.vector.tensor_scalar(int_a[:], src_i[:], float(DIV), None, ALU.mult)
                ch.link(nc.vector.tensor_scalar(int_b[:], dst_i[:], float(DIV), None, ALU.mult))
                nc.vector.tensor_scalar(int_a[:], int_a[:], SHIFT, None, ALU.logical_shift_right)
                ch.link(nc.vector.tensor_scalar(int_b[:], int_b[:], SHIFT, None, ALU.logical_shift_right))
                ch.link(nc.vector.tensor_copy(src_bin[:], int_a[:]))
                for b in range(NB):
                    last = nc.vector.tensor_scalar(hot[:, b, :], src_bin[:], float(b), None, ALU.is_equal)
                ch.link(last)
                hot2, cum2 = (a[:].rearrange("p b t -> p (b t)") for a in (hot, cum))
                ch.link(nc.vector.tensor_tensor_scan(cum2, hot2, hot2, 0.0, ALU.add, ALU.max))
                ch.link(nc.vector.tensor_copy(ends[:, 1:NB + 1], cum[:, :, T - 1]))
                nc.vector.tensor_tensor(cnt[:], ends[:, 1:NB + 1], ends[:, 0:NB], ALU.subtract).then_inc(counted, 1)
                nc.vector.tensor_tensor(cum[:], cum[:], hot[:], ALU.mult).then_inc(picked, 1)
                v.wait_ge(prefixed, 1)
                ch.link(nc.vector.tensor_scalar(tot_i[:], ps_total[:], float(PAIR - 1), None, ALU.add))
                ch.link(nc.vector.tensor_scalar(tot_i[:], tot_i[:], 8, None, ALU.logical_shift_right))
                ch.link(nc.vector.tensor_copy(pairs[:], tot_i[:]))
                ch.link(nc.vector.tensor_tensor_scan(endp[:], pairs[:], pairs[:], 0.0, ALU.add, ALU.max))
                ch.link(nc.vector.tensor_tensor(off[:], endp[:], pairs[:], ALU.subtract))
                ch.link(nc.vector.tensor_scalar(off[:], off[:], float(PAIR), -1.0, ALU.mult, ALU.add))
                ch.link(nc.vector.tensor_tensor(off[:], off[:], ends[:, 0:NB], ALU.subtract))
                ch.link(nc.vector.tensor_tensor(off[:], off[:], ps_before[:], ALU.add))
                for b in range(NB):
                    o = offs[:, b % 2, :]
                    if b < 2:
                        ch.link(nc.vector.tensor_scalar(o, hot[:, b, :], off[:, b:b + 1], None, ALU.mult))
                    else:
                        last = nc.vector.scalar_tensor_tensor(o, hot[:, b, :], off[:, b:b + 1], o, ALU.mult, ALU.add)
                        last.then_inc(summing, 1)
                        if b > 2:
                            v.wait_ge(summing, b - 2)
                v.wait_ge(summing, NB - 2)
                ch.link(nc.vector.tensor_tensor(offs[:, 0, :], offs[:, 0, :], offs[:, 1, :], ALU.add))
                v.wait_ge(ranked, 1)
                ch.link(nc.vector.tensor_tensor(place_i[:], offs[:, 0, :], ps_rank[:], ALU.add))
                nc.vector.tensor_scalar(row_hi[:], place_i[:], P - 1, None, ALU.bitwise_and)
                ch.link(nc.vector.tensor_scalar(row_lo[:], place_i[:], 7, None, ALU.logical_shift_right))
                ch.link(nc.vector.scalar_tensor_tensor(offs[:, 0, :], row_hi[:], float(TT), row_lo[:], ALU.mult, ALU.add))
                nc.vector.tensor_tensor(row_i[:], offs[:, 0, :], pad_row[:], ALU.add)
                nc.vector.tensor_copy(dst_bin[:], int_b[:])
                nc.vector.scalar_tensor_tensor(lo_f[:], int_a[:], float(-BN), src_i[:], ALU.mult, ALU.add)
                nc.vector.scalar_tensor_tensor(dst_lo[:], int_b[:], float(-BN), dst_i[:], ALU.mult, ALU.add)
                nc.vector.scalar_tensor_tensor(dst_f[:], int_b[:], float(P - BN), dst_i[:], ALU.mult, ALU.add)

    copied_ring = sem("ring_copied")
    gated = sem("gated")
    scattered = [sem(f"scattered{k}") for k in range(2)]
    split, lo_hots, lo_counted, deg_ready, root_ready, dsteps = (
        sem(x) for x in ("attr_split", "lo_hots", "lo_counted", "inv_deg_ready", "root_ready", "deg_vsteps"))
    rest = sb("attr_rest", [P, HALF, ED])
    bin_hot = sb("dst_bin_hot", [P, 2, HALF, NB], BF16)
    tmp, sq, st = sb("ln_tmp", [P, NB, D]), sb("ln_sq", [P, NB, D]), sb("ln_stats", [P, 4, NB])
    ended = sb("bins_ended", [P, 2, NB])
    pair_bin = sb("pair_bin", [P, 2])
    ps_bin = ctx.enter_context(nc.psum_tensor("ps_pair_bin", [1, 2, HG], F32))
    var_ready, std_ready, bins_found, bins_turned = (sem(x) for x in ("var_ready", "std_ready", "bins_found", "bins_turned"))
    lo_hot = sb("dst_lo_hot", [P, 2, HALF, P], BF16)
    ideg = sb("inv_deg", [P, NB])
    ps_deg = ctx.enter_context(nc.psum_tensor("ps_deg", [P, NB], F32))
    LOOPS = T // UN
    with nc.Block() as block:
        @block.vector
        def _(v):
            def half(i, k):
                t0 = i * UN + k * HALF
                if not known(i) or i >= 1:
                    v.wait_ge(scattered[k], i * (16 * HALF))
                ch = Chain(v, split, (i * 2 + k) * 3)
                bf = ring[:, k, :, 2:REC].bitcast(BF16).rearrange("p t (b c) -> p t b c", c=ED)
                a = attr_in[:, bass.ds(t0, HALF), :]

                p0, p1, p2, p0_again = (bf[:, :, b, :] for b in range(4))
                nc.vector.tensor_copy(ring_i[:, k, :], row_i[:, bass.ds(t0, HALF)])
                nc.vector.tensor_copy(ring[:, k, :, 0], dst_f[:, bass.ds(t0, HALF)])
                nc.vector.tensor_copy(ring[:, k, :, 1], lo_f[:, bass.ds(t0, HALF)])
                nc.vector.tensor_copy(p0_again, a)
                ch.link(nc.vector.tensor_copy(p0, a))
                ch.link(nc.vector.tensor_tensor(rest[:], a, p0, ALU.subtract))
                ch.link(nc.vector.tensor_copy(p1, rest[:]))
                nc.vector.tensor_tensor(p2, rest[:], p1, ALU.subtract).then_inc(copied_ring, 1)
                if not known(i) or i >= 1:
                    v.wait_ge(lo_counted, i * 2 + k - 1)
                for t in range(HALF):
                    nc.vector.tensor_scalar(bin_hot[:, k, t, :], keep["iota"][:, 0:NB], dst_bin[:, bass.ds(t0 + t, 1)], None, ALU.is_equal)
                    last = nc.vector.tensor_scalar(lo_hot[:, k, t, :], keep["iota"][:, 0:P], dst_lo[:, bass.ds(t0 + t, 1)], None, ALU.is_equal)
                last.then_inc(lo_hots, 1)
            ch = Chain(v, dsteps)
            half(0, 0)
            half(0, 1)
            ln_centre(nc, ch, keep["x"][:], tmp[:], st)
            half(1, 0)
            ln_variance(nc, ch, tmp[:], sq[:], st, var_ready)
            half(1, 1)
            ln_scale(nc, v, ch, tmp[:], sq[:], st, std_ready, keep["h"][:])
            ch.link(nc.vector.tensor_tensor(ended[:], pair_no[:].unsqueeze(2).to_broadcast([P, 2, NB]),
                                            endp[:].unsqueeze(1).to_broadcast([P, 2, NB]), ALU.is_ge))
            nc.vector.tensor_reduce(pair_bin[:], ended[:], AX.X, ALU.add).then_inc(bins_found, 1)
            with v.Fori(2, LOOPS) as i:
                for k in range(2):
                    half(i, k)
            v.wait_ge(bins_turned, 1)
            nc.vector.tensor_scalar(keep["bin_row"][0:1, 0:NG], ps_bin[:].rearrange("a k g -> a (k g)"), float(NB - 1), None, ALU.min)
            v.wait_ge(lo_counted, 2 * LOOPS)
            ch.link(nc.vector.tensor_scalar(ideg[:], ps_deg[:], 1.0, None, ALU.add))
            nc.vector.reciprocal(ideg[:], ideg[:]).then_inc(deg_ready, 1)
            v.wait_ge(root_ready, 1)
            h = keep["h"]
            ch.link(nc.vector.tensor_tensor(h[:], h[:], keep["dinv"][:, 0:NB].unsqueeze(2).to_broadcast([P, NB, D]), ALU.mult))

        @block.scalar
        def _(act):
            act.wait_ge(var_ready, 1)
            nc.scalar.activation(st[:, 2, :], st[:, 1, :], ACT.Sqrt).then_inc(std_ready, 1)
            act.wait_ge(deg_ready, 1)
            nc.scalar.activation(keep["dinv"][:, 0:NB], ideg[:], ACT.Sqrt).then_inc(root_ready, 1)

        @block.tensor
        def _(pe):
            def half(i, k):
                pe.wait_ge(lo_hots, i * 2 + k + 1)
                for t in range(HALF):
                    first = known(i) and i + k + t == 0
                    last = nc.tensor.matmul(ps_deg[:], lo_hot[:, k, t, :], bin_hot[:, k, t, :],
                                            start=first, stop=False, skip_group_check=True)
                last.then_inc(lo_counted, 1)
            for k in range(2):
                half(0, k)
            with pe.Fori(1, LOOPS) as i:
                for k in range(2):
                    half(i, k)
            pe.wait_ge(bins_found, 1)
            for k in range(2):
                last = nc.tensor.matmul(ps_bin[0:1, k, :], pair_bin[0:HG, k:k + 1], keep["ident"][0:HG, 0:HG], start=True, stop=True)
            last.then_inc(bins_turned, 1)

        @block.gpsimd
        def _(pool):
            def half(i, k):
                if not known(i) or 2 * i + k > 0:
                    pool.wait_ge(gated, i * 2 + k)
                pool.wait_ge(copied_ring, i * 2 + k + 1)
                nc.gpsimd.tensor_tensor(gate[:, 1:2], gate[:, 0:1], gate[:, 0:1], ALU.mult).then_inc(gated, 1)
                for j in range(HALF):
                    pool.indirect_dma_start(table[:, :], bass.IndirectOffsetOnAxis(ap=ring_i[:, k, j:j + 1], axis=0),
                                            ring[:, k, j, :], None).then_inc(scattered[k], 16)
            for k in range(2):
                half(0, k)
            with pool.Fori(1, LOOPS) as i:
                for k in range(2):
                    half(i, k)

        @block.sync
        def _(sp):
            for k in range(2):
                sp.wait_ge(scattered[k], 16 * HALF * LOOPS)
            if "table" in dbg:
                sp.dma_start(dbg["table"], table[0:TRASH, :]).then_inc(copied_ring, 16)
                sp.wait_ge(copied_ring, 16 + 2 * LOOPS)
            if "bin_row" in dbg:
                sp.dma_start(dbg["bin_row"], keep["bin_row"][0:1, 0:NG]).then_inc(copied_ring, 16)
                sp.dma_start(dbg["h"], keep["h"][:]).then_inc(copied_ring, 16)
                sp.wait_ge(copied_ring, 48+ 2 * LOOPS)


class Loads:

    def __init__(self, eng, name, top, count):
        self.eng, self.top = eng, top
        self.regs = [eng.alloc_register(f"{name}{k}") for k in range(count)]

    def __call__(self, row, at):
        self.eng.load(self.regs, row[0:1, bass.ds(at, len(self.regs))])
        return [self.eng.snap(r, min_val=0, max_val=self.top) for r in self.regs]


LEAD = 4


def adjacency_and_gcn(nc, ctx, keep, table, dbg):
    def sb(name, shape, dt=F32):
        return ctx.enter_context(nc.sbuf_tensor(name, shape, dt))

    adj = sb("adjacency", [P, ACOLS], BF16)
    edges = ExitStack()
    dst_s = edges.enter_context(nc.sbuf_tensor("dst_sorted", [P, NG, 2], F32))
    rel_s = edges.enter_context(nc.sbuf_tensor("dst_in_window", [P, NG, 2], F32))
    lo_s = edges.enter_context(nc.sbuf_tensor("lo_sorted", [P, NG, 2], F32))
    win_i = edges.enter_context(nc.sbuf_tensor("window_at", [1, NG + 32], I32))
    bin_i = edges.enter_context(nc.sbuf_tensor("bin_at", [1, NG + 32], I32))
    flag_i = edges.enter_context(nc.sbuf_tensor("wide_flag", [1, 1], I32))

    with ExitStack() as c1:
        def sb1(name, shape, dt=F32):
            return c1.enter_context(nc.sbuf_tensor(name, shape, dt))

        def sem1(name):
            return c1.enter_context(nc.semaphore(name))

        rec = adj[:, 0:2 * TT * REC].bitcast(F32).rearrange("p (t c) -> p t c", c=REC)
        low = sb1("low", [P, NG, 2])
        ext = sb1("extremes", [P, 2, NG])
        mm = sb1("pair_extremes", [P, 4])
        row = sb1("extreme_rows", [1, 4, HG])
        w0 = sb1("window_start", [1, NG])
        w_i = sb1("window_start_i", [1, NG], I32)
        tmp = sb1("row_tmp", [1, NG])
        flag = sb1("flag_f", [1, 1])
        ps_t = c1.enter_context(nc.psum_tensor("ps_extremes", [P, 4, P], F32))
        ps_row = c1.enter_context(nc.psum_tensor("ps_rows", [1, 4, HG], F32))
        ps_w = c1.enter_context(nc.psum_tensor("ps_window", [P, NG], F32))
        CH = 4
        TC = TT // CH
        loaded = [sem1(f"records_loaded{k}") for k in range(CH)]
        vsteps = sem1("stat_vsteps")
        cleared = sem1("adj_cleared")
        taken = sem1("last_chunk_taken")
        to_pe = sem1("stat_to_pe")
        from_pe = sem1("stat_from_pe")
        words = adj[:].bitcast(F32)
        with nc.Block() as block:
            @block.gpsimd
            def _(pool):
                nc.gpsimd.memset(words[:, TT * REC:], 0.0).then_inc(cleared, 1)
                pool.wait_ge(taken, 1)
                nc.gpsimd.memset(words[:, (CH - 1) * TC * REC:TT * REC], 0.0).then_inc(cleared, 1)

            @block.sync
            def _(sp):
                tv = table[0:TRASH, :].rearrange("(p t) c -> p t c", t=TT)
                for k in range(CH):
                    sp.dma_start(rec[:, k * TC:(k + 1) * TC, :], tv[:, k * TC:(k + 1) * TC, :]).then_inc(loaded[k], 16)
                for k in range(CH):
                    sp.wait_ge(loaded[k], 16)

            @block.tensor
            def _(pe):
                pe.wait_ge(to_pe, 1)
                for q in range(4):
                    last = nc.tensor.transpose(ps_t[0:HG, q, :], ext[:, q // 2, (q % 2) * HG:(q % 2 + 1) * HG], keep["ident"][:])
                last.then_inc(from_pe, 1)
                pe.wait_ge(to_pe, 2)
                for q in range(4):
                    last = nc.tensor.matmul(ps_row[0:1, q, :], mm[0:HG, q:q + 1], keep["ident"][0:HG, 0:HG], start=True, stop=True)
                last.then_inc(from_pe, 1)
                pe.wait_ge(to_pe, 3)
                nc.tensor.matmul(ps_w[:], keep["ones"][0:1, :], w0[:], start=True, stop=True).then_inc(from_pe, 1)

            @block.vector
            def _(v):
                ch = Chain(v, vsteps)
                nc.vector.memset(win_i[:], 0)
                nc.vector.memset(bin_i[:], 0)
                rec2 = rec.rearrange("p (g j) c -> p g j c", j=2)
                for k in range(CH):
                    v.wait_ge(loaded[k], 16)
                    gs = slice(k * TC // 2, (k + 1) * TC // 2)
                    ch.link(nc.vector.tensor_copy(dst_s[:, gs, :], rec2[:, gs, :, 0]))
                    ch.link(nc.vector.tensor_copy(lo_s[:, gs, :], rec2[:, gs, :, 1]))
                    if k < CH - 1:
                        nc.vector.memset(words[:, k * TC * REC:(k + 1) * TC * REC], 0.0)
                v.sem_inc(taken, 1)
                ch.link(nc.vector.tensor_scalar(low[:], lo_s[:], 0.0, 4096.0, ALU.is_lt, ALU.mult))
                ch.link(nc.vector.tensor_tensor(low[:], low[:], dst_s[:], ALU.add))
                nc.vector.tensor_reduce(ext[:, 0, :], low[:], AX.X, ALU.min)
                nc.vector.tensor_reduce(ext[:, 1, :], dst_s[:], AX.X, ALU.max).then_inc(to_pe, 1)
                v.wait_ge(from_pe, 1)
                nc.vector.tensor_reduce(mm[0:HG, 0:2], ps_t[0:HG, 0:2, :], AX.X, ALU.min)
                nc.vector.tensor_reduce(mm[0:HG, 2:4], ps_t[0:HG, 2:4, :], AX.X, ALU.max).then_inc(to_pe, 1)
                v.wait_ge(from_pe, 2)
                ch.link(nc.vector.tensor_copy(row[:], ps_row[:]))
                least, most = (row[0:1, 2 * k:2 * k + 2, :].rearrange("p a g -> p (a g)") for k in range(2))
                ch.link(nc.vector.tensor_scalar(w_i[:], least, float(NB * P - 1), None, ALU.min))
                ch.link(nc.vector.tensor_scalar(w_i[:], w_i[:], -2, None, ALU.bitwise_and))
                nc.vector.tensor_copy(w0[:], w_i[:]).then_inc(to_pe, 1)
                v.wait_ge(to_pe, 3)
                nc.vector.tensor_scalar(bin_i[0:1, LEAD:LEAD + NG], keep["bin_row"][0:1, 0:NG], float(AC), None, ALU.mult)
                ch.link(nc.vector.scalar_tensor_tensor(win_i[0:1, LEAD:LEAD + NG], keep["bin_row"][0:1, 0:NG], float(AC), w0[:], ALU.mult, ALU.add))
                ch.link(nc.vector.tensor_tensor(tmp[:], most, w0[:], ALU.subtract))
                ch.link(nc.vector.tensor_reduce(flag[:], tmp[:], AX.X, ALU.max))
                ch.link(nc.vector.tensor_scalar(flag_i[:], flag[:], float(WIN), None, ALU.is_ge))
                v.wait_ge(from_pe, 3)
                ch.link(nc.vector.tensor_tensor(rel_s[:], dst_s[:], ps_w[:].unsqueeze(2).to_broadcast([P, NG, 2]), ALU.subtract))

    with ExitStack() as c2:
        def sb2(name, shape, dt=F32):
            return c2.enter_context(nc.sbuf_tensor(name, shape, dt))

        def sem2(name):
            return c2.enter_context(nc.semaphore(name))

        R = 4
        src_hot = sb2("src_hot", [P, R, 2, P], BF16)
        dst_hot = sb2("dst_hot", [P, R, 2, WIN], BF16)
        apart = sb2("src_apart", [P, R, 2, P], F16)
        far = sb2("far_dst", [P, NG, 2])
        far2 = sb2("far_mask", [P, NG, 2])
        ps = [c2.enter_context(nc.psum_tensor(f"ps_counts{k}", [P, WIN], F32)) for k in range(R)]
        diagonal = sem2("adj_diagonal")
        apart_ready, src_hots, dst_hots = sem2("src_apart_ready"), sem2("src_hots"), sem2("dst_hots")
        counted = sem2("pair_counted")
        added = sem2("pair_added")
        far_hots, far_counted, far_added = sem2("far_hots"), sem2("far_counted"), sem2("far_added")
        vsteps = sem2("adj_vsteps")

        def count(u):
            for j in range(2):
                last = nc.tensor.matmul(ps[u][:], src_hot[:, u, j, :], dst_hot[:, u, j, :], start=(j == 0), stop=(j == 1))
            return last

        with nc.Block() as block:
            @block.scalar
            def _(act):
                def one(i, u, live):
                    if live(0):
                        for j in range(2):
                            last = nc.scalar.activation(apart[:, u % R, j, :], keep["iota"][:, 0:P], ACT.Abs,
                                                        bias=lo_s[:, bass.ds(i, 1), j], scale=-1.0)
                        last.then_inc(apart_ready, 1)
                    if live(1):
                        act.wait_ge(apart_ready, i)
                        if not known(i) or i > R:
                            act.wait_ge(counted, i - R)
                        nc.scalar.activation(src_hot[:, (u - 1) % R, :, :], apart[:, (u - 1) % R, :, :], ACT.Relu, bias=1.0, scale=-1.0).then_inc(src_hots, 1)
                run_steps(act, NG, 1, 16, one, head=16)

            @block.vector
            def _(v):
                ch = Chain(v, vsteps)
                step = AC + P
                diag = adj[:, 0:(NB - 1) * step].rearrange("p (b c) -> p b c", c=step)[:, :, 0:P]
                ch.link(nc.vector.tensor_copy(diag, keep["identb"][:].unsqueeze(1).to_broadcast([P, NB - 1, P])))
                ch.link(nc.vector.tensor_copy(adj[:, (NB - 1) * step:(NB - 1) * step + P], keep["identb"][:]))
                load = Loads(v, "window", ACOLS - WIN, 16)
                at = [None]

                def one(i, u, live):
                    if u == 0:
                        at[0] = load(win_i, i + LEAD - 2)
                    if live(0):
                        if not known(i) or i >= R:
                            v.wait_ge(counted, i - R + 1)
                        for j in range(2):
                            last = nc.vector.tensor_scalar(dst_hot[:, u % R, j, :], keep["iota"][:], rel_s[:, bass.ds(i, 1), j], None, ALU.is_equal)
                        last.then_inc(dst_hots, 1)
                    if live(2):
                        v.wait_ge(counted, i - 1)
                        if not known(i) or i >= 3:
                            v.wait_ge(added, i - 2)
                        win = adj[:, bass.ds(at[0][u], WIN)]
                        nc.vector.tensor_tensor(win, win, ps[(u - 2) % R][:], ALU.add).then_inc(added, 1)
                run_steps(v, NG, 2, 16, one, head=16)
                v.wait_ge(added, NG)

            @block.tensor
            def _(pe):
                def one(i, u, live):
                    if live(0):
                        pe.wait_ge(src_hots, i + 1)
                        pe.wait_ge(dst_hots, i + 1)
                        if not known(i) or i >= R:
                            pe.wait_ge(added, i - R + 1)
                        count(u % R).then_inc(counted, 1)
                run_steps(pe, NG, 0, 16, one, head=16)

        with nc.Block() as block:
            @block.vector
            def _(v):
                ch = Chain(v, vsteps, 2)
                wide = v.value_load(flag_i[0:1, 0:1], min_val=0, max_val=1)
                with v.If(wide != 0):
                    load = v.alloc_register("bin_column")
                    ch.link(nc.vector.tensor_scalar(far2[:], rel_s[:], float(WIN), None, ALU.is_ge))
                    ch.link(nc.vector.scalar_tensor_tensor(far[:], dst_s[:], 1.0, far2[:], ALU.add, ALU.mult))
                    ch.link(nc.vector.tensor_scalar(far[:], far[:], -1.0, None, ALU.add))
                    with v.Fori(0, 7) as k:
                        with v.Fori(0, NG) as g:
                            v.load(load, bin_i[0:1, bass.ds(g + LEAD, 1)])
                            col = v.snap(load, min_val=0, max_val=(NB - 1) * AC)
                            for j in range(2):
                                nc.vector.tensor_scalar(src_hot[:, 0, j, :], keep["iota"][:, 0:P], lo_s[:, bass.ds(g, 1), j], None, ALU.is_equal)
                                last = nc.vector.tensor_scalar(dst_hot[:, 0, j, :], keep["iota"][:], far[:, bass.ds(g, 1), j], None, ALU.is_equal)
                            last.then_inc(far_hots, 1)
                            v.wait_ge(far_counted, k * NG + g + 1)
                            win = adj[:, bass.ds(col + k * WIN, WIN)]
                            nc.vector.tensor_tensor(win, win, ps[0][:], ALU.add).then_inc(far_added, 1)
                            v.wait_ge(far_added, k * NG + g + 1)
                        nc.vector.tensor_scalar(far[:], far[:], float(-WIN), None, ALU.add).then_inc(far_hots, 1)
                        v.wait_ge(far_hots, (k + 1) * (NG + 1))

            @block.tensor
            def _(pe):
                wide = pe.value_load(flag_i[0:1, 0:1], min_val=0, max_val=1)
                with pe.If(wide != 0):
                    with pe.Fori(0, 7) as k:
                        with pe.Fori(0, NG) as g:
                            pe.wait_ge(far_hots, k * (NG + 1) + g + 1)
                            count(0).then_inc(far_counted, 1)

            if "A" in dbg:
                @block.sync
                def _(sp):
                    wide = sp.value_load(flag_i[0:1, 0:1], min_val=0, max_val=1)
                    with sp.If(wide != 0):
                        sp.wait_ge(far_added, 7 * NG)
                    sp.dma_start(dbg["A"], adj[:]).then_inc(diagonal, 16)
                    sp.dma_start(dbg["flag"], flag_i[:]).then_inc(diagonal, 16)
                    sp.wait_ge(diagonal, 32)
    edges.close()

    with ExitStack() as c4:
        gcn_layers(nc, c4, keep, adj)
    if "x1" in dbg:
        with nc.semaphore("dbg_x1") as s, nc.Block() as block:
            @block.sync
            def _(sp):
                sp.dma_start(dbg["x1"], keep["x"][:]).then_inc(s, 16)
                sp.wait_ge(s, 16)


def gcn_layers(nc, ctx, keep, adj):
    def sb(name, shape, dt=F32):
        return ctx.enter_context(nc.sbuf_tensor(name, shape, dt))

    def sem(name):
        return ctx.enter_context(nc.semaphore(name))

    def psum(name, shape):
        return [ctx.enter_context(nc.psum_tensor(f"{name}{k}", shape, F32)) for k in range(2)]

    LINKS = 6
    h3, h3_next = sb("h_parts", [P, NB, 3, D], BF16), sb("h_parts_next", [P, NB, 3, D], BF16)
    res_all = sb("layer_out", [P, NB, D])
    agg = sb("agg", [P, 2, P])
    agg_t = sb("agg_t", [D, 2, P])
    act_in = sb("next_in", [P, 2, D])
    w_now = sb("w_layer", [D, 1, D])
    ps_agg, ps_t, ps_o = psum("ps_agg", [P, 3, D]), psum("ps_aggt", [P, P]), psum("ps_out", [P, D])
    first_ready, parts_ready, gathered, summed, turned, turned_c, multiplied, finished, vsteps, ends, weights_ready = (
        sem(x) for x in ("first_ready", "parts_ready", "agg_gathered", "agg_summed", "agg_turned", "agg_turned_c", "multiplied",
                         "tile_finished", "layer_vsteps", "layer_ends", "layer_weights"))

    with nc.Block() as block:
        @block.tensor
        def _(pe):
            with pe.Fori(0, 3) as layer:
                pe.wait_ge(first_ready, layer + 1)
                for m in range(NB + 2):
                    u = m % 2
                    if m < NB:
                        if m >= 2:
                            pe.wait_ge(summed, layer * NB + (m - 1))
                        for b in range(NB):
                            if m == 0 and b == NB - 2:
                                pe.wait_ge(parts_ready, layer + 1)
                            last = nc.tensor.matmul(ps_agg[u][:], adj[:, b * AC + m * P:b * AC + (m + 1) * P], h3[:, b, :, :],
                                                    start=(b == 0), stop=(b == NB - 1))
                        last.then_inc(gathered, 1)
                    if 1 <= m <= NB:
                        pe.wait_ge(summed, layer * NB + m)
                        if m >= 3:
                            pe.wait_ge(turned_c, layer * NB + (m - 2))
                        nc.tensor.transpose(ps_t[1 - u][:], agg[:, 1 - u, :], keep["ident"][:]).then_inc(turned, 1)
                    if m >= 2:
                        pe.wait_ge(turned_c, layer * NB + (m - 1))
                        if m == 2:
                            pe.wait_ge(weights_ready, layer + 1)
                        if m >= 4:
                            pe.wait_ge(finished, layer * NB + (m - 3))
                        nc.tensor.matmul(ps_o[u][:], agg_t[:, u, :], w_now[:], start=True, stop=True).then_inc(multiplied, 1)

        @block.scalar
        def _(act):
            with act.Fori(0, 3) as layer:
                for m in range(NB):
                    act.wait_ge(turned, layer * NB + (m + 1))
                    if m >= 2:
                        act.wait_ge(multiplied, layer * NB + (m - 1))
                    nc.scalar.activation(agg_t[:, m % 2, :], ps_t[m % 2][0:D, :], ACT.Copy).then_inc(turned_c, 1)

        @block.vector
        def _(v):
            ch = Chain(v, ends)
            nc.vector.memset(agg[:], 0.0)
            h = keep["h"]
            ch.link(nc.vector.tensor_copy(h3[:, :, 0, :], h[:]))
            ch.link(nc.vector.tensor_tensor(h[:], h[:], h3[:, :, 0, :], ALU.subtract))
            ch.link(nc.vector.tensor_copy(h3[:, :, 1, :], h[:]))
            ch.link(nc.vector.tensor_tensor(h3[:, :, 2, :], h[:], h3[:, :, 1, :], ALU.subtract))
            v.sem_inc(first_ready, 1)
            v.sem_inc(parts_ready, 1)
            with v.Fori(0, 3) as layer:
                nc.vector.tensor_scalar(w_now[:], keep["wg"][:, bass.ds(layer, 1), :], 1.0, None, ALU.mult).then_inc(weights_ready, 1)
                for m in range(NB + 2):
                    u = m % 2
                    if m < NB:
                        v.wait_ge(gathered, layer * NB + (m + 1))
                        if m >= 2:
                            v.wait_ge(turned, layer * NB + (m - 1))
                        nc.vector.tensor_reduce(agg[:, u, 0:D], ps_agg[u][:].rearrange("p s d -> p d s"), AX.X, ALU.add).then_inc(summed, 1)
                    if m == NB:
                        nc.vector.tensor_copy(h3[:, 0:NB - 2, :, :], h3_next[:, 0:NB - 2, :, :]).then_inc(first_ready, 1)
                    if m >= 2:
                        t = m - 2
                        dinv = keep["dinv"][:, t:t + 1]
                        r, nxt = res_all[:, t:t + 1, :], act_in[:, u:u + 1, :]
                        part = [h3_next[:, t:t + 1, k, :] for k in range(3)]
                        v.wait_ge(multiplied, layer * NB + (m - 1))
                        ch = Chain(v, vsteps)
                        ch.step(layer * NB + t, LINKS)
                        ch.link(nc.vector.scalar_tensor_tensor(r, ps_o[u][:].unsqueeze(1), dinv, keep["bg"][:, bass.ds(layer, 1), :], ALU.mult, ALU.add))
                        ch.link(nc.vector.tensor_scalar(nxt, r, 0.0, dinv, ALU.max, ALU.mult))
                        ch.link(nc.vector.tensor_copy(part[0], nxt))
                        ch.link(nc.vector.tensor_tensor(nxt, nxt, part[0], ALU.subtract))
                        ch.link(nc.vector.tensor_copy(part[1], nxt))
                        ch.link(nc.vector.tensor_tensor(part[2], nxt, part[1], ALU.subtract))
                        ch.end()
                        v.sem_inc(finished, 1)
                nc.vector.tensor_copy(h3[:, NB - 2:NB, :, :], h3_next[:, NB - 2:NB, :, :]).then_inc(parts_ready, 1)
                v.wait_ge(first_ready, layer + 2)
                v.wait_ge(parts_ready, layer + 2)
            nc.vector.tensor_tensor(keep["x"][:], keep["x"][:], res_all[:], ALU.add)


class Bins:

    def __init__(self, eng, count):
        self.eng = eng
        self.regs = [eng.alloc_register(f"bin{k}") for k in range(count)]

    def __call__(self, row, at):
        self.eng.load(self.regs, row[0:1, bass.ds(at, len(self.regs))])
        return [self.eng.snap(r, min_val=0, max_val=NB - 1) for r in self.regs]


def attention(nc, ctx, keep, table, qtable, w_att1t, b_att1, w_att2, b_att2, w_lint, b_lin,
              w_iht, b_ih, w_hht, b_hh, part_mask, out, dbg):
    def sb(name, shape, dt=F32):
        return ctx.enter_context(nc.sbuf_tensor(name, shape, dt))

    p3 = sb("source_parts", [P, NB, 3, HW], BF16)
    gi = sb("gates_in", [P, NB, 3 * D])
    w_edge = sb("w_edge", [P, HW], BF16)
    w2 = sb("w_att2_sb", [P, HW])
    w_hh = sb("w_hh_sb", [D + 1, 3 * D])
    acc = sb("acc", [P, NB, D + 1])
    with ExitStack() as c1:
        node_tables(nc, c1, keep, p3, gi, acc, w_edge, w2, w_hh, qtable, w_att1t, b_att1, w_att2, b_att2,
                    w_lint, b_lin, w_iht, b_ih, w_hht, b_hh, part_mask)
    with ExitStack() as c2:
        edge_attention(nc, c2, keep, p3, w_edge, w2, acc, table, qtable)
    with ExitStack() as c3:
        gru(nc, c3, keep, gi, w_hh, acc, out)


def node_tables(nc, ctx, keep, p3, gi, acc, w_edge, w2, w_hh, qtable, w_att1t, b_att1, w_att2, b_att2,
                w_lint, b_lin, w_iht, b_ih, w_hht, b_hh, part_mask):
    def sb(name, shape, dt=F32):
        return ctx.enter_context(nc.sbuf_tensor(name, shape, dt))

    def sem(name):
        return ctx.enter_context(nc.semaphore(name))

    A1, G1 = 0, HW
    Q1, ONE, L1 = HW + 3 * D, 2 * H1 + 1 + 3 * D, 2 * HW + 3 * D
    w_node = sb("w_node", [D + 1, L1 + D])
    ql = sb("target_values", [P, NB, QL])
    tmp, sq, st = sb("ln_tmp2", [P, NB, D]), sb("ln_sq2", [P, NB, D]), sb("ln_stats2", [P, 4, NB])
    tile = sb("h_tile", [P, 2, P])
    h_t = sb("h_turned", [D + 1, 2, P])
    rest = sb("p_rest", [P, 2, HW])
    we, we_r, we_p, mask = sb("w_edge_f", [P, HW]), sb("w_edge_rest", [P, HW]), sb("w_edge_p", [P, 3, HW], BF16), sb("part_mask_sb", [P, 3])
    ps_t = [ctx.enter_context(nc.psum_tensor(f"ps_ht{k}", [P, P], F32)) for k in range(2)]
    ps_a = [ctx.enter_context(nc.psum_tensor(f"ps_source{k}", [P, HW], F32)) for k in range(2)]
    ps_q = [ctx.enter_context(nc.psum_tensor(f"ps_target{k}", [P, 3 * D + QL], F32)) for k in range(2)]
    weights, zeroed, normed, var_r, std_r, vsteps = (
        sem(x) for x in ("node_weights", "node_zeroed", "node_normed", "var_ready2", "std_ready2", "node_vsteps"))
    tiled, turned, turned_c, made, kept_a, kept_p, stored = (
        sem(x) for x in ("tiled", "h_turned_ready", "h_turned_copied", "made", "kept_act", "kept_parts", "stored"))
    loads = [(w_node[0:D, A1:A1 + H1], w_att1t[0:D, :]), (w_node[0:D, G1:G1 + 3 * D], w_iht),
             (w_node[0:D, Q1:Q1 + H1], w_att1t[D + ED:H1, :]), (w_node[0:D, L1:L1 + D], w_lint),
             (w_node[D:D + 1, A1:A1 + H1], b_att1.unsqueeze(0)),
             (w_node[D:D + 1, G1:G1 + 3 * D], b_ih.unsqueeze(0)),
             (w_node[D:D + 1, L1:L1 + D], b_lin.unsqueeze(0)),
             *((we[k * ED:(k + 1) * ED, 0:H1], w_att1t[D:D + ED, :]) for k in range(len(W_PART))),
             (mask[:], part_mask), (w2[:, 0:H1], w_att2[0, :].partition_broadcast(P)),
             (w2[:, H1:HW], b_att2.partition_broadcast(P)),
             (w_hh[0:D, :], w_hht), (w_hh[D:D + 1, :], b_hh.unsqueeze(0))]
    NW = len(loads)
    SC = 5
    assert NB % SC == 0

    with nc.Block() as block:
        @block.gpsimd
        def _(pool):
            nc.gpsimd.memset(tile[:], 0.0).then_inc(zeroed, 1)
            nc.gpsimd.memset(acc[:], 0.0)

        @block.sync
        def _(sp):
            sp.wait_ge(zeroed, 2)
            for o, i in loads:
                sp.dma_start(o, i).then_inc(weights, 16)
            qv = qtable.rearrange("(t p) c -> p t c", p=P)
            for k in range(0, NB, SC):
                sp.wait_ge(kept_a, k + SC)
                sp.dma_start(qv[:, k:k + SC, :], ql[:, k:k + SC, :]).then_inc(stored, 16)
            sp.wait_ge(stored, 16 * (NB // SC))
            sp.wait_ge(weights, 16 * NW)

        @block.scalar
        def _(act):
            act.wait_ge(var_r, 1)
            nc.scalar.activation(st[:, 2, :], st[:, 1, :], ACT.Sqrt).then_inc(std_r, 1)
            act.wait_ge(normed, 1)
            act.wait_ge(zeroed, 2)

            def one(i, u, live):
                if live(0):
                    if not known(i) or i >= 2:
                        act.wait_ge(turned, i - 1)
                    nc.scalar.activation(tile[:, u:u + 1, 0:D], keep["h"][:, bass.ds(i, 1), :], ACT.Copy).then_inc(tiled, 1)
                if live(1):
                    act.wait_ge(turned, i)
                    if not known(i) or i >= 3:
                        act.wait_ge(made, i - 2)
                    nc.scalar.activation(h_t[0:D, 1 - u, :], ps_t[1 - u][0:D, :], ACT.Copy).then_inc(turned_c, 1)
                if live(2):
                    m = i - 2
                    act.wait_ge(made, i - 1)
                    nc.scalar.activation(gi[:, bass.ds(m, 1), :], ps_q[u][:, 0:3 * D].unsqueeze(1), ACT.Copy)
                    nc.scalar.activation(ql[:, bass.ds(m, 1), :], ps_q[u][:, 3 * D:].unsqueeze(1), ACT.Copy).then_inc(kept_a, 1)
            run_steps(act, NB, 2, 2, one)

        @block.tensor
        def _(pe):
            pe.wait_ge(weights, 16 * NW)
            pe.wait_ge(zeroed, 2)

            def one(i, u, live):
                if live(0):
                    pe.wait_ge(tiled, i + 1)
                    if not known(i) or i >= 2:
                        pe.wait_ge(turned_c, i - 1)
                    nc.tensor.transpose(ps_t[u][:], tile[:, u, :], keep["ident"][:]).then_inc(turned, 1)
                if live(1):
                    pe.wait_ge(turned_c, i)
                    if not known(i) or i >= 3:
                        pe.wait_ge(kept_a, i - 2)
                        pe.wait_ge(kept_p, i - 2)
                    v = 1 - u
                    nc.tensor.matmul(ps_a[v][:], h_t[:, v, :], w_node[:, 0:HW], start=True, stop=True)
                    nc.tensor.matmul(ps_q[v][:], h_t[:, v, :], w_node[:, HW:L1 + D], start=True, stop=True).then_inc(made, 1)
            run_steps(pe, NB, 1, 2, one)

        @block.vector
        def _(v):
            ch = Chain(v, vsteps)
            ch.link(nc.vector.memset(w_node[:], 0.0))
            nc.vector.memset(we[:, H1:HW], 0.0)
            ch.link(nc.vector.memset(h_t[D:D + 1, :, :], 1.0))
            nc.vector.memset(w_node[D:D + 1, ONE:ONE + 1], 1.0).then_inc(zeroed, 1)
            ln_centre(nc, ch, keep["x"][:], tmp[:], st)
            ln_variance(nc, ch, tmp[:], sq[:], st, var_r)
            ln_scale(nc, v, ch, tmp[:], sq[:], st, std_r, keep["h"][:])
            nc.vector.memset(st[0:1, 0, 0:1], 0.0).then_inc(normed, 1)
            v.wait_ge(weights, 16 * NW)
            ch.link(nc.vector.tensor_copy(we_p[:, 0, :], we[:]))
            ch.link(nc.vector.tensor_tensor(we_r[:], we[:], we_p[:, 0, :], ALU.subtract))
            ch.link(nc.vector.tensor_copy(we_p[:, 1, :], we_r[:]))
            ch.link(nc.vector.tensor_tensor(we_p[:, 2, :], we_r[:], we_p[:, 1, :], ALU.subtract))
            ch.link(nc.vector.tensor_scalar(we[:], we_p[:, 0, :], mask[:, 0:1], None, ALU.mult))
            ch.link(nc.vector.scalar_tensor_tensor(we[:], we_p[:, 1, :], mask[:, 1:2], we[:], ALU.mult, ALU.add))
            ch.link(nc.vector.scalar_tensor_tensor(w_edge[:], we_p[:, 2, :], mask[:, 2:3], we[:], ALU.mult, ALU.add))
            before = ch.n
            ch.step(0, 3)

            def one(i, u, live):
                if live(0):
                    v.wait_ge(made, i + 1)
                    ch.base, ch.n = before + i * 3, 0
                    part = [p3[:, bass.ds(i, 1), k, :] for k in range(3)]
                    r = rest[:, u:u + 1, :]
                    ps = ps_a[u][:].unsqueeze(1)
                    ch.link(nc.vector.tensor_scalar(part[0], ps, 1.0, None, ALU.mult))
                    ch.link(nc.vector.tensor_tensor(r, ps, part[0], ALU.subtract))
                    ch.link(nc.vector.tensor_copy(part[1], r))
                    nc.vector.tensor_tensor(part[2], r, part[1], ALU.subtract).then_inc(kept_p, 1)
                    ch.end()
            run_steps(v, NB, 0, 2, one)


def edge_attention(nc, ctx, keep, p3, w_edge, w2, acc, table, qtable):
    def sb(name, shape, dt=F32):
        return ctx.enter_context(nc.sbuf_tensor(name, shape, dt))

    def sem(name):
        return ctx.enter_context(nc.semaphore(name))

    def psum(name, shape, dt=F32, n=2):
        return [ctx.enter_context(nc.psum_tensor(f"{name}{k}", shape, dt)) for k in range(n)]

    U = 16
    R = 8
    GR = 4
    AHEAD = 16
    bin_i = sb("bin_at2", [1, NG + 3 * AHEAD], I32)
    rec = sb("rec_ring", [P, 2 * U, REC])
    idx = sb("idx_ring", [P, 2 * U], I32)
    rows = sb("row_ring2", [P, 2 * U, QL])
    gate = sb("gate2", [1, 2])
    hot = sb("hot", [P, R, 2, P], BF16)
    neg = sb("neg", [P, 4, 2, P], BF16)
    turn = sb("turn", [P, R, 4, P], BF16)
    hid = sb("hidden_sum", [P, 4, 2, HW])
    junk = sb("hidden_relu", [P, 4, 2, HW])
    score = sb("score", [P, 4, 2])
    by_src = sb("by_src", [P, R, 2, P])
    mx = sb("mx", [P, 4])
    mx2 = sb("mx2", [P, 4])
    parts = sb("top_parts", [P, 4, 2], BF16)
    new = sb("top_new", [P, 4])
    rise = sb("top_rise", [P, R])
    scale = sb("scale", [P, 4])
    shift = sb("shift", [P, 4, 2])
    weight = sb("edge_weight", [P, 4, 2, P])
    top = sb("top", [P, NB])

    ps_turn = psum("ps_turn", [P, 4, P], BF16)
    ps_hid = psum("ps_hid", [P, 2, HW])
    ps_src = psum("ps_src", [P, 2, P])
    ps_top = psum("ps_top", [P, 2], n=1)[0]
    ps_sum = psum("ps_sum", [P, D + 1], n=1)[0]

    ready, setup, idx_ready, gated = (sem(x) for x in ("att_ready", "att_setup", "idx_ready", "gated2"))
    rec_in = [sem(f"rec_in{k}") for k in range(U // GR)]
    gathered = [sem(f"gathered{k}") for k in range(U)]
    (hots, turned, turned_c, negated, hidden, added, scored, laid, by_source, topped, top_back,
     shifts, weighed, aggregated, summed) = (
        sem(x) for x in ("hots2", "turned2", "turned_c2", "negated", "hidden", "hid_added", "scored", "laid", "by_source",
                         "topped", "top_back", "shifts", "weighed", "aggregated", "summed2"))
    c_top = sem("c_top")

    def done(eng, sem, i, back):
        if not known(i) or i >= back:
            eng.wait_ge(sem, i - back + 1)

    tview = table[0:TRASH, :].rearrange("(p t) c -> p t c", t=TT)

    with nc.Block() as block:
        @block.sync
        def _(sp):
            def one(i, u, live):
                if u % GR == 0:
                    if not known(i) or i >= U:
                        sp.wait_ge(turned, i - U + GR)
                        sp.wait_ge(hots, i - U + GR)
                    sp.dma_start(rec[:, 2 * u:2 * (u + GR), :], tview[:, bass.ds(i * 2, 2 * GR), :]).then_inc(rec_in[u // GR], 16)
            run_steps(sp, NG, 0, U, one, head=U)
            for h in range(U // GR):
                sp.wait_ge(rec_in[h], 16 * -(-(NG // GR - h) // (U // GR)))

        @block.gpsimd
        def _(pool):
            pool.wait_ge(ready, 1)

            def one(i, u, live):
                done(pool, gated, i, 1)
                done(pool, aggregated, i, U)
                pool.wait_ge(idx_ready, i - u % GR + GR)
                nc.gpsimd.tensor_tensor(gate[:, 1:2], gate[:, 0:1], gate[:, 0:1], ALU.mult).then_inc(gated, 1)
                for t in (2 * u, 2 * u + 1):
                    pool.indirect_dma_start(rows[:, t, :], None, qtable[:, :],
                                            bass.IndirectOffsetOnAxis(ap=idx[:, t:t + 1], axis=0)).then_inc(gathered[u], 16)
            run_steps(pool, NG, 0, U, one, head=U)

        @block.tensor
        def _(pe):
            pe.wait_ge(ready, 1)
            bins = Bins(pe, U)
            at = [None]

            def one(i, u, live):
                if u == 0:
                    at[0] = bins(bin_i, i + AHEAD - 2)
                if live(1):
                    w = (u - 1) % R
                    done(pe, hots, i, 1)
                    done(pe, turned_c, i, 3)
                    for j in range(2):
                        nc.tensor.transpose(ps_turn[w % 2][:, j, :], hot[:, w, j, :], keep["identb"][:])
                    for j in range(2):
                        for half in (slice(0, P // 2), slice(P // 2, P)):
                            last = nc.tensor.transpose(ps_turn[w % 2][half, 2 + j, :], rec[:, 2 * ((u - 1) % U) + j, 2:REC].bitcast(BF16), keep["identb"][:])
                    last.then_inc(turned, 1)
                if live(2):
                    w = (u - 2) % R
                    done(pe, turned_c, i, 2)
                    done(pe, added, i, 4)
                    w16 = (u - 2) % U
                    pe.wait_ge(gathered[w16], (i - 2 - w16) * (32 // U) + 32)
                    for j in range(2):
                        for k in SPLIT3:
                            nc.tensor.matmul(ps_hid[w % 2][:, j, :], turn[:, w, j, :], p3[:, bass.ds(at[0][u], 1), k, :],
                                             start=(k == 0), stop=False)
                        last = nc.tensor.matmul(ps_hid[w % 2][:, j, :], turn[:, w, 2 + j, :], w_edge[:], start=False, stop=True)
                    last.then_inc(hidden, 1)
                if live(4):
                    w = (u - 4) % R
                    done(pe, laid, i, 4)
                    done(pe, topped, i, 6)
                    for j in range(2):
                        last = nc.tensor.transpose(ps_src[w % 2][:, j, :], by_src[:, w, j, :], keep["ident"][:])
                    last.then_inc(by_source, 1)
                if live(6):
                    w = (u - 6) % R
                    done(pe, topped, i, 6)
                    done(pe, shifts, i, 7)
                    for j in range(2):
                        for k in range(2):
                            last = nc.tensor.matmul(ps_top[:, j:j + 1], turn[:, w, j, :], parts[:, w % 4, k:k + 1],
                                                    start=(k == 0), stop=(k == 1))
                    last.then_inc(top_back, 1)
                if live(9):
                    w = (u - 9) % U
                    done(pe, weighed, i, 9)
                    done(pe, summed, i, 10)
                    for j in range(2):
                        last = nc.tensor.matmul(ps_sum[:], weight[:, w % 4, j, :], rows[:, 2 * w + j, H1:QL],
                                                start=(j == 0), stop=(j == 1))
                    last.then_inc(aggregated, 1)
            run_steps(pe, NG, 9, U, one, head=U)

        @block.scalar
        def _(act):
            act.wait_ge(ready, 1)

            def one(i, u, live):
                if live(8):
                    w = (u - 8) % R
                    done(act, shifts, i, 8)
                    done(act, summed, i, 12)
                    done(act, aggregated, i, 12)
                    for j in range(2):
                        nc.scalar.activation(weight[:, w % 4, j, :], by_src[:, w, j, :], ACT.Exp, bias=shift[:, w % 4, j:j + 1])
                    nc.scalar.activation(scale[:, w % 4:w % 4 + 1], rise[:, w:w + 1], ACT.Exp, scale=-1.0).then_inc(weighed, 1)
                if live(1):
                    w = (u - 1) % R
                    done(act, turned, i, 1)
                    done(act, top_back, i, 9)
                    nc.scalar.activation(turn[:, w, :, :], ps_turn[w % 2][:], ACT.Copy).then_inc(turned_c, 1)
                if live(3):
                    w = (u - 3) % R
                    done(act, scored, i, 3)
                    done(act, negated, i, 3)
                    done(act, by_source, i, 11)
                    done(act, weighed, i, 11)
                    for j in range(2):
                        last = nc.scalar.activation(by_src[:, w, j, :], neg[:, w % 4, j, :], ACT.Identity,
                                                    bias=score[:, w % 4, j:j + 1])
                    last.then_inc(laid, 1)
                if live(1):
                    w = (u - 1) % R
                    done(act, hots, i, 1)
                    done(act, laid, i, 5)
                    nc.scalar.activation(neg[:, w % 4, :, :], hot[:, w, :, :], ACT.Copy, bias=-BIG, scale=BIG).then_inc(negated, 1)
            run_steps(act, NG, 8, U, one, head=U)

        @block.vector
        def _(v):
            nc.vector.memset(gate[:], 1.0)
            nc.vector.memset(top[:], -BIG)
            nc.vector.memset(bin_i[:], 0).then_inc(setup, 1)
            v.wait_ge(setup, 1)
            nc.vector.tensor_copy(bin_i[0:1, AHEAD:AHEAD + NG], keep["bin_row"][0:1, 0:NG]).then_inc(setup, 1)
            v.wait_ge(setup, 2)
            v.sem_inc(ready, 1)
            bins = Bins(v, U + 5)
            at = [None]

            def take_targets(w, start):
                v.wait_ge(rec_in[w // GR], start + U)
                nc.vector.tensor_copy(idx[:, 2 * w:2 * w + 2 * GR], rec[:, 2 * w:2 * w + 2 * GR, 0]).then_inc(idx_ready, GR)
            assert U == 16
            take_targets(0, 0)

            def one(i, u, live):
                if u == 0:
                    at[0] = bins(bin_i, i + AHEAD - 10)
                s5, s6 = (u - 5) % 4, (u - 6) % 4

                def top_at(back):
                    return top[:, bass.ds(at[0][u + 10 - back], 1)]

                def top_step(back, n):
                    v.wait_ge(c_top, (i - back) * 6 + n)

                if u % GR == 0 and live(-GR):
                    take_targets((u + GR) % U, i - u + (U if u + GR >= U else 0))
                if live(0):
                    nc.vector.tensor_scalar(hot[:, u % R, 0, :], keep["iota"][:, 0:P], rec[:, 2 * u, 1:2], None, ALU.is_equal)
                if live(6):
                    v.wait_ge(topped, i - 5)
                    nc.vector.scalar_tensor_tensor(new[:, s6:s6 + 1], parts[:, s6, 0:1], -1.0, parts[:, s6, 1:2], ALU.mult, ALU.subtract).then_inc(c_top, 1)
                if live(0):
                    nc.vector.tensor_scalar(hot[:, u % R, 1, :], keep["iota"][:, 0:P], rec[:, 2 * u + 1, 1:2], None, ALU.is_equal).then_inc(hots, 1)
                if live(6):
                    top_step(6, 4)
                    nc.vector.tensor_tensor(rise[:, (u - 6) % R:(u - 6) % R + 1], new[:, s6:s6 + 1], top_at(6), ALU.subtract).then_inc(c_top, 1)
                if live(3):
                    w = (u - 3) % U
                    done(v, hidden, i, 3)
                    nc.vector.tensor_tensor(hid[:, w % 4, :, :], ps_hid[w % 2][:], rows[:, 2 * w:2 * w + 2, 0:HW], ALU.add).then_inc(added, 1)
                if live(6):
                    top_step(6, 5)
                    nc.vector.tensor_scalar(top_at(6), new[:, s6:s6 + 1], 1.0, None, ALU.mult).then_inc(c_top, 1)
                if live(5):
                    done(v, by_source, i, 5)
                    nc.vector.tensor_reduce(mx[:, s5:s5 + 1], ps_src[(u - 5) % 2][:].rearrange("p j e -> p (j e)"), AX.X, ALU.max).then_inc(c_top, 1)

                def score_half(j):
                    return nc.vector.scalar_tensor_tensor(junk[:, w % 4, j, :], hid[:, w % 4, j, :], 0.0, w2[:], ALU.max, ALU.mult,
                                                          accum_out=score[:, w % 4, j:j + 1])
                if live(3):
                    done(v, added, i, 3)
                    score_half(0)
                if live(5):
                    top_step(5, 1)
                    nc.vector.tensor_tensor(mx2[:, s5:s5 + 1], mx[:, s5:s5 + 1], top_at(5), ALU.max).then_inc(c_top, 1)
                if live(3):
                    score_half(1).then_inc(scored, 1)
                if live(5):
                    top_step(5, 2)
                    nc.vector.tensor_scalar(parts[:, s5, 0:1], mx2[:, s5:s5 + 1], -1.0, None, ALU.mult).then_inc(c_top, 1)
                if live(10):
                    w10 = (u - 10) % 4
                    done(v, aggregated, i, 10)
                    a = acc[:, bass.ds(at[0][u], 1), :]
                    nc.vector.scalar_tensor_tensor(a, a, scale[:, w10:w10 + 1], ps_sum[:].unsqueeze(1), ALU.mult, ALU.add).then_inc(summed, 1)
                if live(5):
                    top_step(5, 3)
                    nc.vector.scalar_tensor_tensor(parts[:, s5, 1:2], mx2[:, s5:s5 + 1], -1.0, parts[:, s5, 0:1], ALU.mult, ALU.subtract).then_inc(topped, 1)
                if live(7):
                    w7 = (u - 7) % 4
                    done(v, top_back, i, 7)
                    nc.vector.tensor_scalar(shift[:, w7, :], ps_top[:], 1.0, None, ALU.mult).then_inc(shifts, 1)
            run_steps(v, NG, 10, U, one, head=U)


def gru(nc, ctx, keep, gi, w_hh, acc, out):
    def sb(name, shape, dt=F32):
        return ctx.enter_context(nc.sbuf_tensor(name, shape, dt))

    def sem(name):
        return ctx.enter_context(nc.semaphore(name))

    G = 5
    GROUPS = NB // G
    msg, gh = sb("message", [P, NB, D]), sb("n_of_msg", [P, NB, D])
    den, has = sb("den", [P, NB]), sb("has_edge", [P, NB])
    tile, m_t = sb("msg_tile", [P, 2, P]), sb("msg_turned", [D + 1, 2, P])
    rz, nn, t1 = sb("rz", [P, NB, 2 * D]), sb("nn", [P, NB, D]), sb("gru_t1", [P, NB, D])
    xh = sb("x_plus_h", [P, NB, D])
    ps_t = [ctx.enter_context(nc.psum_tensor(f"ps_mt{k}", [P, P], F32)) for k in range(2)]
    ps_g = [ctx.enter_context(nc.psum_tensor(f"ps_gates{k}", [P, 3 * D], F32)) for k in range(2)]
    zeroed, begun, vsteps, tiled, turned, turned_c, made, kept, added, summed, gated, pre_n, n_done, pre_steps, finished, stored = (
        sem(x) for x in ("gru_zeroed", "msg_ready", "gru_vsteps", "gru_tiled", "gru_turned", "gru_turned_c", "gru_made",
                         "gru_kept", "x_h_added", "gru_summed", "gru_gated", "gru_pre_n", "gru_n", "gru_pre_steps",
                         "gru_finished", "out_stored"))
    x, h = keep["x"], keep["h"]

    def done(eng, sem, i, back):
        if not known(i) or i >= back:
            eng.wait_ge(sem, i - back + 1)

    def at(array, i):
        return array[:, bass.ds(i, 1), :]

    with nc.Block() as block:
        @block.gpsimd
        def _(pool):
            nc.gpsimd.memset(tile[:], 0.0).then_inc(zeroed, 1)
            nc.gpsimd.tensor_tensor(xh[:], x[:], h[:], ALU.add).then_inc(added, 1)

        @block.scalar
        def _(act):
            act.wait_ge(begun, 1)
            act.wait_ge(zeroed, 2)

            def one(i, u, live):
                u %= 2
                if live(0):
                    done(act, turned, i, 2)
                    nc.scalar.activation(tile[:, u:u + 1, 0:D], at(msg, i), ACT.Copy).then_inc(tiled, 1)
                if live(1):
                    done(act, turned, i, 1)
                    done(act, made, i, 3)
                    nc.scalar.activation(m_t[0:D, 1 - u, :], ps_t[1 - u][0:D, :], ACT.Copy).then_inc(turned_c, 1)
                if live(3):
                    done(act, summed, i, 3)
                    nc.scalar.activation(at(rz, i - 3), at(rz, i - 3), ACT.Tanh, scale=0.5).then_inc(gated, 1)
                if live(5):
                    done(act, pre_n, i, 5)
                    nc.scalar.activation(at(nn, i - 5), at(nn, i - 5), ACT.Tanh).then_inc(n_done, 1)
            run_steps(act, NB, 5, 4, one, head=8)

        @block.tensor
        def _(pe):
            def one(i, u, live):
                u %= 2
                if live(0):
                    done(pe, tiled, i, 0)
                    done(pe, turned_c, i, 2)
                    nc.tensor.transpose(ps_t[u][:], tile[:, u, :], keep["ident"][:]).then_inc(turned, 1)
                if live(1):
                    done(pe, turned_c, i, 1)
                    done(pe, kept, i, 3)
                    nc.tensor.matmul(ps_g[1 - u][:], m_t[:, 1 - u, :], w_hh[:], start=True, stop=True).then_inc(made, 1)
            run_steps(pe, NB, 1, 4, one, head=8)

        @block.vector
        def _(v):
            ch = Chain(v, vsteps)
            nc.vector.memset(m_t[D:D + 1, :, :], 1.0).then_inc(zeroed, 1)
            nc.vector.tensor_scalar(has[:], acc[:, :, 0], 0.5, None, ALU.is_ge)
            ch.link(nc.vector.tensor_scalar(den[:], acc[:, :, 0], 0.5, None, ALU.max))
            ch.link(nc.vector.reciprocal(den[:], den[:]))
            nc.vector.tensor_tensor(msg[:], acc[:, :, 1:D + 1], den[:].unsqueeze(2).to_broadcast([P, NB, D]), ALU.mult).then_inc(begun, 1)

            def one(i, u, live):
                u %= 2
                if live(2):
                    done(v, made, i, 2)
                    g = ps_g[u][:].unsqueeze(1)
                    nc.vector.tensor_tensor(at(rz, i - 2), gi[:, bass.ds(i - 2, 1), 0:2 * D], g[:, :, 0:2 * D], ALU.add).then_inc(summed, 1)
                    nc.vector.tensor_scalar(at(gh, i - 2), g[:, :, 2 * D:3 * D], 1.0, None, ALU.mult).then_inc(kept, 1)
                if live(4):
                    done(v, gated, i, 4)
                    done(v, kept, i, 4)
                    ch_pre = Chain(v, pre_steps)
                    ch_pre.step(i - 4, 1)
                    t = at(t1, i - 4)
                    ch_pre.link(nc.vector.scalar_tensor_tensor(t, rz[:, bass.ds(i - 4, 1), 0:D], 1.0, at(gh, i - 4), ALU.add, ALU.mult))
                    nc.vector.scalar_tensor_tensor(at(nn, i - 4), t, 0.5, gi[:, bass.ds(i - 4, 1), 2 * D:3 * D], ALU.mult, ALU.add).then_inc(pre_n, 1)
            run_steps(v, NB, 4, 4, one, head=8)
            v.wait_ge(added, 1)
            for g in range(GROUPS):
                gs = slice(g * G, (g + 1) * G)
                v.wait_ge(n_done, (g + 1) * G)
                z, t, n = rz[:, gs, D:2 * D], t1[:, gs, :], nn[:, gs, :]
                ch.link(nc.vector.tensor_tensor(t, msg[:, gs, :], n, ALU.subtract))
                ch.link(nc.vector.scalar_tensor_tensor(t, z, 1.0, t, ALU.add, ALU.mult))
                ch.link(nc.vector.scalar_tensor_tensor(t, t, 0.5, n, ALU.mult, ALU.add))
                ch.link(nc.vector.tensor_tensor(t, t, h[:, gs, :], ALU.subtract))
                ch.link(nc.vector.tensor_tensor(t, t, has[:, gs].unsqueeze(2).to_broadcast([P, G, D]), ALU.mult))
                nc.vector.tensor_tensor(xh[:, gs, :], xh[:, gs, :], t, ALU.add).then_inc(finished, 1)

        @block.sync
        def _(sp):
            ov = out.rearrange("(t p) d -> p t d", p=BN)
            with sp.Fori(0, GROUPS) as g:
                gs = bass.ds(g * G, G)
                sp.wait_ge(finished, g + 1)
                for a, b in node_parts():
                    sp.dma_start(ov[a:b, gs, :], xh[a:b, gs, :]).then_inc(stored, 16)
            sp.wait_ge(stored, 2 * 16 * GROUPS)


_OUT = ((N, D), "float32")


def kernel(x, src, dst, edge_attr_16, L0_gnn_W0, L0_gnn_b0, L0_gnn_W1, L0_gnn_b1, L0_gnn_W2, L0_gnn_b2,
           L1_gnn_W_att1, L1_gnn_b_att1, L1_gnn_W_att2, L1_gnn_b_att2, L1_gnn_W_lin, L1_gnn_b_lin,
           L1_gnn_W_ih, L1_gnn_b_ih, L1_gnn_W_hh, L1_gnn_b_hh):
    import numpy as np
    import concourse.bacc as bacc
    from concourse.bass_utils import run_bass_kernel_spmd

    def turned(w):
        return np.ascontiguousarray(np.asarray(w).T)

    arrays = dict(
        x=x, src=src, dst=dst, attr=edge_attr_16,
        w_gcn=np.stack([np.asarray(w) for w in (L0_gnn_W0, L0_gnn_W1, L0_gnn_W2)]),
        b_gcn=np.stack([np.asarray(b) for b in (L0_gnn_b0, L0_gnn_b1, L0_gnn_b2)]),
        w_att1t=turned(L1_gnn_W_att1), b_att1=L1_gnn_b_att1, w_att2=L1_gnn_W_att2, b_att2=L1_gnn_b_att2,
        w_lint=turned(L1_gnn_W_lin), b_lin=L1_gnn_b_lin, w_iht=turned(L1_gnn_W_ih), b_ih=L1_gnn_b_ih,
        w_hht=turned(L1_gnn_W_hh), b_hh=L1_gnn_b_hh,
        part_mask=np.repeat(np.array([[w == k for k in SPLIT3] for w in W_PART], np.float32), ED, axis=0),
        eye=np.eye(P, dtype=np.float32), upper=np.triu(np.ones((P, P), np.float32), 1),
    )
    nc = bacc.Bacc("TRN2", target_bir_lowering=False, num_devices=1)
    ins, args = {}, {}
    for name, a in arrays.items():
        a = np.ascontiguousarray(a)
        ins[f"in_{name}"] = a
        args[name] = nc.dram_tensor(f"in_{name}", a.shape, mybir.dt.from_np(a.dtype), kind="ExternalInput").ap()
    args["out"] = nc.dram_tensor("out_0", _OUT[0], F32, kind="ExternalOutput").ap()
    gnn_kernel(nc, **args)
    r = run_bass_kernel_spmd(nc, [ins], core_ids=[0])
    return r.results[0]["out_0"]
```
